# Optimizing a Trainium2 kernel written in Bass

```python
import numpy as np
import jax
import jax.numpy as jnp

def _softmax(x, axis=-1):
    return jax.nn.softmax(x, axis=axis)

def _gelu(x):
    return jax.nn.gelu(x, approximate=True)

def _silu(x):
    return jax.nn.silu(x)

def _sigmoid(x):
    return jax.nn.sigmoid(x)

def _layernorm(x, axis=-1, eps=1e-05):
    m = jnp.mean(x, axis=axis, keepdims=True)
    v = jnp.var(x, axis=axis, keepdims=True)
    return (x - m) / jnp.sqrt(v + eps)

def _scatter_add(tgt, idx, src, axis=0):
    return tgt.at[idx].add(src)

def _segment_sum(src, seg, n):
    return jax.ops.segment_sum(src, seg, n)
kernel_name = 'mk_recurrent_d2_jaxref_r8_55c615'

def setup_inputs(seed: int=0):
    np.random.seed(seed)
    _w = jnp.asarray

    def _L0_attn_setup():
        import jax, jax.numpy as jnp
        import numpy as np
        D_MODEL = 128
        N_HEADS = 16
        HEAD_DIM = D_MODEL // N_HEADS
        N_EXPERTS = 4
        HIDDEN = 4 * D_MODEL
        B, T = (1, 256)

        def _apply_rope(x, sin, cos):
            x1, x2 = (x[..., ::2], x[..., 1::2])
            r1 = x1 * cos - x2 * sin
            r2 = x1 * sin + x2 * cos
            return jnp.stack((r1, r2), axis=-1).reshape(x.shape)
        key = jax.random.key(seed)
        ks = jax.random.split(key, 16)
        s = 0.02
        d, E, Hd = (D_MODEL, N_EXPERTS, HIDDEN)
        return {'x': jax.random.normal(ks[0], (B, T, d), dtype=jnp.float32), 'w_dw': jax.random.normal(ks[1], (d, 3), dtype=jnp.float32) * s, 'w_pw': jax.random.normal(ks[2], (d, d), dtype=jnp.float32) * s, 'w_qkv': jax.random.normal(ks[3], (3 * d, d), dtype=jnp.float32) * s, 'w_o': jax.random.normal(ks[4], (d, d), dtype=jnp.float32) * s, 'w_gate': jax.random.normal(ks[5], (d, d), dtype=jnp.float32) * s, 'b_gate': jnp.zeros((d,), dtype=jnp.float32), 'ln_g': jnp.ones((d,), dtype=jnp.float32), 'ln_b': jnp.zeros((d,), dtype=jnp.float32), 'w_moe_gate': jax.random.normal(ks[6], (E, d), dtype=jnp.float32) * s, 'w1': jax.random.normal(ks[7], (E, Hd, d), dtype=jnp.float32) * s, 'b1': jnp.zeros((E, Hd), dtype=jnp.float32), 'w2': jax.random.normal(ks[8], (E, d, Hd), dtype=jnp.float32) * s, 'b2': jnp.zeros((E, d), dtype=jnp.float32)}
    _L0_attn_in = _L0_attn_setup()

    def _L0_ffn_setup():
        import math
        import jax, jax.numpy as jnp
        import numpy as np
        B, T, D, N, H = (8, 256, 128, 16, 256)
        CAP_FACTOR = 1.25
        key = jax.random.key(seed)
        ks = jax.random.split(key, 4)
        x = jax.random.normal(ks[0], (B, T, D), jnp.float32)
        Wg = jax.random.normal(ks[1], (D, N), jnp.float32) * D ** (-0.5)
        W1 = jax.random.normal(ks[2], (N, D, H), jnp.float32) * D ** (-0.5)
        b1 = jnp.zeros((N, H), jnp.float32)
        W2 = jax.random.normal(ks[3], (N, H, D), jnp.float32) * H ** (-0.5)
        b2 = jnp.zeros((N, D), jnp.float32)
        return {'x': x, 'Wg': Wg, 'W1': W1, 'b1': b1, 'W2': W2, 'b2': b2}
    _L0_ffn_in = _L0_ffn_setup()

    def _L1_attn_setup():
        import jax, jax.numpy as jnp
        import numpy as np
        HEADS, HEAD_SIZE, FREQS, MAX_PERIOD = (16, 64, 32, 1250)
        D_MODEL = 128
        NEG_INF = -1000000000.0

        def sinusoid_embedding(seq_len, frequencies, max_period):
            pos = np.arange(seq_len, dtype=np.float64)[:, None]
            idx = np.arange(frequencies)[None, :]
            inv_freq = max_period ** (-(idx // 2 * 2) / frequencies)
            angle = pos * inv_freq
            table = np.where(idx % 2 == 0, np.sin(angle), np.cos(angle))
            return table.astype(np.float32)

        def relative_causal(scores):
            L = scores.shape[-1]
            d = jnp.clip(jnp.arange(L)[:, None] - jnp.arange(L)[None, :], 0, L - 1)
            return jnp.take_along_axis(scores, d[None, None, :, :], axis=-1)
        key = jax.random.key(seed)
        ks = jax.random.split(key, 4)
        u = np.sqrt(3.0)
        inp = jax.random.normal(ks[0], (2, 256, D_MODEL), dtype=jnp.float32)
        qkv = jax.random.uniform(ks[1], (D_MODEL, 3, HEADS, HEAD_SIZE), jnp.float32, -u, u)
        q_bias = jnp.zeros((HEADS, HEAD_SIZE), jnp.float32)
        positional = jax.random.uniform(ks[2], (FREQS, HEADS, HEAD_SIZE), jnp.float32, -u, u)
        out_kernel = jax.random.uniform(ks[3], (HEADS * HEAD_SIZE, D_MODEL), jnp.float32, -u, u)
        out_bias = jnp.zeros((D_MODEL,), jnp.float32)
        return {'input': inp, 'qkv': qkv, 'q_bias': q_bias, 'positional': positional, 'out_kernel': out_kernel, 'out_bias': out_bias}
    _L1_attn_in = _L1_attn_setup()

    def _L1_ffn_setup():
        import jax, jax.numpy as jnp
        import numpy as np
        DIM = 128

        def _reference_tuple_inner(x, W_r, W_k, W_v, mu_r, mu_k):
            B, T, C = x.shape
            x_prev = jnp.concatenate([jnp.zeros((B, 1, C), x.dtype), x[:, :-1, :]], axis=1)
            xr = mu_r * x + (1.0 - mu_r) * x_prev
            xk = mu_k * x + (1.0 - mu_k) * x_prev
            r = jax.nn.sigmoid(jnp.einsum('btc,dc->btd', xr, W_r))
            k = jnp.einsum('btc,dc->btd', xk, W_k)
            k_act = jnp.square(jax.nn.relu(k))
            out = r * jnp.einsum('btc,dc->btd', k_act, W_v)
            new_state = x[:, -1, :]
            return (out, new_state)
        key = jax.random.key(seed)
        ks = jax.random.split(key, 6)
        B, T, C = (8, 256, DIM)
        x = jax.random.normal(ks[0], (B, T, C), dtype=jnp.float32)
        s = 1.0 / np.sqrt(C)
        W_r = jax.random.uniform(ks[1], (C, C), jnp.float32, -s, s)
        W_k = jax.random.uniform(ks[2], (C, C), jnp.float32, -s, s)
        W_v = jax.random.uniform(ks[3], (C, C), jnp.float32, -s, s)
        mu_r = jax.random.uniform(ks[4], (C,), jnp.float32)
        mu_k = jax.random.uniform(ks[5], (C,), jnp.float32)
        return {'x': x, 'W_r': W_r, 'W_k': W_k, 'W_v': W_v, 'mu_r': mu_r, 'mu_k': mu_k}
    _L1_ffn_in = _L1_ffn_setup()
    _d = {'L0_attn_x': _L0_attn_in['x'], 'L0_attn_w_dw': _L0_attn_in['w_dw'], 'L0_attn_w_pw': _L0_attn_in['w_pw'], 'L0_attn_w_qkv': _L0_attn_in['w_qkv'], 'L0_attn_w_o': _L0_attn_in['w_o'], 'L0_attn_w_gate': _L0_attn_in['w_gate'], 'L0_attn_b_gate': _L0_attn_in['b_gate'], 'L0_attn_ln_g': _L0_attn_in['ln_g'], 'L0_attn_ln_b': _L0_attn_in['ln_b'], 'L0_attn_w_moe_gate': _L0_attn_in['w_moe_gate'], 'L0_attn_w1': _L0_attn_in['w1'], 'L0_attn_b1': _L0_attn_in['b1'], 'L0_attn_w2': _L0_attn_in['w2'], 'L0_attn_b2': _L0_attn_in['b2'], 'L0_ffn_Wg': _L0_ffn_in['Wg'], 'L0_ffn_W1': _L0_ffn_in['W1'], 'L0_ffn_b1': _L0_ffn_in['b1'], 'L0_ffn_W2': _L0_ffn_in['W2'], 'L0_ffn_b2': _L0_ffn_in['b2'], 'L1_attn_qkv': _L1_attn_in['qkv'], 'L1_attn_q_bias': _L1_attn_in['q_bias'], 'L1_attn_positional': _L1_attn_in['positional'], 'L1_attn_out_kernel': _L1_attn_in['out_kernel'], 'L1_attn_out_bias': _L1_attn_in['out_bias'], 'L1_ffn_W_r': _L1_ffn_in['W_r'], 'L1_ffn_W_k': _L1_ffn_in['W_k'], 'L1_ffn_W_v': _L1_ffn_in['W_v'], 'L1_ffn_mu_r': _L1_ffn_in['mu_r'], 'L1_ffn_mu_k': _L1_ffn_in['mu_k']}
    _x0 = _d['L0_attn_x']
    _d['L0_attn_x'] = jax.random.normal(jax.random.fold_in(jax.random.key(seed), 1), (1, 2048, 128), dtype=_x0.dtype)
    del _x0
    return _d

def reference(L0_attn_x, L0_attn_w_dw, L0_attn_w_pw, L0_attn_w_qkv, L0_attn_w_o, L0_attn_w_gate, L0_attn_b_gate, L0_attn_ln_g, L0_attn_ln_b, L0_attn_w_moe_gate, L0_attn_w1, L0_attn_b1, L0_attn_w2, L0_attn_b2, L0_ffn_Wg, L0_ffn_W1, L0_ffn_b1, L0_ffn_W2, L0_ffn_b2, L1_attn_qkv, L1_attn_q_bias, L1_attn_positional, L1_attn_out_kernel, L1_attn_out_bias, L1_ffn_W_r, L1_ffn_W_k, L1_ffn_W_v, L1_ffn_mu_r, L1_ffn_mu_k):

    def _L0_attn_ref(x, w_dw, w_pw, w_qkv, w_o, w_gate, b_gate, ln_g, ln_b, w_moe_gate, w1, b1, w2, b2):
        import jax, jax.numpy as jnp
        import numpy as np
        D_MODEL = 128
        N_HEADS = 16
        HEAD_DIM = D_MODEL // N_HEADS
        N_EXPERTS = 4
        HIDDEN = 4 * D_MODEL
        B, T = (1, 256)

        def _apply_rope(x, sin, cos):
            x1, x2 = (x[..., ::2], x[..., 1::2])
            r1 = x1 * cos - x2 * sin
            r2 = x1 * sin + x2 * cos
            return jnp.stack((r1, r2), axis=-1).reshape(x.shape)
        Bv, Tv, d = x.shape
        H, Dh = (N_HEADS, HEAD_DIM)
        dt = x.dtype
        xp = jnp.pad(x, ((0, 0), (2, 0), (0, 0)))
        y = xp[:, 0:Tv] * w_dw[:, 0] + xp[:, 1:Tv + 1] * w_dw[:, 1] + xp[:, 2:Tv + 2] * w_dw[:, 2]
        y = jnp.einsum('btd,ed->bte', y, w_pw)
        x = x + y
        qkv = jnp.einsum('btd,ed->bte', x, w_qkv).reshape(Bv, Tv, 3, H, Dh)
        q, k, v = (qkv[:, :, 0], qkv[:, :, 1], qkv[:, :, 2])
        inv_freq = 1.0 / 10000.0 ** (jnp.arange(0, Dh, 2, dtype=dt) / Dh)
        pos = jnp.arange(Tv, dtype=dt)
        theta = pos[:, None] * inv_freq[None, :]
        sin = jnp.sin(theta)[None, :, None, :]
        cos = jnp.cos(theta)[None, :, None, :]
        q = _apply_rope(q, sin, cos)
        k = _apply_rope(k, sin, cos)
        q_phi = jax.nn.elu(q) + 1.0
        k_phi = jax.nn.elu(k) + 1.0
        kv = k_phi[..., :, None] * v[..., None, :]
        kv_prefix = jnp.cumsum(kv, axis=1)
        k_prefix = jnp.cumsum(k_phi, axis=1)
        num = jnp.einsum('bthd,bthdm->bthm', q_phi, kv_prefix)
        denom = jnp.sum(q_phi * k_prefix, axis=-1, keepdims=True)
        attn = num / (denom + 1e-06)
        attn = attn.reshape(Bv, Tv, d)
        attn = jnp.einsum('btd,ed->bte', attn, w_o)
        delta = x - jnp.concatenate([x[:, :1], x[:, :-1]], axis=1)
        gate = jax.nn.sigmoid(jnp.einsum('btd,ed->bte', delta, w_gate) + b_gate)
        x = x + gate * attn
        mu = jnp.mean(x, axis=-1, keepdims=True)
        var = jnp.mean((x - mu) ** 2, axis=-1, keepdims=True)
        h = (x - mu) / jnp.sqrt(var + 1e-05) * ln_g + ln_b
        gw = jax.nn.softmax(jnp.einsum('btd,ed->bte', h, w_moe_gate), axis=-1)
        hid = jax.nn.silu(jnp.einsum('btd,efd->btef', h, w1) + b1)
        eo = jnp.einsum('btef,edf->bted', hid, w2) + b2
        ffn = jnp.einsum('bte,bted->btd', gw, eo)
        return x + ffn

    def _L0_ffn_ref(x, Wg, W1, b1, W2, b2):
        import math
        import jax, jax.numpy as jnp
        import numpy as np
        B, T, D, N, H = (8, 256, 128, 16, 256)
        CAP_FACTOR = 1.25
        b, t, d = x.shape
        n = Wg.shape[1]
        bt = b * t
        cap = math.ceil(CAP_FACTOR * bt / n)
        logits = jnp.einsum('btd,dn->btn', x, Wg)
        probs = jax.nn.softmax(logits, axis=-1)
        top1_val = probs.max(axis=-1).reshape(bt)
        top1_idx = probs.argmax(axis=-1).reshape(bt)
        x_flat = x.reshape(bt, d)
        masked = jnp.where(top1_idx[None, :] == jnp.arange(n)[:, None], top1_val[None, :], -jnp.inf)
        vals, idx = jax.lax.top_k(masked, cap)
        valid = jnp.isfinite(vals)
        xe = x_flat[idx]
        h = jax.nn.gelu(jnp.einsum('ncd,ndh->nch', xe, W1) + b1[:, None, :])
        out = jnp.einsum('nch,nhd->ncd', h, W2) + b2[:, None, :]
        safe_idx = jnp.where(valid, idx, bt)
        y_flat = x_flat.at[safe_idx.reshape(-1)].set(out.reshape(-1, d), mode='drop')
        return y_flat.reshape(b, t, d)

    def _L1_attn_ref(input, qkv, q_bias, positional, out_kernel, out_bias):
        import jax, jax.numpy as jnp
        import numpy as np
        HEADS, HEAD_SIZE, FREQS, MAX_PERIOD = (16, 64, 32, 1250)
        D_MODEL = 128
        NEG_INF = -1000000000.0

        def sinusoid_embedding(seq_len, frequencies, max_period):
            pos = np.arange(seq_len, dtype=np.float64)[:, None]
            idx = np.arange(frequencies)[None, :]
            inv_freq = max_period ** (-(idx // 2 * 2) / frequencies)
            angle = pos * inv_freq
            table = np.where(idx % 2 == 0, np.sin(angle), np.cos(angle))
            return table.astype(np.float32)

        def relative_causal(scores):
            L = scores.shape[-1]
            d = jnp.clip(jnp.arange(L)[:, None] - jnp.arange(L)[None, :], 0, L - 1)
            return jnp.take_along_axis(scores, d[None, None, :, :], axis=-1)
        b, s, x = input.shape
        n, h = (HEADS, HEAD_SIZE)
        w = qkv * (3.0 * x * h * n) ** (-0.25)
        q, k, v = jnp.einsum('bsx,xAnh->Abnsh', input, w)
        q = q + q_bias[:, None, :]
        a = jnp.einsum('bnqh,bnkh->bnqk', q, k) * h ** (-0.5)
        sins = jnp.asarray(np.sqrt(2.0) * sinusoid_embedding(s, FREQS, MAX_PERIOD))
        emb = jnp.einsum('sf,fnh->nsh', sins, positional * FREQS ** (-0.5))
        pos_scores = jnp.einsum('bnqh,nvh->bnqv', q, emb) * h ** (-0.5)
        a = a + relative_causal(pos_scores)
        mask = jnp.tril(jnp.ones((s, s), dtype=bool))
        a = jax.nn.softmax(jnp.where(mask, a, NEG_INF), axis=-1)
        o = jnp.einsum('bnqk,bnkh->bqnh', a, v).reshape(b, s, n * h)
        fan_in, fan_out = out_kernel.shape
        out = o @ (out_kernel * (fan_in * fan_out) ** (-0.25)) + out_bias
        return out

    def _L1_ffn_ref(x, W_r, W_k, W_v, mu_r, mu_k):
        import jax, jax.numpy as jnp
        import numpy as np
        DIM = 128

        def _reference_tuple_inner(x, W_r, W_k, W_v, mu_r, mu_k):
            B, T, C = x.shape
            x_prev = jnp.concatenate([jnp.zeros((B, 1, C), x.dtype), x[:, :-1, :]], axis=1)
            xr = mu_r * x + (1.0 - mu_r) * x_prev
            xk = mu_k * x + (1.0 - mu_k) * x_prev
            r = jax.nn.sigmoid(jnp.einsum('btc,dc->btd', xr, W_r))
            k = jnp.einsum('btc,dc->btd', xk, W_k)
            k_act = jnp.square(jax.nn.relu(k))
            out = r * jnp.einsum('btc,dc->btd', k_act, W_v)
            new_state = x[:, -1, :]
            return (out, new_state)
        return _reference_tuple_inner(x, W_r, W_k, W_v, mu_r, mu_k)[0]
    x = L0_attn_x
    xn = _layernorm(x, axis=-1)
    s = _L0_attn_ref(xn, L0_attn_w_dw, L0_attn_w_pw, L0_attn_w_qkv, L0_attn_w_o, L0_attn_w_gate, L0_attn_b_gate, L0_attn_ln_g, L0_attn_ln_b, L0_attn_w_moe_gate, L0_attn_w1, L0_attn_b1, L0_attn_w2, L0_attn_b2)
    g = _silu(_L0_ffn_ref(xn, L0_ffn_Wg, L0_ffn_W1, L0_ffn_b1, L0_ffn_W2, L0_ffn_b2))
    x = x + s * g
    xn = _layernorm(x, axis=-1)
    s = _L1_attn_ref(xn, L1_attn_qkv, L1_attn_q_bias, L1_attn_positional, L1_attn_out_kernel, L1_attn_out_bias)
    g = _silu(_L1_ffn_ref(xn, L1_ffn_W_r, L1_ffn_W_k, L1_ffn_W_v, L1_ffn_mu_r, L1_ffn_mu_k))
    x = x + s * g
    return x

_drawn_inputs = setup_inputs


def setup_inputs(seed=0):
    import zlib

    import numpy as np

    out = dict(_drawn_inputs(seed))
    spreads = {'L0_attn_b_gate': (0.0, 0.1),
     'L0_attn_ln_g': (1.0, 0.2),
     'L0_attn_ln_b': (0.0, 0.1),
     'L0_attn_b1': (0.0, 0.1),
     'L0_attn_b2': (0.0, 0.1),
     'L0_ffn_b1': (0.0, 0.1),
     'L0_ffn_b2': (0.0, 0.1),
     'L1_attn_q_bias': (0.0, 0.1),
     'L1_attn_out_bias': (0.0, 0.1)}
    factors = {}
    for name, (base, spread) in spreads.items():
        noise = np.random.default_rng([zlib.crc32(name.encode()), seed]).standard_normal(out[name].shape)
        drawn = base * np.exp(spread * noise) if base else spread * noise
        out[name] = jnp.asarray(drawn.astype(out[name].dtype))
    for name, factor in factors.items():
        out[name] = (out[name] * factor).astype(out[name].dtype)
    return out
```

```python
from contextlib import ExitStack

import numpy as np
import concourse.bass as bass
from concourse import mybir

F32 = mybir.dt.float32
F32R = mybir.dt.float32r
BF16 = mybir.dt.bfloat16
F16 = mybir.dt.float16
ACT = mybir.ActivationFunctionType
ALU = mybir.AluOpType
AX_X = mybir.AxisListType.X

P = 128
T = 2048
D = 128
NT = T // P
CW = 512
NC = T // CW
TPC = CW // P
HEADS, HS, FREQS = 16, 64, 32
PAIRS = HEADS // 2
VW = 2 * HS + 1
C_QKV = (3.0 * D * HEADS * HS) ** -0.25
C_OUT = (HEADS * HS * D) ** -0.25
EPS = 1e-5

MH, MD = 16, 8
ME, MHID = 4, 4 * D
HB = MHID // P
RE, RH2 = 16, 2
CAP = -(-5 * T // (4 * RE))
SLOT_ROWS = RE * CAP
XT_ = SLOT_ROWS // P
EPS_DEN = 1e-6
I32 = mybir.dt.int32

B_TILES = [(c, j) for c in range(NC) for j in range(TPC * (c + 1))]
A_TILES = [(i, cc) for i in range(NT) for cc in range(i // TPC + 1)]
NB = len(B_TILES)
LEAD = 8


def a_end(c):
    return sum(i // TPC + 1 for i in range(TPC * (c + 1)))


SLOTS = 2 * NB
DRAIN = 2
A_SLOTS = ([(0, NB - LEAD + n) for n in range(LEAD)] + [(1, n) for n in range(NB)]
           + [(2, n) for n in range(NB - LEAD)])


def plan_items(last):
    items = {n: [] for n in range(SLOTS)}
    items[4].append(("turn", -1, 3))
    items[7].append(("project", -1, 3))
    for n, a in enumerate(A_SLOTS):
        if last and a[0] == 2:
            continue
        for c in range(NC):
            if a[1] == a_end(c) - 1 and n + 2 < SLOTS:
                items[n + 2].append(("maxima", a[0], c))
    if not last:
        n = LEAD + 5
        for c in range(NC):
            for kind in ("q", "k", "pos", "v", "possum"):
                while items[n]:
                    n += 1
                items[n].append((kind, 1, c))
                n += 1
        assert n <= NB
    for c in range(NC - 1):
        n = NB + sum(TPC * (k + 1) for k in range(c + 1)) + DRAIN + 3
        while items[n]:
            n += 1
        items[n].append(("turn", 0, c))
        n += 3
        while items[n]:
            n += 1
        items[n].append(("project", 0, c))
    return items


class Bank:

    def __init__(self):
        self.n = 0
        self.of_bank = [0, 0]

    def take(self):
        bank = self.n % 2
        got = (self.n, bank, self.of_bank[bank])
        self.n += 1
        self.of_bank[bank] += 1
        return got



def ahead(p):
    return isinstance(p, int) and p == -1


def raw(ap):
    return ap.bitcast(F32)


def layernorm(dve, step, s_ln, s_sqrt, tok, stats, mv, vare, std, rstd, newt):
    for i in range(NT):
        ins = dve.bn_stats(stats[:, i, :], tok[:, i, :])
    step(ins)
    for i in range(NT):
        ins = dve.bn_aggr(mv[:, i, :], stats[:, i, :])
    step(ins)
    dve.tensor_scalar(vare[:], mv[:, :, 1], EPS, None, ALU.add).then_inc(s_ln, 1)
    dve.wait_ge(s_sqrt, 1)
    step(dve.reciprocal(rstd[:], std[:]))
    step(dve.tensor_tensor(newt[:], rstd[:], rstd[:], ALU.mult))
    step(dve.tensor_tensor(newt[:], newt[:], vare[:], ALU.mult))
    step(dve.tensor_scalar(newt[:], newt[:], -0.5, 1.5, ALU.mult, ALU.add))
    step(dve.tensor_tensor(rstd[:], rstd[:], newt[:], ALU.mult))


def mixer0(nc, dram, keep, t0):
    ident = keep["ident"]
    x_tok, xn_tok, xnT, x2T = t0["x_tok"], t0["xn_tok"], t0["xnT"], t0["x2T"]
    with ExitStack() as ctx:
        def sb(name, shape, dt=F32):
            return ctx.enter_context(nc.sbuf_tensor(name, shape, dt))

        def sem(name):
            return ctx.enter_context(nc.semaphore(name))

        stats, mv = sb("stats0", [P, NT, 6]), sb("mv0", [P, NT, 2])
        vare, std, rstd, newt = (sb(n + "0", [P, NT]) for n in ("vare", "std", "rstd", "newt"))
        w_dw, w_sq = sb("w_dw", [P, 3]), sb("w_sq", [P, 7, D])
        b_gate = sb("b_gate", [P, 1])
        w_vrep = sb("w_vrep", [P, MD, P])
        cos, sin = sb("cos0", [P, T]), sb("sin0", [P, T])
        sel = sb("sel0", [P, MD + 1, P])
        ones = sb("ones0", [P, CW])
        x1T = sb("x1T", [P, T + 1])
        y = sb("y0", [P, 2, CW])
        qk = sb("qk0", [P, 2, CW])
        qk2 = sb("qk20", [P, 2, CW])
        neg = sb("neg0", [P, 2, CW])
        phi = sb("phi0", [P, 2, 2, CW])
        delta = sb("delta0", [P, 2, CW])
        gate = sb("gate0", [P, 2, CW])
        kv = sb("kv0", [P, 2, CW])
        cum = sb("cum0", [P, 3, CW])
        last = sb("last0", [P, MD + 1])
        z = sb("z0", [P, 3, CW])
        den, attn = sb("den0", [P, CW]), sb("attn0", [P, CW])
        G = [ctx.enter_context(nc.psum_tensor(f"G{i}", [P, CW], F32)) for i in range(4)]
        V = [ctx.enter_context(nc.psum_tensor(f"VB{i}", [P, CW], F32)) for i in range(2)]
        N = ctx.enter_context(nc.psum_tensor("NB", [P, CW], F32))
        DEN = ctx.enter_context(nc.psum_tensor("DB", [P, CW], F32))

        s_x, s_w, s_v = sem("x_loaded"), sem("w0_loaded"), sem("dve_step0")
        s_ln, s_sqrt, s_xn = sem("ln_var0"), sem("ln_sqrt0"), sem("xn_tiles0")
        s_pad = sem("pads0")
        s_g, s_gf = sem("general_sums0"), [sem(f"general_out{i}") for i in range(4)]
        s_xnT, s_y, s_x1 = sem("xnT_chunks"), sem("conv_chunks"), sem("x1T_chunks")
        s_rot, s_sum, s_exp, s_phi = sem("rotated"), sem("rot_summed"), sem("phi_exp"), sem("phi_done")
        s_relu = sem("phi_relu")
        s_delta, s_gate = sem("deltas"), sem("gates0")
        s_vr, s_kv, s_cum, s_z = sem("v_rows"), sem("kv_products"), sem("prefixes"), sem("q_products")
        s_last = sem("last_columns")
        s_zu, s_num, s_attn, s_x2 = sem("products_summed"), sem("numerators"), sem("attn_chunks"), sem("x2_chunks")

        order = [("T", 0), ("T", 1), ("T", 2), ("T", 3)]
        phases = [("P", 0), ("P", 1), ("S", 0), ("P", 2), ("S", 1), ("P", 3), ("S", 2), ("S", 3)]
        for kind, c in phases:
            order += [(k, c) for k in (("Y", "Q", "QS", "K", "KS", "G") if kind == "P" else ("O",))]
        number = {k: n for n, k in enumerate(order)}
        SC = MD + 1
        block = ctx.enter_context(nc.Block())

        def bank(k):
            return G[number[k] % 4]

        def span(c, off=0):
            return slice(off + c * CW, off + (c + 1) * CW)

        @block.sync
        def _(sp):
            sp.dma_start(x_tok[:], dram["x"].rearrange("(n p) d -> p n d", p=P)).then_inc(s_x, 16)
            for dst, src in ((w_dw, "w_dw"), (w_sq, "w_sq"), (cos, "cos0"), (sin, "sin0"), (b_gate, "b_gate"),
                             (w_vrep, "w_vrep"), (sel, "sel0")):
                sp.dma_start(dst[:], dram[src]).then_inc(s_w, 16)
        WLOAD = 16 * 7

        @block.tensor
        def _(pe):
            def begin(k):
                n = number[k]
                if n >= 4:
                    pe.wait_ge(s_gf[n % 4], n // 4)

            for c in range(NC):
                begin(("T", c))
                for i in range(TPC):
                    pe.wait_ge(s_xn, TPC * c + i + 1)
                    ins = pe.transpose(bank(("T", c))[:, i * P:(i + 1) * P], xn_tok[:, TPC * c + i, :], ident[:])
                ins.then_inc(s_g, 1)
            pe.wait_ge(s_w, WLOAD)

            def project(k, w, rhs):
                begin(k)
                pe.matmul(bank(k)[:], w_sq[:, w, :], rhs, start=True, stop=True).then_inc(s_g, 1)

            for kind, c in phases:
                if kind == "P":
                    pe.wait_ge(s_y, c + 1)
                    project(("Y", c), 0, y[:, c % 2, :])
                    pe.wait_ge(s_x1, c + 1)
                    for w, k in enumerate(("Q", "QS", "K", "KS")):
                        project((k, c), w + 1, x1T[:, span(c, 1)])
                    pe.wait_ge(s_delta, c + 1)
                    project(("G", c), 5, delta[:, c % 2, :])
                else:
                    def product(m):
                        pe.wait_ge(s_z, SC * c + m + 1)
                        out = DEN if m == MD else N
                        if c > 0 and m == 0:
                            pe.wait_ge(s_attn, c)
                        pe.matmul(out[:], sel[:, m, :], z[:, (SC * c + m) % 3, :], start=m in (0, MD),
                                  stop=m >= MD - 1).then_inc(s_zu, 1)
                    for m in range(MD):
                        g = MD * c + m
                        if g >= 2:
                            pe.wait_ge(s_kv, g - 1)
                        pe.matmul(V[g % 2][:], w_vrep[:, m, :], x1T[:, span(c, 1)], start=True, stop=True).then_inc(s_vr, 1)
                        if m >= 2:
                            product(m - 2)
                    for m in range(MD - 2, SC):
                        product(m)
                    pe.wait_ge(s_attn, c + 1)
                    project(("O", c), 6, attn[:])

        @block.scalar
        def _(act):
            act.wait_ge(s_ln, 1)
            act.activation(std[:], vare[:], ACT.Sqrt).then_inc(s_sqrt, 1)
            for c in range(NC):
                act.wait_ge(s_g, number[("T", c)] + 1)
                act.activation(xnT[:, span(c, 2)], bank(("T", c))[:], ACT.Copy).then_inc(s_xnT, 1)
                act.wait_ge(s_xnT, c + 1)
                act.sem_inc(s_gf[c], 1)
            act.wait_ge(s_w, WLOAD)
            for kind, c in phases:
                if kind != "P":
                    continue
                for j in range(2):
                    act.wait_ge(s_sum, 2 * c + j + 1)
                    act.activation(neg[:, j, :], qk[:, j, :], ACT.Relu, scale=-1.0).then_inc(s_relu, 1)
                    act.wait_ge(s_relu, 2 * c + j + 1)
                    act.activation(neg[:, j, :], neg[:, j, :], ACT.Exp, scale=-1.0).then_inc(s_exp, 1)
                k = ("G", c)
                act.wait_ge(s_g, number[k] + 1)
                if c >= 2:
                    act.wait_ge(s_x2, c - 1)
                act.activation(gate[:, c % 2, :], bank(k)[:], ACT.Sigmoid, bias=b_gate[:, 0:1]).then_inc(s_gate, 1)
                act.wait_ge(s_gate, c + 1)
                act.sem_inc(s_gf[number[k] % 4], 1)

        @block.gpsimd
        def _(pool):
            pool.memset(ones[:], 1.0)
            pool.memset(xnT[:, 0:2], 0.0).then_inc(s_pad, 1)
            for kind, c in phases:
                if kind == "P":
                    for j in range(2):
                        pool.wait_ge(s_rot, 2 * (2 * c + j) + 2)
                        pool.tensor_tensor(qk[:, j, :], qk[:, j, :], qk2[:, j, :], ALU.add).then_inc(s_sum, 1)
                else:
                    for m in range(SC):
                        g = SC * c + m
                        pool.wait_ge(s_cum, g + 1)
                        if g >= 3:
                            pool.wait_ge(s_zu, g - 2)
                        pool.tensor_tensor(z[:, g % 3, :], cum[:, g % 3, :], phi[:, c % 2, 0, :], ALU.mult).then_inc(s_z, 1)

        @block.vector
        def _(dve):
            steps = [0]

            def step(ins):
                steps[0] += 1
                ins.then_inc(s_v, 1)
                dve.wait_ge(s_v, steps[0])

            dve.wait_ge(s_x, 16)
            layernorm(dve, step, s_ln, s_sqrt, x_tok, stats, mv, vare, std, rstd, newt)
            for i in range(NT):
                dve.tensor_scalar(xn_tok[:, i, :], x_tok[:, i, :], mv[:, i, 0:1], rstd[:, i:i + 1], ALU.subtract,
                                  ALU.mult).then_inc(s_xn, 1)
            dve.memset(last[:], 0.0).then_inc(s_last, 1)
            dve.wait_ge(s_w, WLOAD)
            dve.wait_ge(s_pad, 1)

            def free(k, ins):
                ins.then_inc(s_gf[number[k] % 4], 1)

            for kind, c in phases:
                if kind == "P":
                    dve.wait_ge(s_xnT, c + 1)
                    if c >= 2:
                        dve.wait_ge(s_g, number[("Y", c - 2)] + 1)
                    yc = y[:, c % 2, :]
                    step(dve.tensor_scalar(yc, xnT[:, span(c, 0)], w_dw[:, 0:1], None, ALU.mult))
                    step(dve.scalar_tensor_tensor(yc, xnT[:, span(c, 1)], w_dw[:, 1:2], yc, ALU.mult, ALU.add))
                    dve.scalar_tensor_tensor(yc, xnT[:, span(c, 2)], w_dw[:, 2:3], yc, ALU.mult, ALU.add).then_inc(s_y, 1)
                    dve.wait_ge(s_g, number[("Y", c)] + 1)
                    dve.tensor_tensor(x1T[:, span(c, 1)], bank(("Y", c))[:], xnT[:, span(c, 2)], ALU.add).then_inc(s_x1, 1)
                    dve.wait_ge(s_x1, c + 1)
                    dve.sem_inc(s_gf[number[("Y", c)] % 4], 1)
                    if c == 0:
                        step(dve.tensor_copy(x1T[:, 0:1], x1T[:, 1:2]))
                    if c >= 2:
                        dve.wait_ge(s_g, number[("G", c - 2)] + 1)
                    dve.tensor_tensor(delta[:, c % 2, :], x1T[:, span(c, 1)], x1T[:, span(c, 0)], ALU.subtract).then_inc(s_delta, 1)
                    for j, k in enumerate(("Q", "K")):
                        if c > 0:
                            dve.wait_ge(s_phi, 2 * (c - 1) + j + 1)
                            dve.wait_ge(s_exp, 2 * (c - 1) + j + 1)
                        for t, kk, tab in ((qk, k, cos), (qk2, k + "S", sin)):
                            dve.wait_ge(s_g, number[(kk, c)] + 1)
                            ins = dve.tensor_tensor(t[:, j, :], bank((kk, c))[:], tab[:, span(c)], ALU.mult)
                            ins.then_inc(s_rot, 1)
                            dve.wait_ge(s_rot, 2 * (2 * c + j) + (1 if t is qk else 2))
                            dve.sem_inc(s_gf[number[(kk, c)] % 4], 1)
                    for j in range(2):
                        dve.wait_ge(s_exp, 2 * c + j + 1)
                        if c >= 2:
                            dve.wait_ge(s_z, SC * (c - 1))
                        dve.scalar_tensor_tensor(phi[:, c % 2, j, :], qk[:, j, :], 0.0, neg[:, j, :], ALU.max,
                                                 ALU.add).then_inc(s_phi, 1)
                else:
                    dve.wait_ge(s_phi, 2 * c + 2)
                    kphi = phi[:, c % 2, 1, :]
                    for m in range(SC):
                        g = SC * c + m
                        if m < MD:
                            gv = MD * c + m
                            dve.wait_ge(s_vr, gv + 1)
                            dve.wait_ge(s_cum, g) if g > 0 else None
                            dve.tensor_tensor(kv[:, gv % 2, :], V[gv % 2][:], kphi, ALU.mult).then_inc(s_kv, 1)
                            dve.wait_ge(s_kv, gv + 1)
                            src = kv[:, gv % 2, :]
                        else:
                            src = kphi
                        if g >= 3:
                            dve.wait_ge(s_z, g - 2)
                        dve.wait_ge(s_last, max(1, g - SC + 2))
                        dve.tensor_tensor_scan(cum[:, g % 3, :], ones[:], src, last[:, m:m + 1], ALU.mult,
                                               ALU.add).then_inc(s_cum, 1)
                        dve.wait_ge(s_cum, g + 1)
                        dve.tensor_copy(last[:, m:m + 1], cum[:, g % 3, CW - 1:CW]).then_inc(s_last, 1)
                    dve.wait_ge(s_zu, SC * (c + 1))
                    if c > 0:
                        dve.wait_ge(s_g, number[("O", c - 1)] + 1)
                    step(dve.tensor_scalar(den[:], DEN[:], EPS_DEN, None, ALU.add))
                    step(dve.reciprocal(den[:], den[:]))
                    dve.tensor_tensor(attn[:], N[:], den[:], ALU.mult).then_inc(s_attn, 1)
                    dve.wait_ge(s_attn, c + 1)
                    dve.wait_ge(s_g, number[("O", c)] + 1)
                    dve.wait_ge(s_gate, c + 1)
                    step(dve.tensor_tensor(x2T[:, span(c)], bank(("O", c))[:], gate[:, c % 2, :], ALU.mult))
                    dve.sem_inc(s_gf[number[("O", c)] % 4], 1)
                    dve.tensor_tensor(x2T[:, span(c)], x2T[:, span(c)], x1T[:, span(c, 1)], ALU.add).then_inc(s_x2, 1)


def experts0(nc, dram, keep, t0):
    ident = keep["ident"]
    xn_tok, xnT, x2T, s_tok = t0["xn_tok"], t0["xnT"], t0["x2T"], t0["s_tok"]
    slot, y_tok, xe = t0["slot"], t0["y_tok"], t0["xe"]
    with ExitStack() as ctx:
        def sb(name, shape, dt=F32):
            return ctx.enter_context(nc.sbuf_tensor(name, shape, dt))

        def sem(name):
            return ctx.enter_context(nc.semaphore(name))

        stats, mv = sb("stats0b", [P, NT, 6]), sb("mv0b", [P, NT, 2])
        vare, std, rstd, newt = (sb(n + "0b", [P, NT]) for n in ("vare", "std", "rstd", "newt"))
        lng, lnb = sb("ln_g", [P, 1]), sb("ln_b", [P, 1])
        w_mg = sb("w_mg", [P, ME])
        w1, b1 = sb("w1_0", [P, ME * HB, P]), sb("b1_0", [P, ME * HB])
        w2, b2 = sb("w2_0", [P, ME * HB, D]), sb("b2_0", [ME, D])
        wg = sb("wg0", [P, RE])
        rank_order, below = sb("rank_order", [P, RE]), sb("below", [P, P])
        h_tok, hT = sb("h_tok", [P, NT, D]), sb("hT", [P, T])
        hid = sb("hid0", [P, 2, HB, CW])
        rdiff, rexp = sb("rdiff", [P, NT, RE]), sb("rexp", [P, NT, RE])
        cand, onehot = sb("cand", [P, NT, RE]), sb("onehot", [P, NT, RE])
        rmax, rsum, val, r1, r2, cmax, rank, over, slotf = (
            sb(n, [P, NT]) for n in ("rmax", "rsum0", "val", "r1", "r2", "cmax", "rank", "over", "slotf"))
        vparts_b, vparts = sb("vparts_b", [P, 2, NT], BF16), sb("vparts", [P, 3, NT])
        OH3, MV3 = sb("OH3", [P, NT, 3, RE]), sb("MV3", [P, NT, 3, RE])
        ohT, mvT = sb("ohT", [3 * RE, T], BF16), sb("mvT", [3 * RE, T], BF16)
        counts = sb("counts", [P, NT, NC + 2])
        seen = sb("seen", [P, CW])
        gdiff, gexp, gw = sb("gdiff", [P, NT, ME]), sb("gexp", [P, NT, ME]), sb("gw", [P, NT, ME])
        gmax, gsum = sb("gmax", [P, NT]), sb("gsum", [P, NT])
        gwT = sb("gwT", [ME, T])
        zero = sb("zero0", [P, P])
        G = [ctx.enter_context(nc.psum_tensor(f"EG{i}", [P, CW], F32)) for i in range(2)]
        H = [ctx.enter_context(nc.psum_tensor(f"EH{i}", [P, CW], F32)) for i in range(2)]
        E = [ctx.enter_context(nc.psum_tensor(f"EE{i}", [P, CW], F32)) for i in range(2)]
        R = [ctx.enter_context(nc.psum_tensor(f"ER{i}", [P, CW], F32)) for i in range(2)]

        s_w, s_v = sem("w0b_loaded"), sem("dve_step0b")
        s_ln, s_sqrt, s_hn = sem("ln_var0b"), sem("ln_sqrt0b"), sem("h_tiles")
        s_g, s_gf = sem("general_sums0b"), [sem(f"general_outb{i}") for i in range(2)]
        s_x2, s_hT = sem("x2_tokens"), sem("hT_chunks")
        s_rd, s_re = sem("route_diff"), sem("route_exp")
        s_oh, s_ohT = sem("onehots"), sem("onehots_turned")
        s_gd, s_ge, s_gw = sem("gate_diff"), sem("gate_exp"), sem("gate_weights")
        s_gwT, s_b2 = sem("gate_turned"), sem("bias_added")
        s_h, s_hid, s_e, s_acc = sem("hidden_sums"), sem("hidden"), sem("expert_sums"), sem("expert_added")
        s_r, s_rc = sem("route_rows"), sem("route_counted")
        s_slot, s_zero, s_fill = sem("slots"), sem("zero_set"), sem("slots_filled")
        s_sc, s_xe, s_y = sem("tokens_sent"), sem("tokens_back"), sem("y_filled")
        WLOAD = 16 * 11

        order = ([("RL", 0)] + [("X", c) for c in range(NC)] + [("OT", c) for c in range(NC)] + [("MT", c) for c in range(NC)]
                 + [("HT", c) for c in range(NC)] + [("GL", 0)] + [("GT", c) for c in range(NC)]
                 + [("B2", c) for c in range(NC)])
        number = {k: n for n, k in enumerate(order)}

        def bank(k):
            return G[number[k] % 2]

        def span(c, off=0):
            return slice(off + c * CW, off + (c + 1) * CW)

        def tiles(c):
            return slice(TPC * c, TPC * (c + 1))

        def t4(ap):
            return ap.rearrange("p (n d) -> p n d", n=TPC)

        UNITS = [(i, cc) for i in range(NT) for cc in range(NC)]
        GROUPS = [(c, e) for c in range(NC) for e in range(ME)]
        PER_HB = 2
        block = ctx.enter_context(nc.Block())

        @block.sync
        def _(sp):
            for dst, src in ((wg, "wg"), (rank_order, "rank_order"), (lng, "ln_g"), (lnb, "ln_b"), (w_mg, "w_mg"),
                             (w1, "w1"), (b1, "b1"), (w2, "w2"), (b2, "b2"), (below, "below")):
                sp.dma_start(dst[:], dram[src]).then_inc(s_w, 16)
            sp.dma_start(t0["W1"][:], dram["W1"]).then_inc(s_w, 16)
            sp.wait_ge(s_zero, 1)
            sp.dma_start(dram["xe_rows"].rearrange("(n p) d -> p n d", p=P),
                         zero[:].unsqueeze(1).to_broadcast([P, XT_, P])).then_inc(s_fill, 16)
            for dst, src in ((t0["W2"], "W2"), (t0["be1"], "be1"), (t0["be2"], "be2")):
                sp.dma_start(dst[:], dram[src]).then_inc(s_fill, 16)
            sp.wait_ge(s_sc, 16 * NT)
            sp.dma_start(xe[:], dram["xe_rows"].rearrange("(n p) d -> p n d", p=P)).then_inc(s_xe, 16)
            sp.wait_ge(s_xe, 16)

        @block.gpsimd
        def _(pool):
            pool.memset(zero[:], 0.0).then_inc(s_zero, 1)
            pool.tensor_copy(y_tok[:], xn_tok[:]).then_inc(s_y, 1)
            pool.wait_ge(s_fill, 64)
            pool.wait_ge(s_slot, 1)
            for i in range(NT):
                pool.indirect_dma_start(dram["xe_rows"], bass.IndirectOffsetOnAxis(slot[:, i:i + 1], 0), xn_tok[:, i, :], None,
                                        bounds_check=SLOT_ROWS - 1, oob_is_err=False).then_inc(s_sc, 16)
            pool.wait_ge(s_sc, 16 * NT)

        @block.tensor
        def _(pe):
            def begin(k):
                n = number[k]
                if n >= 2:
                    pe.wait_ge(s_gf[n % 2], n // 2)

            def turn(k, src, rows=P, waits=None):
                begin(k)
                for i in range(TPC):
                    t = TPC * k[1] + i
                    if waits is not None:
                        pe.wait_ge(waits, t + 1)
                    ins = pe.transpose(bank(k)[0:rows, i * P:(i + 1) * P], src(t), ident[:])
                ins.then_inc(s_g, 1)

            pe.wait_ge(s_w, WLOAD)
            for i in range(NT):
                ins = pe.matmul(bank(("RL", 0))[:, i * RE:(i + 1) * RE], xnT[:, 2 + i * P:2 + (i + 1) * P], wg[:],
                                start=True, stop=True)
            ins.then_inc(s_g, 1)
            for c in range(NC):
                turn(("X", c), lambda t: x2T[:, t * P:(t + 1) * P])
            pe.wait_ge(s_oh, 1)
            for c in range(NC):
                turn(("OT", c), lambda t: OH3[:, t, :, :].rearrange("p a b -> p (a b)"), 3 * RE)
            for c in range(NC):
                turn(("MT", c), lambda t: MV3[:, t, :, :].rearrange("p a b -> p (a b)"), 3 * RE)
            for c in range(NC):
                turn(("HT", c), lambda t: h_tok[:, t, :], P, s_hn)
            pe.wait_ge(s_hT, NC)
            begin(("GL", 0))
            for i in range(NT):
                ins = pe.matmul(bank(("GL", 0))[:, i * ME:(i + 1) * ME], hT[:, i * P:(i + 1) * P], w_mg[:],
                                start=True, stop=True)
            ins.then_inc(s_g, 1)

            def bias_part():
                pe.wait_ge(s_gw, 1)
                for c in range(NC):
                    turn(("GT", c), lambda t: gw[:, t, :], ME)
                for c in range(NC):
                    pe.wait_ge(s_gwT, c + 1)
                    begin(("B2", c))
                    for i in range(TPC):
                        t = TPC * c + i
                        ins = pe.matmul(bank(("B2", c))[:, i * P:(i + 1) * P], gwT[:, t * P:(t + 1) * P], b2[:],
                                        start=True, stop=True)
                    ins.then_inc(s_g, 1)

            unit = [0]

            def route_rows():
                for _ in range(PER_HB):
                    u = unit[0]
                    if u >= len(UNITS):
                        return
                    i, cc = UNITS[u]
                    if u == 0:
                        pe.wait_ge(s_ohT, 2 * NC)
                    if u >= 2:
                        pe.wait_ge(s_rc, u - 1)
                    pe.matmul(R[u % 2][:], ohT[:, i * P:(i + 1) * P], mvT[:, span(cc)], start=True, stop=True).then_inc(s_r, 1)
                    unit[0] += 1

            def first(n):
                c, e = GROUPS[n]
                for hb in range(HB):
                    k = n * HB + hb
                    if k >= 2:
                        pe.wait_ge(s_hid, k - 1)
                    pe.matmul(H[k % 2][:], w1[:, e * HB + hb, :], hT[:, span(c)], start=True, stop=True).then_inc(s_h, 1)
                    route_rows()

            def second(n):
                c, e = GROUPS[n]
                pe.wait_ge(s_hid, (n + 1) * HB)
                if n >= 2:
                    pe.wait_ge(s_acc, n - 1)
                for i in range(TPC):
                    for hb in range(HB):
                        ins = pe.matmul(E[n % 2][:, i * P:(i + 1) * P], hid[:, n % 2, hb, i * P:(i + 1) * P],
                                        w2[:, e * HB + hb, :], start=hb == 0, stop=hb == HB - 1)
                ins.then_inc(s_e, 1)

            first(0)
            bias_part()
            for n in range(len(GROUPS)):
                if n + 1 < len(GROUPS):
                    first(n + 1)
                second(n)

        @block.scalar
        def _(act):
            def out(k, dst, src, sem_done, n_done, func=ACT.Copy, **kw):
                act.wait_ge(s_g, number[k] + 1)
                act.activation(dst, src, func, **kw).then_inc(sem_done, 1)
                act.wait_ge(sem_done, n_done)
                act.sem_inc(s_gf[number[k] % 2], 1)

            for c in range(NC):
                out(("X", c), s_tok[:, tiles(c), :], t4(bank(("X", c))[:]), s_x2, c + 1)
            act.wait_ge(s_rd, 1)
            act.activation(rexp[:], rdiff[:], ACT.Exp).then_inc(s_re, 1)
            for c in range(NC):
                out(("OT", c), ohT[:, span(c)], bank(("OT", c))[0:3 * RE, :], s_ohT, c + 1)
            for c in range(NC):
                out(("MT", c), mvT[:, span(c)], bank(("MT", c))[0:3 * RE, :], s_ohT, NC + c + 1)
            act.wait_ge(s_ln, 1)
            act.activation(std[:], vare[:], ACT.Sqrt).then_inc(s_sqrt, 1)
            for c in range(NC):
                out(("HT", c), hT[:, span(c)], bank(("HT", c))[:], s_hT, c + 1, ACT.Identity, bias=lnb[:, 0:1],
                    scale=lng[:, 0:1])

            def hidden(n):
                c, e = GROUPS[n]
                for hb in range(HB):
                    k = n * HB + hb
                    act.wait_ge(s_h, k + 1)
                    if n >= 2:
                        act.wait_ge(s_e, n - 1)
                    act.activation(hid[:, n % 2, hb, :], H[k % 2][:], ACT.Silu,
                                   bias=b1[:, e * HB + hb:e * HB + hb + 1]).then_inc(s_hid, 1)

            act.wait_ge(s_gd, 1)
            act.activation(gexp[:], gdiff[:], ACT.Exp).then_inc(s_ge, 1)
            hidden(0)
            for c in range(NC):
                out(("GT", c), gwT[:, span(c)], bank(("GT", c))[0:ME, :], s_gwT, c + 1)
            for n in range(1, len(GROUPS)):
                hidden(n)

        @block.vector
        def _(dve):
            steps = [0]

            def step(ins):
                steps[0] += 1
                ins.then_inc(s_v, 1)
                dve.wait_ge(s_v, steps[0])

            def bc(t, n):
                return t[:].unsqueeze(2).to_broadcast([P, NT, n])

            dve.memset(counts[:], 0.0)
            dve.wait_ge(s_w, WLOAD)
            L = bank(("RL", 0))[:, 0:NT * RE].rearrange("p (n e) -> p n e", n=NT)
            dve.wait_ge(s_g, 1)
            step(dve.tensor_reduce(rmax[:], L, AX_X, ALU.max))
            dve.tensor_tensor(rdiff[:], L, bc(rmax, RE), ALU.subtract).then_inc(s_rd, 1)
            step(dve.tensor_tensor(cand[:], L, bc(rmax, RE), ALU.is_ge))
            dve.sem_inc(s_gf[0], 1)
            step(dve.tensor_tensor(cand[:], cand[:], rank_order[:].unsqueeze(1).to_broadcast([P, NT, RE]), ALU.mult))
            step(dve.tensor_reduce(cmax[:], cand[:], AX_X, ALU.max))
            step(dve.tensor_tensor(onehot[:], cand[:], bc(cmax, RE), ALU.is_equal))
            dve.wait_ge(s_re, 1)
            step(dve.tensor_reduce(rsum[:], rexp[:], AX_X, ALU.add))
            step(dve.reciprocal(val[:], rsum[:]))
            step(dve.tensor_copy(vparts_b[:, 0, :], val[:]))
            step(dve.tensor_tensor(r1[:], val[:], vparts_b[:, 0, :], ALU.subtract))
            step(dve.tensor_copy(vparts_b[:, 1, :], r1[:]))
            dve.tensor_tensor(vparts[:, 2, :], r1[:], vparts_b[:, 1, :], ALU.subtract)
            step(dve.tensor_copy(vparts[:, 0:2, :], vparts_b[:]))
            for k in range(3):
                dve.tensor_copy(OH3[:, :, k, :], onehot[:])
                ins = dve.tensor_tensor(MV3[:, :, k, :], onehot[:], vparts[:, k, :].unsqueeze(2).to_broadcast([P, NT, RE]),
                                        ALU.mult)
            ins.then_inc(s_oh, 1)
            dve.wait_ge(s_x2, NC)
            layernorm(dve, step, s_ln, s_sqrt, s_tok, stats, mv, vare, std, rstd, newt)
            for i in range(NT):
                dve.tensor_scalar(h_tok[:, i, :], s_tok[:, i, :], mv[:, i, 0:1], rstd[:, i:i + 1], ALU.subtract,
                                  ALU.mult).then_inc(s_hn, 1)
            k = ("GL", 0)
            L2 = bank(k)[:, 0:NT * ME].rearrange("p (n e) -> p n e", n=NT)
            dve.wait_ge(s_g, number[k] + 1)
            step(dve.tensor_reduce(gmax[:], L2, AX_X, ALU.max))
            dve.tensor_tensor(gdiff[:], L2, bc(gmax, ME), ALU.subtract).then_inc(s_gd, 1)
            dve.wait_ge(s_gd, 1)
            dve.sem_inc(s_gf[number[k] % 2], 1)
            dve.wait_ge(s_ge, 1)
            step(dve.tensor_reduce(gsum[:], gexp[:], AX_X, ALU.add))
            step(dve.reciprocal(gsum[:], gsum[:]))
            dve.tensor_tensor(gw[:], gexp[:], bc(gsum, ME), ALU.mult).then_inc(s_gw, 1)

            unit = [0]

            def count_rows():
                u = unit[0]
                if u >= len(UNITS):
                    return
                i, cc = UNITS[u]
                r = R[u % 2]
                v = val[:, i:i + 1]
                dve.wait_ge(s_r, u + 1)
                own = i // TPC
                if cc != own:
                    dve.wait_ge(s_rc, u) if u else None
                    ins = dve.tensor_scalar(seen[:], r[:], v, None, ALU.is_ge if cc < own else ALU.is_gt, ALU.add,
                                            counts[:, i, cc:cc + 1])
                else:
                    q = (i % TPC) * P
                    dve.wait_ge(s_rc, u) if u else None
                    if q:
                        step(dve.tensor_scalar(seen[:, 0:q], r[:, 0:q], v, None, ALU.is_ge, ALU.add, counts[:, i, cc:cc + 1]))
                    step(dve.tensor_scalar(seen[:, q:], r[:, q:], v, None, ALU.is_gt, ALU.add, counts[:, i, NC:NC + 1]))
                    ins = dve.scalar_tensor_tensor(seen[:, q:q + P], r[:, q:q + P], v, below[:], ALU.is_equal, ALU.mult,
                                                   counts[:, i, NC + 1:NC + 2])
                ins.then_inc(s_rc, 1)
                unit[0] += 1
                if unit[0] == len(UNITS):
                    slots()

            def slots():
                dve.wait_ge(s_rc, len(UNITS))
                step(dve.tensor_reduce(rank[:], counts[:], AX_X, ALU.add))
                step(dve.tensor_scalar(over[:], rank[:], float(CAP) - 0.5, float(2 * SLOT_ROWS), ALU.is_ge, ALU.mult))
                step(dve.tensor_scalar(slotf[:], cmax[:], -float(CAP), float(CAP * RE), ALU.mult, ALU.add))
                step(dve.tensor_tensor(slotf[:], slotf[:], rank[:], ALU.add))
                step(dve.tensor_tensor(slotf[:], slotf[:], over[:], ALU.add))
                dve.tensor_copy(slot[:], slotf[:]).then_inc(s_slot, 1)

            def route_counts(k):
                for _ in range(k):
                    count_rows()

            def add(n):
                c, e = GROUPS[n]
                dve.wait_ge(s_e, n + 1)
                dve.wait_ge(s_b2, c + 1)
                if e > 0:
                    dve.wait_ge(s_acc, n)
                for i in range(TPC):
                    t = TPC * c + i
                    ins = dve.scalar_tensor_tensor(s_tok[:, t, :], E[n % 2][:, i * P:(i + 1) * P], gw[:, t, e:e + 1],
                                                   s_tok[:, t, :], ALU.mult, ALU.add)
                ins.then_inc(s_acc, 1)

            route_counts(PER_HB * HB)
            for c in range(NC):
                k = ("B2", c)
                dve.wait_ge(s_g, number[k] + 1)
                dve.tensor_tensor(s_tok[:, tiles(c), :], t4(bank(k)[:]), s_tok[:, tiles(c), :], ALU.add).then_inc(s_b2, 1)
                dve.wait_ge(s_b2, c + 1)
                dve.sem_inc(s_gf[number[k] % 2], 1)
            for n in range(len(GROUPS)):
                if n + 1 < len(GROUPS):
                    route_counts(PER_HB * HB)
                add(n)


def routed0(nc, dram, keep, t0):
    ident = keep["ident"]
    x_tok, s_tok, slot, y_tok, xe = t0["x_tok"], t0["s_tok"], t0["slot"], t0["y_tok"], t0["xe"]
    W1, W2, be1, be2, x1_tok = t0["W1"], t0["W2"], t0["be1"], t0["be2"], t0["x_tok"]
    with ExitStack() as ctx:
        def sb(name, shape, dt=F32):
            return ctx.enter_context(nc.sbuf_tensor(name, shape, dt))

        def sem(name):
            return ctx.enter_context(nc.semaphore(name))

        xeT, yeT, ye = sb("xeT", [P, SLOT_ROWS]), sb("yeT", [P, SLOT_ROWS]), sb("ye", [P, XT_, D])
        hE = sb("hE", [P, 3, RH2, CAP])
        g = sb("g0", [P, NT, D])
        G = [ctx.enter_context(nc.psum_tensor(f"CG{i}", [P, CW], F32)) for i in range(2)]
        H = [ctx.enter_context(nc.psum_tensor(f"CH{i}", [P, CW], F32)) for i in range(3)]
        Y = [ctx.enter_context(nc.psum_tensor(f"CY{i}", [P, CW], F32)) for i in range(2)]
        s_t, s_xT, s_h, s_hid = sem("xe_turned"), sem("xeT_out"), sem("hidden_sums0c"), sem("hidden0c")
        s_y, s_yT, s_ye, s_st = sem("y_sums"), sem("yT_out"), sem("ye_out"), sem("ye_stored")
        s_ga, s_g, s_m, s_end = sem("gathered"), sem("silu0c"), sem("s_times_g"), sem("x1_done")
        s_keep = sem("x1_stored")
        XC = XT_ // TPC
        block = ctx.enter_context(nc.Block())

        @block.tensor
        def _(pe):
            for c in range(XC):
                if c >= 2:
                    pe.wait_ge(s_xT, c - 1)
                for i in range(TPC):
                    ins = pe.transpose(G[c % 2][:, i * P:(i + 1) * P], xe[:, TPC * c + i, :], ident[:])
                ins.then_inc(s_t, 1)

            def first(e):
                pe.wait_ge(s_xT, -(-(e + 1) * CAP // CW))
                if e >= 3:
                    pe.wait_ge(s_hid, 2 * (e - 2))
                for b in range(RH2):
                    ins = pe.matmul(H[e % 3][:, b * CAP:(b + 1) * CAP], W1[:, e, b * P:(b + 1) * P],
                                    xeT[:, e * CAP:(e + 1) * CAP], start=True, stop=True)
                ins.then_inc(s_h, 1)

            def second(e):
                pe.wait_ge(s_hid, 2 * e + 2)
                if e >= 2:
                    pe.wait_ge(s_yT, e - 1)
                for b in range(RH2):
                    ins = pe.matmul(Y[e % 2][:, 0:CAP], W2[:, e, b, :], hE[:, e % 3, b, :], start=b == 0, stop=b == RH2 - 1)
                ins.then_inc(s_y, 1)

            turned = 0
            for e in range(RE + 2):
                if e < RE:
                    first(e)
                if e >= 2:
                    second(e - 2)
                while turned < XC and (e - 3) * CAP >= (turned + 1) * CW or (e == RE + 1 and turned < XC):
                    pe.wait_ge(s_yT, -(-(turned + 1) * CW // CAP))
                    if turned >= 2:
                        pe.wait_ge(s_ye, turned - 1)
                    else:
                        pe.wait_ge(s_xT, XC)
                    for i in range(TPC):
                        t = TPC * turned + i
                        ins = pe.transpose(G[turned % 2][:, i * P:(i + 1) * P], yeT[:, t * P:(t + 1) * P], ident[:])
                    ins.then_inc(s_t, 1)
                    turned += 1

        @block.scalar
        def _(act):
            for c in range(XC):
                act.wait_ge(s_t, c + 1)
                act.activation(xeT[:, c * CW:(c + 1) * CW], G[c % 2][:], ACT.Copy).then_inc(s_xT, 1)
            for e in range(RE):
                act.wait_ge(s_h, e + 1)
                if e >= 3:
                    act.wait_ge(s_y, e - 2)
                for b in range(RH2):
                    act.activation(hE[:, e % 3, b, :], H[e % 3][:, b * CAP:(b + 1) * CAP], ACT.Gelu_apprx_tanh,
                                   bias=be1[:, e, b:b + 1]).then_inc(s_hid, 1)
            act.wait_ge(s_ga, 16 * NT)
            for c in range(NC):
                act.activation(g[:, TPC * c:TPC * (c + 1), :], y_tok[:, TPC * c:TPC * (c + 1), :], ACT.Silu).then_inc(s_g, 1)

        @block.vector
        def _(dve):
            done = 0
            for e in range(RE):
                dve.wait_ge(s_y, e + 1)
                dve.tensor_scalar(yeT[:, e * CAP:(e + 1) * CAP], Y[e % 2][:, 0:CAP], be2[:, e:e + 1], None,
                                  ALU.add).then_inc(s_yT, 1)
                while done < XC and ((e - 3) * CAP >= (done + 1) * CW or e == RE - 1):
                    dve.wait_ge(s_t, XC + done + 1)
                    dve.tensor_copy(ye[:, TPC * done:TPC * (done + 1), :],
                                    G[done % 2][:].rearrange("p (n d) -> p n d", d=D)).then_inc(s_ye, 1)
                    done += 1
            for c in range(NC):
                a = slice(TPC * c, TPC * (c + 1))
                dve.wait_ge(s_g, c + 1)
                dve.tensor_tensor(g[:, a, :], s_tok[:, a, :], g[:, a, :], ALU.mult).then_inc(s_m, 1)
                dve.wait_ge(s_m, c + 1)
                dve.tensor_tensor(x1_tok[:, a, :], x_tok[:, a, :], g[:, a, :], ALU.add).then_inc(s_end, 1)

        @block.sync
        def _(sp):
            rows = dram["ye_rows"].rearrange("(n p) d -> p n d", p=P)
            for c in range(XC):
                a = slice(TPC * c, TPC * (c + 1))
                sp.wait_ge(s_ye, c + 1)
                sp.dma_start(rows[:, a, :], ye[:, a, :]).then_inc(s_st, 16)
            for c in range(NC):
                a = slice(TPC * c, TPC * (c + 1))
                sp.wait_ge(s_end, c + 1)
                sp.dma_start(dram["x1_kept"][:, c * CW:(c + 1) * CW], x1_tok[:, a, :].rearrange("p n d -> p (n d)")).then_inc(s_keep, 16)
            sp.wait_ge(s_keep, 16 * NC)

        @block.gpsimd
        def _(pool):
            pool.wait_ge(s_st, 16 * XC)
            for i in range(NT):
                pool.indirect_dma_start(y_tok[:, i, :], None, dram["ye_rows"], bass.IndirectOffsetOnAxis(slot[:, i:i + 1], 0),
                                        bounds_check=SLOT_ROWS - 1, oob_is_err=False).then_inc(s_ga, 16)
            pool.wait_ge(s_ga, 16 * NT)


def layer0(nc, dram, keep):
    with ExitStack() as ctx:
        t0 = {}

        def sb(name, shape, dt=F32):
            t0[name] = ctx.enter_context(nc.sbuf_tensor(name, shape, dt))

        for name, shape, dt in (("x_tok", [P, NT, D], F32), ("xn_tok", [P, NT, D], F32), ("s_tok", [P, NT, D], F32),
                                ("slot", [P, NT], I32), ("be1", [P, RE, RH2], F32), ("be2", [P, RE], F32),
                                ("x2T", [P, T], F32), ("xnT", [P, T + 2], F32)):
            sb(name, shape, dt)
        mixer0(nc, dram, keep, t0)
        for name, shape in (("y_tok", [P, NT, D]), ("xe", [P, XT_, D]), ("W1", [P, RE, RH2 * P]), ("W2", [P, RE, RH2, D])):
            sb(name, shape)
        experts0(nc, dram, keep, t0)
        routed0(nc, dram, keep, t0)


def setup1(nc, dram, keep):
    ident, ones, xT = keep["ident"], keep["ones"], keep["xT"]
    wq, wk, wv, wo, wpos, bpos, bq = (keep[n] for n in ("wq", "wk", "wv", "wo", "wpos", "bpos", "bq"))
    with ExitStack() as ctx:
        def sb(name, shape, dt=F32):
            return ctx.enter_context(nc.sbuf_tensor(name, shape, dt))

        def sem(name):
            return ctx.enter_context(nc.semaphore(name))

        x1_tok = sb("x1_tok", [P, NT, D])
        stats = sb("stats1", [P, NT, 6])
        mv = sb("mv1", [P, NT, 2])
        vare = sb("vare1", [P, NT])
        std = sb("std1", [P, NT])
        rstd = sb("rstd1", [P, NT])
        newt = sb("newt1", [P, NT])
        xn = sb("xn1", [P, NT, D])
        diff = sb("diff1", [P, T])
        xr = sb("xr1", [P, T])
        xk = sb("xk1", [P, T])
        krelu = sb("krelu1", [P, T])
        kact = sb("kact1", [P, T])
        rsig = sb("rsig1", [P, NT, D])
        gate = sb("gate1", [P, NT, D])
        ffw = sb("ffw1", [P, 3, D])
        mu = sb("mu1", [P, 2])
        wqT = sb("wqT1", [P, PAIRS, P])
        pblk = sb("pblk1", [P, PAIRS, P])
        sq = sb("sq1", [P, HEADS * HS])
        norm = sb("norm1", [P, HEADS * HS])
        rnorm = sb("rnorm1", [P, HEADS * HS])
        ncol = sb("ncol1", [P, PAIRS])
        B = [ctx.enter_context(nc.psum_tensor(f"SB{i}", [P, CW], F32)) for i in range(8)]

        s_x = sem("x1_loaded")
        s_w = sem("w1_loaded")
        s_v = sem("dve_step1")
        s_ln = sem("ln_var1")
        s_sqrt = sem("ln_sqrt1")
        s_xn = sem("xn_tiles1")
        s_turn = sem("xn_turned1")
        s_xT = sem("xT_chunks1")
        s_sq = sem("squares1")
        s_nsum = sem("norm_sums1")
        s_nrt = sem("norm_roots1")
        s_rn = sem("norm_recips1")
        s_ncol = sem("norm_cols1")
        s_wp = sem("wpos_sums1")
        s_wpc = sem("wpos_copied1")
        s_mix = sem("mixed1")
        s_k = sem("k_sums1")
        s_relu = sem("k_relu1")
        s_kact = sem("k_act1")
        s_r = sem("r_sums1")
        s_sig = sem("r_sigmoid1")
        s_kv = sem("kv_sums1")
        s_rkv = sem("rkv1")
        s_gate = sem("gate_done1")
        s_st = sem("stored1")
        NLOAD = 16 * 10
        block = ctx.enter_context(nc.Block())

        @block.sync
        def _(sp):
            sp.dma_start(x1_tok[:].rearrange("p n d -> p (n d)"), dram["x1_kept"]).then_inc(s_x, 16)
            for dst, src in ((wq[:], dram["wq"]), (wk[:], dram["wk"]), (wv[:], dram["wv"]), (bq[:], dram["bq"]),
                             (wo[:, 1:, :], dram["wo"]), (wqT[:], dram["wqT"]), (pblk[:], dram["pblk"]),
                             (ffw[:], dram["ffw"]), (mu[:], dram["mu"]), (keep["angle"][:], dram["angle"])):
                sp.dma_start(dst, src).then_inc(s_w, 16)
            sp.wait_ge(s_gate, NC)
            sp.dma_start(dram["gate_kept"], gate[:].rearrange("p n d -> p (n d)")).then_inc(s_st, 16)
            sp.wait_ge(s_st, 16)

        def square(dve, c):
            dve.wait_ge(s_relu, c + 1)
            dve.scalar_tensor_tensor(kact[:, c * CW:(c + 1) * CW], B[2 + c % 2][:], 0.0,
                                     krelu[:, c * CW:(c + 1) * CW], ALU.max, ALU.mult).then_inc(s_kact, 1)

        @block.vector
        def _(dve):
            steps = [0]

            def step(ins):
                steps[0] += 1
                ins.then_inc(s_v, 1)
                dve.wait_ge(s_v, steps[0])

            dve.memset(xT[:, 0:1], 0.0)
            dve.memset(wo[:, 0, :], 0.0)
            dve.wait_ge(s_x, 16)
            for i in range(NT):
                ins = dve.bn_stats(stats[:, i, :], x1_tok[:, i, :])
            step(ins)
            for i in range(NT):
                ins = dve.bn_aggr(mv[:, i, :], stats[:, i, :])
            step(ins)
            dve.tensor_scalar(vare[:], mv[:, :, 1], EPS, None, ALU.add).then_inc(s_ln, 1)
            dve.wait_ge(s_sqrt, 1)
            step(dve.reciprocal(rstd[:], std[:]))
            step(dve.tensor_tensor(newt[:], rstd[:], rstd[:], ALU.mult))
            step(dve.tensor_tensor(newt[:], newt[:], vare[:], ALU.mult))
            step(dve.tensor_scalar(newt[:], newt[:], -0.5, 1.5, ALU.mult, ALU.add))
            step(dve.tensor_tensor(rstd[:], rstd[:], newt[:], ALU.mult))
            for i in range(NT):
                dve.tensor_scalar(xn[:, i, :], x1_tok[:, i, :], mv[:, i, 0:1], rstd[:, i:i + 1], ALU.subtract,
                                  ALU.mult).then_inc(s_xn, 1)
            dve.wait_ge(s_w, NLOAD)
            dve.tensor_tensor(sq[:], wv[:], wv[:], ALU.mult).then_inc(s_sq, 1)
            dve.tensor_scalar(wq[:], wq[:], C_QKV, None, ALU.mult)
            dve.tensor_scalar(wk[:], wk[:], C_QKV * HS ** -0.5, None, ALU.mult)
            for c in range(NC):
                a, b = c * CW, (c + 1) * CW
                dve.wait_ge(s_xT, c + 1)
                step(dve.tensor_tensor(diff[:, a:b], xT[:, a + 1:b + 1], xT[:, a:b], ALU.subtract))
                dve.scalar_tensor_tensor(xk[:, a:b], diff[:, a:b], mu[:, 1:2], xT[:, a:b], ALU.mult,
                                         ALU.add).then_inc(s_mix, 1)
                dve.scalar_tensor_tensor(xr[:, a:b], diff[:, a:b], mu[:, 0:1], xT[:, a:b], ALU.mult,
                                         ALU.add).then_inc(s_mix, 1)
                if c > 0:
                    square(dve, c - 1)
            square(dve, NC - 1)
            dve.wait_ge(s_nrt, 2)
            step(dve.tensor_scalar(norm[:], norm[:], 1e-18, None, ALU.max))
            step(dve.reciprocal(rnorm[:], norm[:]))
            dve.tensor_tensor(wv[:], wv[:], rnorm[:], ALU.mult).then_inc(s_rn, 1)
            for c in range(NC):
                dve.wait_ge(s_sig, c + 1)
                dve.wait_ge(s_kv, c + 1)
                dve.tensor_tensor(gate[:, TPC * c:TPC * (c + 1), :], B[6 + c % 2][:].rearrange("p (n d) -> p n d", d=D),
                                  rsig[:, TPC * c:TPC * (c + 1), :], ALU.mult).then_inc(s_rkv, 1)
            dve.wait_ge(s_ncol, 1)
            step(dve.reciprocal(ncol[:], B[0][:, 0:PAIRS]))
            for j in range(PAIRS):
                ins = dve.tensor_scalar(wo[:, j + 1, :], wo[:, j + 1, :], ncol[:, j:j + 1], C_OUT * C_QKV, ALU.mult,
                                        ALU.mult)
            step(ins)

        @block.scalar
        def _(act):
            act.wait_ge(s_ln, 1)
            act.activation(std[:], vare[:], ACT.Sqrt).then_inc(s_sqrt, 1)
            for k in range(2):
                act.wait_ge(s_nsum, k + 1)
                act.activation(norm[:, k * CW:(k + 1) * CW], B[4 + k][:], ACT.Sqrt).then_inc(s_nrt, 1)
            for c in range(NC):
                act.wait_ge(s_turn, c + 1)
                act.activation(xT[:, 1 + c * CW:1 + (c + 1) * CW], B[c % 2][:], ACT.Copy).then_inc(s_xT, 1)
            for c in range(NC):
                act.wait_ge(s_k, c + 1)
                act.activation(krelu[:, c * CW:(c + 1) * CW], B[2 + c % 2][:], ACT.Relu).then_inc(s_relu, 1)
                act.wait_ge(s_r, c + 1)
                act.activation(rsig[:, TPC * c:TPC * (c + 1), :], B[4 + c % 2][:].rearrange("p (n d) -> p n d", d=D),
                               ACT.Sigmoid).then_inc(s_sig, 1)
            for k in range(2):
                act.wait_ge(s_wp, k + 1)
                act.activation(wpos[:, k * CW:(k + 1) * CW], B[k][:], ACT.Copy, scale=C_QKV).then_inc(s_wpc, 1)
            act.wait_ge(s_wp, 3)
            act.activation(bpos[:], B[2][:, 0:PAIRS], ACT.Copy).then_inc(s_wpc, 1)
            for c in range(NC):
                act.wait_ge(s_rkv, c + 1)
                g = gate[:, TPC * c:TPC * (c + 1), :]
                act.activation(g, g, ACT.Silu).then_inc(s_gate, 1)

        @block.tensor
        def _(pe):
            pe.wait_ge(s_sq, 1)
            for k in range(2):
                pe.matmul(B[4 + k][:], ones[:], sq[:, k * CW:(k + 1) * CW], start=True, stop=True).then_inc(s_nsum, 1)
            for c in range(NC):
                if c >= 2:
                    pe.wait_ge(s_xT, c - 1)
                for i in range(TPC):
                    pe.wait_ge(s_xn, TPC * c + i + 1)
                    ins = pe.transpose(B[c % 2][:, i * P:(i + 1) * P], xn[:, TPC * c + i, :], ident[:])
                ins.then_inc(s_turn, 1)
            pe.wait_ge(s_nrt, 2)
            for c in range(NC):
                pe.wait_ge(s_mix, 2 * c + 2)
                if c >= 2:
                    pe.wait_ge(s_kact, c - 1)
                pe.matmul(B[2 + c % 2][:], ffw[:, 1, :], xk[:, c * CW:(c + 1) * CW], start=True, stop=True).then_inc(s_k, 1)
                if c >= 2:
                    pe.wait_ge(s_sig, c - 1)
                for i in range(TPC):
                    t = c * CW + i * P
                    ins = pe.matmul(B[4 + c % 2][:, i * P:(i + 1) * P], xr[:, t:t + P], ffw[:, 0, :], start=True, stop=True)
                ins.then_inc(s_r, 1)
            pe.wait_ge(s_xT, NC)
            for k in range(2):
                for i in range(TPC):
                    j = TPC * k + i
                    ins = pe.matmul(B[k][:, i * P:(i + 1) * P], wqT[:, j, :], pblk[:, j, :], start=True, stop=True)
                ins.then_inc(s_wp, 1)
            pe.wait_ge(s_kact, NC)
            for j in range(PAIRS):
                ins = pe.matmul(B[2][:, j:j + 1], pblk[:, j, :], bq[:, j:j + 1], start=True, stop=True)
            ins.then_inc(s_wp, 1)
            for c in range(NC):
                if c >= 2:
                    pe.wait_ge(s_rkv, c - 1)
                for i in range(TPC):
                    t = c * CW + i * P
                    ins = pe.matmul(B[6 + c % 2][:, i * P:(i + 1) * P], kact[:, t:t + P], ffw[:, 2, :], start=True, stop=True)
                ins.then_inc(s_kv, 1)
            pe.wait_ge(s_rn, 1)
            pe.wait_ge(s_wpc, 1)
            for j in range(PAIRS):
                ins = pe.matmul(B[0][:, j:j + 1], rnorm[0:1, j * P:(j + 1) * P], ones[0:1, 0:1], start=True, stop=True)
            ins.then_inc(s_ncol, 1)


def attention1(nc, dram, keep, out_dram):
    ident, identh, ones, xT, fold, angle = (keep[n] for n in ("ident", "identh", "ones", "xT", "fold", "angle"))
    mask_rows, mask_cols = keep["mask_rows"], keep["mask_cols"]
    wq, wk, wv, wo, wpos, bpos, bq = (keep[n] for n in ("wq", "wk", "wv", "wo", "wpos", "bpos", "bq"))
    RH = HS + FREQS
    KR = RH + 1
    QHI, QLO, KHI, KLO = range(4)
    with ExitStack() as ctx:
        def sb(name, shape, dt=F32):
            return ctx.enter_context(nc.sbuf_tensor(name, shape, dt))

        def sem(name):
            return ctx.enter_context(nc.semaphore(name))

        heads = [[sb(f"{n}{h}", [P, T], F32R) for n in ("QH", "QL", "KH", "KL")] for h in (0, 1)]
        vh = [sb(f"V{h}", [P, NT, VW], F16) for h in (0, 1)]
        stage = [sb(f"stage{n}", [P, T], F32R) for n in ("QH", "QL", "KH", "KL")]
        stage_pos = sb("stage_pos", [P, T], F32R)
        stage_v = sb("stage_v", [P, NT, 2, VW], F16)
        pair_wq = sb("pair_wq", [P, P])
        pair_wk = sb("pair_wk", [P, P])
        pair_wpos = sb("pair_wpos", [P, P])
        pair_b = sb("pair_b", [P, 2])
        turned = sb("turned", [P, CW])
        acc = sb("acc", [P, NT, D])
        negm = sb("negm", [P, 2, NT])
        part = sb("part", [P, 2, TPC])
        mrow = sb("mrow", [TPC, NC, P], F32R)
        prob = sb("prob", [P, 3, CW])
        plow = sb("plow", [P, 3, CW], F16)
        osb = sb("osb", [P, 2, TPC, VW])
        rsum = sb("rsum", [P, 2, TPC])
        oadd = sb("oadd", [P, TPC, HS])
        otok = sb("otok", [P, NT, P])
        oT = sb("oT", [P, CW])

        S = [ctx.enter_context(nc.psum_tensor(f"S{i}", [P, CW], F32)) for i in range(2)]
        A = [ctx.enter_context(nc.psum_tensor(f"A{i}", [P, CW], F32)) for i in range(2)]
        O = ctx.enter_context(nc.psum_tensor("O", [P, 2, CW], F32))
        M = [ctx.enter_context(nc.psum_tensor(f"M{i}", [P, CW], F32)) for i in range(2)]

        s_const = sem("const_loaded")
        s_init = sem("buffers_set")
        s_item = sem("item_sums")
        s_free = [sem(f"item_out{i}") for i in range(2)]
        s_high = sem("item_high")
        s_st = sem("scores")
        s_exp = sem("exps")
        s_low = sem("lows")
        s_pv = sem("values_added")
        s_a = sem("row_scores")
        s_max = sem("row_maxima")
        s_neg = sem("joined_maxima")
        s_pair = sem("pair_weights")
        s_oev = sem("outputs_copied")
        s_rec = sem("sums_inverted")
        s_oad = sem("outputs_joined")
        s_otok = sem("outputs_scaled")
        s_mrow = [sem(f"max_moved{c}") for c in range(NC)]
        s_move = [sem(f"rows_moved{c}") for c in range(NC)]
        s_mv = [sem(f"values_moved{h}") for h in (0, 1)]
        s_back = sem("reloaded")
        s_fin = sem("finished")
        s_out = sem("stored")
        MOVES = 6 * 16

        bank = Bank()
        pro_items = [(kind, 0, c, bank.take()) for c in range(NC) for kind in ("q", "k", "pos", "v", "possum")]
        pro_max = [("maxima", 0, c, bank.take()) for c in range(NC - 1)]
        base_n, base_bank = bank.n, list(bank.of_bank)
        plan = {}
        for last in (False, True):
            items, k = plan_items(last), 0
            plan[last] = {}
            for n in range(SLOTS):
                plan[last][n] = []
                for (kind, rel, c) in items[n]:
                    plan[last][n].append((kind, rel, c, (base_n + k, (k + base_n) % 2, base_bank[(k + base_n) % 2] + k // 2)))
                    k += 1
            if not last:
                PER = k
                assert PER % 2 == 0
            else:
                TAIL = k
        bank.n, bank.of_bank = 0, [0, 0]
        for _ in range(base_n + 7 * PER + TAIL):
            bank.take()
        fin_items = [("turn", 0, 3, bank.take()), ("project", 0, 3, bank.take())]

        PRO_A = NB - LEAD
        PER_A = len(A_SLOTS)
        HIGHS = 4 * NC

        def count(tok, p):
            n, b, before = tok
            return n + 1 + PER * p, b, before + (PER // 2) * p

        def column(t, p):
            return t[:, p:p + 1] if isinstance(p, int) else t[:, bass.ds(p, 1)]

        block = ctx.enter_context(nc.Block())

        @block.sync
        def _(sp):
            sp.dma_start(otok[HS:RH, :, :].rearrange("p n d -> p (n d)"), dram["ktab"]).then_inc(s_const, 16)
            sp.dma_start(acc[:], dram["out_bias"]).then_inc(s_const, 16)

            def move_head(h):
                for c in range(NC):
                    a, b = c * CW, (c + 1) * CW
                    for k in range(4):
                        sp.dma_start(raw(heads[h][k][0:HS, a:b]), raw(stage[k][HS * h:HS * (h + 1), a:b])).then_inc(s_move[c], 16)
                    for k in (QHI, QLO):
                        r = k * 2 * FREQS + FREQS * h
                        sp.dma_start(raw(heads[h][k][HS:RH, a:b]), raw(stage_pos[r:r + FREQS, a:b])).then_inc(s_move[c], 16)
                sp.dma_start(vh[h][:], stage_v[:, :, h, :]).then_inc(s_mv[h], 16)

            def move_max(h, c, tok, p):
                _, b, before = count(tok, p)
                sp.wait_ge(s_free[b], before + 1)
                sp.dma_start(raw(heads[h][QHI][RH:KR, c * CW:(c + 1) * CW]), raw(mrow[:, c, :])).then_inc(s_mrow[c], 16)

            def staged(last_tok, before_tok, p):
                for tok in (last_tok, before_tok):
                    _, b, before = count(tok, p)
                    sp.wait_ge(s_free[b], before + 1)

            sp.wait_ge(s_init, 1)
            staged(pro_items[-1][3], pro_items[-2][3], 0)
            move_head(0)
            move_head(1)
            for (_, _, c, tok) in pro_max:
                move_max(0, c, tok, 0)

            def pair(p, last):
                items = plan[last]
                preps = [x[3] for n in range(SLOTS) for x in items[n] if x[0] in ("q", "k", "pos", "v", "possum")]
                for n in range(SLOTS):
                    for (kind, rel, c, tok) in items[n]:
                        if kind == "maxima":
                            move_max(rel % 2, c, tok, p)
                    if n == NB - 1 and not last:
                        staged(preps[-1], preps[-2], p)
                        sp.wait_ge(s_st, SLOTS * p + NB)
                        sp.wait_ge(s_pv, SLOTS * p + NB)
                        move_head(0)
                if not last:
                    sp.wait_ge(s_st, SLOTS * (p + 1))
                    sp.wait_ge(s_pv, SLOTS * (p + 1))
                    move_head(1)

            with sp.Fori(0, PAIRS - 1) as p:
                pair(p, False)
            pair(PAIRS - 1, True)
            _, b, before = fin_items[0][3]
            sp.wait_ge(s_free[b], before + 1)
            sp.dma_start(angle[:], dram["x1_kept"]).then_inc(s_back, 16)
            sp.dma_start(xT[:, 0:T], dram["gate_kept"]).then_inc(s_back, 16)
            for c in range(NC):
                sp.wait_ge(s_fin, 2 * c + 2)
                sp.dma_start(out_dram.rearrange("b (n p) d -> p (b n) d", p=P)[:, TPC * c:TPC * (c + 1), :],
                             acc[:, TPC * c:TPC * (c + 1), :]).then_inc(s_out, 16)
            sp.wait_ge(s_out, 16 * NC)

        @block.gpsimd
        def _(pool):
            def weights(p, p_next, first):
                if not first:
                    pool.wait_ge(s_item, base_n + PER * p)
                at = slice(p_next * P, (p_next + 1) * P) if isinstance(p_next, int) else bass.ds(p_next * P, P)
                pool.tensor_copy(pair_wq[:], wq[:, at])
                pool.tensor_copy(pair_wk[:], wk[:, at])
                pool.tensor_copy(pair_b[:, 0:1], column(bq, p_next))
                pool.tensor_copy(pair_b[:, 1:2], column(bpos, p_next))
                pool.tensor_copy(pair_wpos[:], wpos[:, at]).then_inc(s_pair, 1)

            def scale(k, h, c, g):
                pool.wait_ge(s_oev, g + 2)
                pool.wait_ge(s_otok, g + 1)
                pool.tensor_tensor(oadd[:], osb[:, k, :, 0:HS], osb[:, k, :, HS + 1:VW], ALU.add).then_inc(s_oad, 1)
                pool.wait_ge(s_oad, g + 1)
                pool.wait_ge(s_rec, g + 1)
                pool.tensor_tensor(otok[:, TPC * c:TPC * (c + 1), HS * h:HS * (h + 1)], oadd[:],
                                   rsum[:, k, :].unsqueeze(2).to_broadcast([P, TPC, HS]),
                                   ALU.mult).then_inc(s_otok, 1)

            for h in (0, 1):
                ins = pool.memset(stage_v[:, :, h, HS:HS + 1], 1.0)
            ins.then_inc(s_init, 1)
            weights(0, 0, True)

            def pair(p, last):
                if not last:
                    weights(p, p + 1, False)
                for h in (0, 1):
                    for c in range(NC):
                        if h == 0 and c == 0:
                            first_turn = plan[last][4][0][3]
                            pool.wait_ge(s_item, count(first_turn, p)[0])
                        scale(c % 2, h, c, 2 * NC * p + NC * h + c)

            with pool.Fori(0, PAIRS - 1) as p:
                pair(p, False)
            pair(PAIRS - 1, True)

        def pos_item(items, c):
            return next(x[3] for n in range(SLOTS) for x in items[n] if x[0] == "pos" and x[2] == c)

        def turn_item(items, rel, c):
            return next(x[3] for n in range(SLOTS) for x in items[n] if x[:3] == ("turn", rel, c))

        @block.tensor
        def _(pe):
            def item(kind, rel, c, tok, p, pos_tok=None, turn_tok=None):
                _, b, before = count(tok, max(p, 0) if isinstance(p, int) else p)
                if not isinstance(before, int) or before > 0:
                    pe.wait_ge(s_free[b], before)
                out = M[b]
                a0, a1 = c * CW, (c + 1) * CW
                if kind in ("q", "k", "pos"):
                    if kind == "q" and c == 0:
                        pe.wait_ge(s_pair, p + 2)
                    w = {"q": pair_wq, "k": pair_wk, "pos": pair_wpos}[kind]
                    ins = pe.matmul(out[:], w[:], xT[:, 1 + a0:1 + a1], start=True, stop=True)
                elif kind == "possum":
                    _, b2, before2 = count(pos_tok, max(p, 0) if isinstance(p, int) else p)
                    pe.wait_ge(s_free[b2], before2 + 1)
                    ins = pe.matmul(out[0:2 * FREQS, :], fold[:], turned[:], start=True, stop=True)
                elif kind == "v":
                    w = wv[:, (p + 1) * P:(p + 2) * P] if isinstance(p, int) else wv[:, bass.ds((p + 1) * P, P)]
                    for i in range(TPC):
                        ins = pe.matmul(out[:, i * P:(i + 1) * P], xT[:, 1 + a0 + i * P:1 + a0 + (i + 1) * P], w,
                                        start=True, stop=True)
                elif kind == "maxima":
                    head = 2 * p + rel
                    if c == 0:
                        pe.wait_ge(s_max, a_end(0) if ahead(p) else PRO_A + PER_A * p + {1: LEAD, 2: LEAD + NB}[rel] + a_end(0))
                    else:
                        pe.wait_ge(s_neg, (NT - TPC) * (0 if ahead(p) else head) + TPC * c)
                    ins = pe.transpose(out[0:TPC, 0:P], negm[:, rel % 2, TPC * c:TPC * (c + 1)], ident[:])
                elif kind == "turn":
                    pe.wait_ge(s_otok, 2 * NC * p + (NC + c + 2 if rel == 0 else 1))
                    for i in range(TPC):
                        ins = pe.transpose(out[:, i * P:(i + 1) * P], otok[:, TPC * c + i, :], ident[:])
                elif kind == "project":
                    _, b2, before2 = count(turn_tok, p)
                    pe.wait_ge(s_free[b2], before2 + 1)
                    w = wo[:, p + 1 + rel, :] if isinstance(p, int) else wo[:, bass.ds(p + (1 + rel), 1), :]
                    for i in range(TPC):
                        ins = pe.matmul(out[:, i * P:(i + 1) * P], oT[:, i * P:(i + 1) * P], w, start=True, stop=True)
                ins.then_inc(s_item, 1)

            def row_scores(h, a, g):
                i, cc = A_TILES[a]
                out = A[g % 2]
                diagonal = cc == i // TPC
                w = (i % TPC + 1) * P if diagonal else CW
                if diagonal:
                    pe.matmul(out[:, w - P:w], identh[:], mask_rows[:], start=True, stop=False, skip_group_check=True)
                pe.matmul(out[:, 0:w], heads[h][QHI][0:RH, i * P:(i + 1) * P], heads[h][KHI][0:RH, cc * CW:cc * CW + w],
                          start=not diagonal, stop=True, skip_group_check=True).then_inc(s_a, 1)

            def scores(h, c, j, n):
                r = max(0, j - TPC * c)
                w = CW - r * P
                out = S[n % 2]
                qh, ql, kh, kl = heads[h]
                q0, q1, k0, k1 = c * CW + r * P, (c + 1) * CW, j * P, (j + 1) * P
                diagonal = j >= TPC * c
                if diagonal:
                    pe.matmul(out[:, 0:P], identh[:], mask_cols[:], start=True, stop=False, skip_group_check=True)
                pe.matmul(out[:, 0:w], kh[0:KR, k0:k1], qh[0:KR, q0:q1], start=not diagonal, stop=False,
                          skip_group_check=True)
                pe.matmul(out[:, 0:w], kl[0:RH, k0:k1], qh[0:RH, q0:q1], start=False, stop=False, skip_group_check=True)
                pe.matmul(out[:, 0:w], kh[0:RH, k0:k1], ql[0:RH, q0:q1], start=False, stop=True,
                          skip_group_check=True).then_inc(s_st, 1)

            def values(h, c, j, n):
                r = max(0, j - TPC * c)
                high = prob[:, n % 3, :].bitcast(BF16).rearrange("p (q e) -> p q e", e=2)
                for s in range(r, TPC):
                    cs = slice((s - r) * P, (s - r + 1) * P)
                    at = (s % 2) * VW
                    done = j == TPC * c + s
                    pe.matmul(O[:, s // 2, at:at + VW], high[:, cs, 1], vh[h][:, j, :], start=(j == 0 and s % 2 == 0),
                              stop=False, skip_group_check=True)
                    ins = pe.matmul(O[:, s // 2, at:at + HS + 1], plow[:, n % 3, cs], vh[h][:, j, 0:HS + 1], start=False,
                                    stop=done, skip_group_check=True)
                ins.then_inc(s_pv, 1)

            pe.wait_ge(s_init, 1)
            for (kind, rel, c, tok) in pro_items:
                item(kind, rel, c, tok, -1, pos_tok=next(x[3] for x in pro_items if x[0] == "pos" and x[2] == c))
            for a in range(PRO_A):
                i, cc = A_TILES[a]
                if i % TPC == 0 and cc == 0:
                    pe.wait_ge(s_move[i // TPC], 2 * MOVES)
                if a >= 2:
                    pe.wait_ge(s_max, a - 1)
                row_scores(0, a, a)
                for (kind, rel, c, tok) in pro_max:
                    if a == a_end(c) + 1:
                        item(kind, rel, c, tok, -1)

            def pair(p, last):
                items = plan[last]
                for n in range(SLOTS + DRAIN):
                    if n < SLOTS:
                        h, (c, j) = n // NB, B_TILES[n % NB]
                        if n >= 2:
                            pe.wait_ge(s_exp, SLOTS * p + n - 1)
                        if j == 0:
                            pe.wait_ge(s_mrow[c], 16 * (2 * p + h + 1))
                        scores(h, c, j, n)
                        rel, a = A_SLOTS[n]
                        if not (last and rel == 2):
                            i, cc = A_TILES[a]
                            if i % TPC == 0 and cc == 0 and rel > 0:
                                pe.wait_ge(s_move[i // TPC], 2 * MOVES * (p + 1) + (MOVES if rel == 2 else 0))
                            pe.wait_ge(s_max, PRO_A + PER_A * p + n - 1)
                            row_scores(rel % 2, a, PRO_A + n)
                        for (kind, rel, c, tok) in items[n]:
                            item(kind, rel, c, tok, p, pos_tok=pos_item(items, c) if kind == "possum" else None,
                                 turn_tok=turn_item(items, rel, c) if kind == "project" else None)
                    if n >= DRAIN:
                        m = n - DRAIN
                        h, (c, j) = m // NB, B_TILES[m % NB]
                        if j == 0:
                            pe.wait_ge(s_oev, 2 * NC * p + NC * h + c + 1)
                            if c == 0:
                                pe.wait_ge(s_mv[h], 16 * (p + 1))
                        pe.wait_ge(s_low, SLOTS * p + m + 1)
                        values(h, c, j, m)

            with pe.Fori(0, PAIRS - 1) as p:
                pair(p, False)
            pair(PAIRS - 1, True)
            for (kind, rel, c, tok) in fin_items:
                item(kind, rel, c, (tok[0] - PER * (PAIRS - 1), tok[1], tok[2] - PER // 2 * (PAIRS - 1)), PAIRS - 1,
                     turn_tok=(fin_items[0][3][0], fin_items[0][3][1], fin_items[0][3][2] - PER // 2 * (PAIRS - 1)))

        @block.scalar
        def _(act):
            def item(kind, rel, c, tok, p, highs):
                it = max(p, 0) if isinstance(p, int) else p
                done, b, _ = count(tok, it)
                a0, a1 = c * CW, (c + 1) * CW
                if kind in ("pos", "project"):
                    return
                act.wait_ge(s_item, done)
                if kind in ("q", "k"):
                    if not ahead(p) and kind == "q":
                        act.wait_ge(s_move[c], 2 * MOVES * (p + 1))
                    if kind == "q":
                        act.activation(stage[QHI][:, a0:a1], M[b][:], ACT.Identity, bias=pair_b[:, 0:1]).then_inc(s_high, 1)
                    else:
                        act.activation(stage[KHI][:, a0:a1], M[b][:], ACT.Copy).then_inc(s_high, 1)
                elif kind == "possum":
                    act.activation(stage_pos[0:2 * FREQS, a0:a1], M[b][0:2 * FREQS, :], ACT.Copy).then_inc(s_high, 1)
                elif kind == "v":
                    if not ahead(p) and c == 0:
                        for h in (0, 1):
                            act.wait_ge(s_mv[h], 16 * (p + 1))
                    act.activation(stage_v[:, TPC * c:TPC * (c + 1), :, 0:HS],
                                   M[b][:].rearrange("p (n h d) -> p n h d", n=TPC, h=2), ACT.Copy).then_inc(s_high, 1)
                elif kind == "maxima":
                    if rel > 0:
                        act.wait_ge(s_mrow[c], 16 * (2 * p + rel))
                    act.activation(mrow[:, c, :], M[b][0:TPC, 0:P], ACT.Copy).then_inc(s_free[b], 1)
                elif kind == "turn":
                    act.activation(oT[:], M[b][:], ACT.Copy).then_inc(s_free[b], 1)

            act.sem_inc(s_oev, 1)
            for (kind, rel, c, tok) in pro_items:
                item(kind, rel, c, tok, -1, 0)
            for (kind, rel, c, tok) in pro_max:
                item(kind, rel, c, tok, -1, 0)

            def pair(p, last):
                for n in range(SLOTS + DRAIN):
                    if n < SLOTS:
                        h, (c, j) = n // NB, B_TILES[n % NB]
                        w = CW - max(0, j - TPC * c) * P
                        act.wait_ge(s_st, SLOTS * p + n + 1)
                        if n >= 3:
                            act.wait_ge(s_pv, SLOTS * p + n - 2)
                        act.activation(prob[:, n % 3, 0:w], S[n % 2][:, 0:w], ACT.Exp).then_inc(s_exp, 1)
                        for (kind, rel, c, tok) in plan[last][n]:
                            item(kind, rel, c, tok, p, 0)
                    if n >= DRAIN:
                        m = n - DRAIN
                        h, (c, j) = m // NB, B_TILES[m % NB]
                        if j == TPC * (c + 1) - 1:
                            g = NC * h + c
                            act.wait_ge(s_pv, SLOTS * p + m + 1)
                            if g > 0:
                                act.wait_ge(s_otok, 2 * NC * p + g)
                            act.activation(osb[:, c % 2, :, :].rearrange("p (a b) v -> p a (b v)", a=2),
                                           O[:, :, 0:2 * VW], ACT.Copy).then_inc(s_oev, 1)

            with act.Fori(0, PAIRS - 1) as p:
                pair(p, False)
            pair(PAIRS - 1, True)
            kind, rel, c, tok = fin_items[0]
            act.wait_ge(s_item, tok[0] + 1)
            act.activation(oT[:], M[tok[1]][:], ACT.Copy).then_inc(s_free[tok[1]], 1)

        @block.vector
        def _(dve):
            def item(kind, rel, c, tok, p, high):
                it = max(p, 0) if isinstance(p, int) else p
                done, b, _ = count(tok, it)
                a0, a1 = c * CW, (c + 1) * CW
                if kind in ("maxima", "turn"):
                    return
                dve.wait_ge(s_item, done)
                if kind == "pos":
                    ins = dve.scalar_tensor_tensor(turned[:], M[b][:], pair_b[:, 1:2], angle[:, a0:a1], ALU.add, ALU.mult)
                elif kind == "project":
                    s = acc[:, TPC * c:TPC * (c + 1), :]
                    ins = dve.tensor_tensor(s, M[b][:].rearrange("p (n d) -> p n d", d=D), s, ALU.add)
                else:
                    dve.wait_ge(s_high, HIGHS * (p + 1) + high + 1)
                    if kind == "q":
                        ins = dve.scalar_tensor_tensor(stage[QLO][:, a0:a1], M[b][:], pair_b[:, 0:1], stage[QHI][:, a0:a1],
                                                       ALU.add, ALU.subtract)
                    elif kind == "k":
                        ins = dve.tensor_tensor(stage[KLO][:, a0:a1], M[b][:], stage[KHI][:, a0:a1], ALU.subtract)
                    elif kind == "possum":
                        ins = dve.tensor_tensor(stage_pos[2 * FREQS:4 * FREQS, a0:a1], M[b][0:2 * FREQS, :],
                                                stage_pos[0:2 * FREQS, a0:a1], ALU.subtract)
                    elif kind == "v":
                        t = slice(TPC * c, TPC * (c + 1))
                        ins = dve.tensor_tensor(stage_v[:, t, :, HS + 1:VW], M[b][:].rearrange("p (n h d) -> p n h d", n=TPC, h=2),
                                                stage_v[:, t, :, 0:HS], ALU.subtract)
                ins.then_inc(s_free[b], 1)

            def row_max(h, a, g, p, head):
                i, cc = A_TILES[a]
                w = (i % TPC + 1) * P if cc == i // TPC else CW
                dve.wait_ge(s_a, g + 1 + PER_A * p)
                joins = (NT - TPC) * head + i - TPC
                if cc == 0 and i >= TPC and not (isinstance(joins, int) and joins < 2):
                    dve.wait_ge(s_neg, joins - 1)
                out = negm[:, h, i:i + 1] if i < TPC else part[:, i % 2, cc:cc + 1]
                dve.tensor_reduce(out, A[g % 2][:, 0:w], AX_X, ALU.max, negate=i < TPC).then_inc(s_max, 1)
                if cc == i // TPC and i >= TPC:
                    dve.wait_ge(s_max, g + 1 + PER_A * p)
                    dve.tensor_reduce(negm[:, h, i:i + 1], part[:, i % 2, 0:cc + 1], AX_X, ALU.max, negate=True).then_inc(s_neg, 1)

            dve.wait_ge(s_const, 32)
            table = otok[HS:RH, :, :].rearrange("p n d -> p (n d)")
            for h in (0, 1):
                dve.tensor_copy(heads[h][KHI][HS:RH, :], table).then_inc(s_init, 1)
                dve.memset(heads[h][KHI][RH:KR, :].bitcast(F32), 1.0)
            dve.wait_ge(s_init, 3)
            for h in (0, 1):
                ins = dve.tensor_tensor(heads[h][KLO][HS:RH, :], table, heads[h][KHI][HS:RH, :], ALU.subtract)
            ins.then_inc(s_init, 1)
            dve.wait_ge(s_init, 4)
            dve.memset(otok[:], 0.0).then_inc(s_otok, 1)

            high = 0
            for (kind, rel, c, tok) in pro_items:
                item(kind, rel, c, tok, -1, high)
                high += kind != "pos"
            for a in range(PRO_A):
                row_max(0, a, a, 0, 0)

            def pair(p, last):
                high = 0
                for n in range(SLOTS + 3):
                    if 1 <= n <= SLOTS:
                        m = n - 1
                        c, j = B_TILES[m % NB]
                        w = CW - max(0, j - TPC * c) * P
                        dve.wait_ge(s_exp, SLOTS * p + m + 1)
                        full = prob[:, m % 3, 0:w]
                        dve.tensor_tensor(plow[:, m % 3, 0:w], full,
                                          full.bitcast(BF16).rearrange("p (q e) -> p q e", e=2)[:, :, 1],
                                          ALU.subtract).then_inc(s_low, 1)
                    if n < SLOTS:
                        rel, a = A_SLOTS[n]
                        if not (last and rel == 2):
                            row_max(rel % 2, a, PRO_A + n, p, 2 * p + rel)
                        for (kind, rel, c, tok) in plan[last][n]:
                            item(kind, rel, c, tok, p, high)
                            high += kind in ("q", "k", "possum", "v")
                    if n >= 3:
                        m = n - 3
                        h, (c, j) = m // NB, B_TILES[m % NB]
                        if j == TPC * (c + 1) - 1:
                            dve.wait_ge(s_oev, 2 * NC * p + NC * h + c + 2)
                            dve.reciprocal(rsum[:, c % 2, :], osb[:, c % 2, :, HS]).then_inc(s_rec, 1)

            with dve.Fori(0, PAIRS - 1) as p:
                pair(p, False)
            pair(PAIRS - 1, True)
            kind, rel, c, tok = fin_items[1]
            dve.wait_ge(s_item, tok[0] + 1)
            s = acc[:, TPC * c:TPC * (c + 1), :]
            dve.tensor_tensor(s, M[tok[1]][:].rearrange("p (n d) -> p n d", d=D), s, ALU.add).then_inc(s_free[tok[1]], 1)
            dve.wait_ge(s_free[tok[1]], tok[2] + 1)
            dve.wait_ge(s_back, 32)
            for c in range(NC):
                s = acc[:, TPC * c:TPC * (c + 1), :].rearrange("p n d -> p (n d)")
                dve.tensor_tensor(s, s, xT[:, c * CW:(c + 1) * CW], ALU.mult).then_inc(s_fin, 1)
                dve.wait_ge(s_fin, 2 * c + 1)
                dve.tensor_tensor(s, s, angle[:, c * CW:(c + 1) * CW], ALU.add).then_inc(s_fin, 1)


def load_constants(nc, dram, keep):
    with ExitStack() as ctx:
        s_tables = ctx.enter_context(nc.semaphore("tables_loaded"))
        s_ones = ctx.enter_context(nc.semaphore("ones_set"))
        block = ctx.enter_context(nc.Block())

        @block.sync
        def _(sp):
            names = ("ident", "identh", "mask_rows", "mask_cols", "fold")
            for n in names:
                sp.dma_start(keep[n][:], dram[n]).then_inc(s_tables, 16)
            sp.wait_ge(s_tables, 16 * len(names))
            sp.wait_ge(s_ones, 1)

        @block.vector
        def _(dve):
            dve.memset(keep["ones"][:], 1.0).then_inc(s_ones, 1)


KEEP_BOTH = [("ident", [P, P], F32), ("identh", [P, P], BF16), ("mask_rows", [P, P], BF16),
             ("mask_cols", [P, P], BF16), ("ones", [P, P], F32), ("fold", [P, 2 * FREQS], F32)]
KEEP_L1 = [("wq", [P, HEADS * HS], F32), ("wk", [P, HEADS * HS], F32), ("wv", [P, HEADS * HS], F32),
           ("wpos", [P, PAIRS * P], F32), ("bpos", [P, PAIRS], F32), ("bq", [P, PAIRS], F32),
           ("wo", [P, PAIRS + 1, D], F32), ("xT", [P, T + 1], F32), ("angle", [P, T], F32)]
SCRATCH = [("x1_kept", [P, T]), ("gate_kept", [P, T]), ("xe_rows", [SLOT_ROWS, D]), ("ye_rows", [SLOT_ROWS, D])]


def build(nc, dram, out):
    for name, shape in SCRATCH:
        dram[name] = nc.dram_tensor(name, shape, F32, kind="Internal").ap()
    with ExitStack() as ctx:
        keep = {}
        for name, shape, dt in KEEP_BOTH:
            keep[name] = ctx.enter_context(nc.sbuf_tensor("keep_" + name, shape, dt))
        load_constants(nc, dram, keep)
        layer0(nc, dram, keep)
        for name, shape, dt in KEEP_L1:
            keep[name] = ctx.enter_context(nc.sbuf_tensor("keep_" + name, shape, dt))
        setup1(nc, dram, keep)
        attention1(nc, dram, keep, out)


def tables():
    f = np.float32
    i = np.arange(P)
    out = {}
    inv = (f(1.0) / np.power(f(10000.0), np.arange(0, MD, 2, dtype=f) / f(MD))).astype(f)
    theta = (np.arange(T, dtype=f)[:, None] * inv[None]).astype(np.float64)
    r = i % MD
    out["cos0"] = np.cos(theta)[:, r // 2].T.astype(f)
    out["sin0"] = (np.sin(theta)[:, r // 2] * np.where(r % 2 == 0, -1, 1)[None]).T.astype(f)
    same = (i // MD)[:, None] == (i // MD)[None]
    out["sel0"] = np.stack([same & (r[None] == m) for m in range(MD)] + [same], 1).astype(f)
    out["rank_order"] = np.broadcast_to(RE - np.arange(RE, dtype=f), (P, RE))
    out["below"] = (i[None] < i[:, None]).astype(f)
    w = 1250.0 ** (-(np.arange(0, FREQS, 2)) / FREQS)
    angle = w[:, None] * np.arange(T)[None]
    s, c = np.sin(angle), np.cos(angle)
    out["angle"] = np.concatenate([s, s, s, s, c, -c, c, -c]).astype(f)
    out["ktab"] = (np.concatenate([c, s]) / FREQS).astype(f)
    fold = np.zeros((P, 2 * FREQS), f)
    fold[i, i % (2 * FREQS)] = 1
    out["fold"] = fold
    bf16 = mybir.dt.np(BF16)
    out["ident"] = np.eye(P, dtype=f)
    out["identh"] = np.eye(P).astype(bf16)
    out["mask_rows"] = np.where(i[None] > i[:, None], -1e30, 0).astype(bf16)
    out["mask_cols"] = np.where(i[None] < i[:, None], -1e30, 0).astype(bf16)
    return out


def layout(a):
    out = {}
    out["x"] = a["L0_attn_x"][0]
    out["w_dw"] = a["L0_attn_w_dw"]
    wq, wk, wv = (a["L0_attn_w_qkv"][D * k:D * (k + 1)] for k in range(3))
    swap = np.arange(D) ^ 1
    out["w_sq"] = np.stack([a["L0_attn_w_pw"].T, wq.T, wq.T[:, swap], wk.T, wk.T[:, swap], a["L0_attn_w_gate"].T,
                            a["L0_attn_w_o"].T], 1)
    values = wv.T.reshape(D, MH, MD).transpose(0, 2, 1)
    out["w_vrep"] = np.repeat(values[:, :, :, None], MD, 3).reshape(D, MD, P)
    for name, key in (("b_gate", "b_gate"), ("ln_g", "ln_g"), ("ln_b", "ln_b")):
        out[name] = a["L0_attn_" + key][:, None]
    out["w_mg"] = a["L0_attn_w_moe_gate"].T
    out["w1"] = a["L0_attn_w1"].transpose(2, 0, 1).reshape(D, ME * HB, P)
    out["b1"] = a["L0_attn_b1"].reshape(ME * HB, P).T
    out["w2"] = a["L0_attn_w2"].reshape(ME, D, HB, P).transpose(3, 0, 2, 1).reshape(P, ME * HB, D)
    out["b2"] = a["L0_attn_b2"]
    out["wg"] = a["L0_ffn_Wg"]
    out["W1"] = a["L0_ffn_W1"].transpose(1, 0, 2)
    out["be1"] = a["L0_ffn_b1"].reshape(RE, RH2, P).transpose(2, 0, 1)
    out["W2"] = a["L0_ffn_W2"].reshape(RE, RH2, P, D).transpose(2, 0, 1, 3)
    out["be2"] = a["L0_ffn_b2"].T
    qkv = a["L1_attn_qkv"]
    for k, name in enumerate(("wq", "wk", "wv")):
        out[name] = qkv[:, k].reshape(D, HEADS * HS)
    out["wqT"] = qkv[:, 0].reshape(D, PAIRS, P).transpose(2, 1, 0)
    pos = a["L1_attn_positional"]
    even, odd = pos[0::2], pos[1::2]
    straight, swapped = np.concatenate([even, odd], 0), np.concatenate([odd, even], 0)
    pblk = np.zeros((P, PAIRS, P), pos.dtype)
    for h in (0, 1):
        rows = slice(HS * h, HS * (h + 1))
        pblk[rows, :, FREQS * h:FREQS * (h + 1)] = straight[:, h::2].transpose(2, 1, 0)
        pblk[rows, :, FREQS * (2 + h):FREQS * (3 + h)] = swapped[:, h::2].transpose(2, 1, 0)
    out["pblk"] = pblk
    out["bq"] = a["L1_attn_q_bias"].reshape(PAIRS, P).T
    out["wo"] = a["L1_attn_out_kernel"].reshape(PAIRS, P, D).transpose(1, 0, 2)
    out["out_bias"] = np.broadcast_to(a["L1_attn_out_bias"], (P, NT, D))
    out["ffw"] = np.stack([a["L1_ffn_W_r"].T, a["L1_ffn_W_k"].T, a["L1_ffn_W_v"].T], 1)
    out["mu"] = np.stack([a["L1_ffn_mu_r"], a["L1_ffn_mu_k"]], 1)
    return out


def kernel(**inputs):
    import concourse.bacc as _bacc
    from concourse.bass_utils import run_bass_kernel_spmd as _run

    nc = _bacc.Bacc("TRN2", target_bir_lowering=False, num_devices=1)
    arrays, dram = {}, {}
    host = {**layout({k: np.asarray(v) for k, v in inputs.items()}), **tables()}
    for name, a in host.items():
        a = np.ascontiguousarray(a)
        arrays["in_" + name] = a
        dram[name] = nc.dram_tensor("in_" + name, a.shape, mybir.dt.from_np(a.dtype), kind="ExternalInput").ap()
    out = nc.dram_tensor("out_0", (1, T, D), F32, kind="ExternalOutput").ap()
    build(nc, dram, out)
    r = _run(nc, [arrays], core_ids=[0])
    return r.results[0]["out_0"]
```

```python
from contextlib import ExitStack

import numpy as np
import concourse.bass as bass
from concourse import mybir

F32 = mybir.dt.float32
F32R = mybir.dt.float32r
BF16 = mybir.dt.bfloat16
F16 = mybir.dt.float16
ACT = mybir.ActivationFunctionType
ALU = mybir.AluOpType
AX_X = mybir.AxisListType.X

P = 128
T = 2048
D = 128
NT = T // P
CW = 512
NC = T // CW
TPC = CW // P
HEADS, HS, FREQS = 16, 64, 32
PAIRS = HEADS // 2
VW = 2 * HS + 1
C_QKV = (3.0 * D * HEADS * HS) ** -0.25
C_OUT = (HEADS * HS * D) ** -0.25
EPS = 1e-5

MH, MD = 16, 8
ME, MHID = 4, 4 * D
HB = MHID // P
RE, RH2 = 16, 2
CAP = -(-5 * T // (4 * RE))
SLOT_ROWS = RE * CAP
XT_ = SLOT_ROWS // P
EPS_DEN = 1e-6
I32 = mybir.dt.int32

B_TILES = [(c, j) for c in range(NC) for j in range(TPC * (c + 1))]
A_TILES = [(i, cc) for i in range(NT) for cc in range(i // TPC + 1)]
NB = len(B_TILES)
FAST = 256
LEAD = 10


def a_end(c):
    return sum(i // TPC + 1 for i in range(TPC * (c + 1)))


SLOTS = 2 * NB
PB = 6
POOL_EVERY = 4
DRAIN = 4
A_SLOTS = ([(0, NB - LEAD + n) for n in range(LEAD)] + [(1, n) for n in range(NB)]
           + [(2, n) for n in range(NB - LEAD)])


def on_pool(n):
    return n % POOL_EVERY == 2


def split_before(n, pool):
    return sum(on_pool(k) == pool for k in range(n + 1))


def plan_items(last):
    items = {n: [] for n in range(SLOTS)}
    items[4].append(("turn", -1, 3))
    items[7].append(("project", -1, 3))
    for n, a in enumerate(A_SLOTS):
        if last and a[0] == 2:
            continue
        for c in range(NC):
            if a[1] == a_end(c) - 1 and n + 2 < SLOTS:
                items[n + 2].append(("maxima", a[0], c))
    if not last:
        n = LEAD + 5
        for c in range(NC):
            for kind in ("q", "k", "pos", "v", "possum"):
                while items[n]:
                    n += 1
                items[n].append((kind, 1, c))
                n += 1
        assert n <= NB
    for c in range(NC - 1):
        n = NB + sum(TPC * (k + 1) for k in range(c + 1)) + DRAIN + 3
        while items[n]:
            n += 1
        items[n].append(("turn", 0, c))
        n += 3
        while items[n]:
            n += 1
        items[n].append(("project", 0, c))
    return items


class Bank:

    def __init__(self):
        self.n = 0
        self.of_bank = [0, 0]

    def take(self):
        bank = self.n % 2
        got = (self.n, bank, self.of_bank[bank])
        self.n += 1
        self.of_bank[bank] += 1
        return got



def ahead(p):
    return isinstance(p, int) and p == -1


def raw(ap):
    return ap.bitcast(F32)


def layernorm(dve, step, s_ln, s_sqrt, tok, stats, mv, vare, std, rstd, newt):
    for i in range(NT):
        ins = dve.bn_stats(stats[:, i, :], tok[:, i, :])
    step(ins)
    for i in range(NT):
        ins = dve.bn_aggr(mv[:, i, :], stats[:, i, :])
    step(ins)
    dve.tensor_scalar(vare[:], mv[:, :, 1], EPS, None, ALU.add).then_inc(s_ln, 1)
    dve.wait_ge(s_sqrt, 1)
    step(dve.reciprocal(rstd[:], std[:]))
    step(dve.tensor_tensor(newt[:], rstd[:], rstd[:], ALU.mult))
    step(dve.tensor_tensor(newt[:], newt[:], vare[:], ALU.mult))
    step(dve.tensor_scalar(newt[:], newt[:], -0.5, 1.5, ALU.mult, ALU.add))
    step(dve.tensor_tensor(rstd[:], rstd[:], newt[:], ALU.mult))


LATER = ("wg", "rank_order", "ln_g", "ln_b", "w_mg", "w1", "b1", "w2", "b2", "below", "W1", "W2", "be1", "be2")


def mixer0(nc, dram, keep, t0):
    ident = keep["ident"]
    x_tok, xn_tok, xnT, x2T = t0["x_tok"], t0["xn_tok"], t0["xnT"], t0["x2T"]
    with ExitStack() as ctx:
        def sb(name, shape, dt=F32):
            return ctx.enter_context(nc.sbuf_tensor(name, shape, dt))

        def sem(name):
            return ctx.enter_context(nc.semaphore(name))

        stats, mv = sb("stats0", [P, NT, 6]), sb("mv0", [P, NT, 2])
        vare, std, rstd, newt = (sb(n + "0", [P, NT]) for n in ("vare", "std", "rstd", "newt"))
        w_dw, w_sq = sb("w_dw", [P, 3]), sb("w_sq", [P, 7, D])
        b_gate = sb("b_gate", [P, 1])
        w_vrep = sb("w_vrep", [P, MD, P])
        cos, sin = keep["angle"], t0["s_tok"][:].rearrange("p n d -> p (n d)")
        sel = sb("sel0", [P, MD + 1, P])
        ones = sb("ones0", [P, CW])
        x1T = sb("x1T", [P, T + 1])
        y = sb("y0", [P, 2, CW])
        qk = sb("qk0", [P, 2, CW])
        qk2 = sb("qk20", [P, 2, CW])
        neg = sb("neg0", [P, 2, CW])
        phi = sb("phi0", [P, 2, 2, CW])
        delta = sb("delta0", [P, 2, CW])
        gate = sb("gate0", [P, 2, CW])
        kv = sb("kv0", [P, 2, CW])
        cum = sb("cum0", [P, 3, CW])
        last = sb("last0", [P, MD + 1])
        z = sb("z0", [P, 3, CW])
        den, attn = sb("den0", [P, CW]), sb("attn0", [P, CW])
        def banks(name, n):
            return [ctx.enter_context(nc.psum_tensor(f"{name}{i}", [P, CW], F32)) for i in range(n)]

        G, V, N, DEN = banks("general", 2), banks("values", 2), banks("numer", 2), banks("denom", 2)

        s_x, s_w, s_v = sem("x_loaded"), sem("w0_loaded"), sem("dve_step0")
        s_later = sem("later_loaded")
        s_ln, s_sqrt, s_xn = sem("ln_var0"), sem("ln_sqrt0"), sem("xn_tiles0")
        s_pad = sem("pads0")
        s_g, s_gf = sem("general_sums0"), [sem(f"general_out{i}") for i in range(2)]
        s_tap, s_y, s_shift = sem("conv_taps"), sem("conv_chunks"), sem("first_shift")
        s_sum, s_relu, s_exp, s_phi = sem("rot_summed"), sem("phi_relu"), sem("phi_exp"), sem("phi_done")
        s_delta = sem("deltas")
        s_vr, s_kv, s_cum, s_z = sem("v_rows"), sem("kv_products"), sem("prefixes"), sem("q_products")
        s_last = sem("last_columns")
        s_zu, s_attn, s_x2 = sem("products_summed"), sem("attn_chunks"), sem("x2_chunks")

        order = [("T", c) for c in range(NC)] + [(k, 0) for k in ("Y", "Q", "QS", "K", "KS", "G")]
        for c in range(NC + 1):
            for k, cc in (("Y", c + 1), ("Q", c + 1), ("QS", c + 1), ("K", c + 1), ("KS", c + 1), ("G", c + 1), ("O", c - 1)):
                if (0 <= cc < NC) and (k != "O" or cc >= 0):
                    order.append((k, cc))
        number = {k: n for n, k in enumerate(order)}
        SC = MD + 1
        block = ctx.enter_context(nc.Block())

        def bank(k):
            return G[number[k] % 2]

        def out(k, ins):
            ins.then_inc(s_gf[number[k] % 2], 1)

        def wait_out(engine, k):
            engine.wait_ge(s_gf[number[k] % 2], number[k] // 2 + 1)

        def span(c, off=0):
            return slice(off + c * CW, off + (c + 1) * CW)

        @block.sync
        def _(sp):
            for c in range(NC):
                a = slice(TPC * c, TPC * (c + 1))
                sp.dma_start(x_tok[:, a, :], dram["x"].rearrange("(n p) d -> p n d", p=P)[:, a, :]).then_inc(s_x, 16)
            for dst, src in ((w_dw, "w_dw"), (w_sq, "w_sq"), (cos, "cos0"), (sin, "sin0"), (b_gate, "b_gate"),
                             (w_vrep, "w_vrep"), (sel, "sel0")):
                sp.dma_start(dst[:], dram[src]).then_inc(s_w, 16)
            for name in ("wq", "wk", "wv", "bq"):
                sp.dma_start(keep[name][:], dram[name]).then_inc(s_later, 16)
            sp.dma_start(keep["wo"][:, 1:, :], dram["wo"]).then_inc(s_later, 16)
            for name in LATER:
                sp.dma_start(t0[name][:], dram[name]).then_inc(s_later, 16)
            sp.wait_ge(s_later, 16 * (5 + len(LATER)))
        WLOAD = 16 * 7

        @block.tensor
        def _(pe):
            def begin(k):
                n = number[k]
                if n >= 2:
                    pe.wait_ge(s_gf[n % 2], n // 2)

            def project(k, w, rhs):
                begin(k)
                pe.matmul(bank(k)[:], w_sq[:, w, :], rhs, start=True, stop=True).then_inc(s_g, 1)

            def projections(c, m):
                if m == 0:
                    pe.wait_ge(s_y, c + 1)
                    project(("Y", c), 0, y[:, c % 2, :])
                elif m == 1:
                    wait_out(pe, ("Y", c))
                    project(("Q", c), 1, x1T[:, span(c, 1)])
                    project(("QS", c), 2, x1T[:, span(c, 1)])
                elif m == 3:
                    project(("K", c), 3, x1T[:, span(c, 1)])
                    project(("KS", c), 4, x1T[:, span(c, 1)])
                elif m == 5:
                    pe.wait_ge(s_delta, c + 1)
                    project(("G", c), 5, delta[:, c % 2, :])

            def finish(c, m):
                if m == 6:
                    pe.wait_ge(s_attn, c + 1)
                    project(("O", c), 6, attn[:])

            for c in range(NC):
                begin(("T", c))
                for i in range(TPC):
                    pe.wait_ge(s_xn, TPC * c + i + 1)
                    ins = pe.transpose(bank(("T", c))[:, i * P:(i + 1) * P], xn_tok[:, TPC * c + i, :], ident[:])
                ins.then_inc(s_g, 1)
            pe.wait_ge(s_w, WLOAD)
            for m in range(SC):
                projections(0, m)
            for c in range(NC):
                def product(m):
                    pe.wait_ge(s_z, SC * c + m + 1)
                    out = (DEN if m == MD else N)[c % 2]
                    if c > 1 and m == 0:
                        pe.wait_ge(s_attn, c - 1)
                    pe.matmul(out[:], sel[:, m, :], z[:, (SC * c + m) % 3, :], start=m in (0, MD),
                              stop=m >= MD - 1).then_inc(s_zu, 1)
                def rows(c, m):
                    g = MD * c + m
                    if g >= 2:
                        pe.wait_ge(s_kv, g - 1)
                    pe.matmul(V[g % 2][:], w_vrep[:, m, :], x1T[:, span(c, 1)], start=True, stop=True).then_inc(s_vr, 1)

                if c == 0:
                    rows(0, 0)
                for m in range(MD):
                    if m + 1 < MD:
                        rows(c, m + 1)
                    elif c + 1 < NC:
                        rows(c + 1, 0)
                    if m >= 2:
                        product(m - 2)
                    if c > 0:
                        finish(c - 1, m)
                    if c + 1 < NC:
                        projections(c + 1, m)
                for m in range(MD - 2, SC):
                    product(m)
            finish(NC - 1, 6)

        @block.scalar
        def _(act):
            def first_tap(c):
                wait_out(act, ("T", c))
                if c >= 2:
                    act.wait_ge(s_g, number[("Y", c - 2)] + 1)
                act.activation(y[:, c % 2, :], xnT[:, span(c, 0)], ACT.Copy, scale=w_dw[:, 0:1]).then_inc(s_tap, 1)

            def projections(c, m):
                if m in (3, 5):
                    j = (m - 3) // 2
                    act.wait_ge(s_sum, 2 * c + j + 1)
                    act.activation(neg[:, j, :], qk[:, j, :], ACT.Relu, scale=-1.0).then_inc(s_relu, 1)
                    act.wait_ge(s_relu, 2 * c + j + 1)
                    act.activation(neg[:, j, :], neg[:, j, :], ACT.Exp, scale=-1.0).then_inc(s_exp, 1)
                elif m == 6:
                    k = ("G", c)
                    act.wait_ge(s_g, number[k] + 1)
                    if c >= 2:
                        act.wait_ge(s_x2, c - 1)
                    out(k, act.activation(gate[:, c % 2, :], bank(k)[:], ACT.Sigmoid, bias=b_gate[:, 0:1]))

            act.wait_ge(s_ln, 1)
            act.activation(std[:], vare[:], ACT.Sqrt).then_inc(s_sqrt, 1)
            for c in range(NC):
                act.wait_ge(s_g, number[("T", c)] + 1)
                out(("T", c), act.activation(xnT[:, span(c, 2)], bank(("T", c))[:], ACT.Copy))
            act.wait_ge(s_w, WLOAD)
            act.wait_ge(s_pad, 1)
            first_tap(0)
            for m in range(SC):
                projections(0, m)
            for c in range(NC):
                if c + 1 < NC:
                    first_tap(c + 1)
                for m in range(SC):
                    g = SC * c + m
                    act.wait_ge(s_cum, g + 1)
                    act.activation(last[:, m:m + 1], cum[:, g % 3, CW - 1:CW], ACT.Copy).then_inc(s_last, 1)
                    if c + 1 < NC:
                        projections(c + 1, m)

        @block.gpsimd
        def _(pool):
            def projections(c, m):
                if m == 1:
                    wait_out(pool, ("Y", c))
                    if c == 0:
                        pool.wait_ge(s_shift, 1)
                    else:
                        wait_out(pool, ("G", c - 1))
                    pool.tensor_tensor(delta[:, c % 2, :], x1T[:, span(c, 1)], x1T[:, span(c, 0)],
                                       ALU.subtract).then_inc(s_delta, 1)
                elif m in (2, 4):
                    j = (m - 2) // 2
                    for k in (("Q", "QS"), ("K", "KS"))[j]:
                        wait_out(pool, (k, c))
                    pool.tensor_tensor(qk[:, j, :], qk[:, j, :], qk2[:, j, :], ALU.add).then_inc(s_sum, 1)

            pool.memset(ones[:], 1.0)
            pool.memset(xnT[:, 0:2], 0.0).then_inc(s_pad, 1)
            for m in range(SC):
                projections(0, m)
            for c in range(NC):
                for m in range(SC):
                    g = SC * c + m
                    pool.wait_ge(s_cum, g + 1)
                    if g >= 3:
                        pool.wait_ge(s_zu, g - 2)
                    pool.tensor_tensor(z[:, g % 3, :], cum[:, g % 3, :], phi[:, c % 2, 0, :], ALU.mult).then_inc(s_z, 1)
                    if c + 1 < NC:
                        projections(c + 1, m)

        @block.vector
        def _(dve):
            steps = [0]

            def step(ins):
                steps[0] += 1
                ins.then_inc(s_v, 1)
                dve.wait_ge(s_v, steps[0])

            def projections(c, m):
                if m == 0:
                    yc = y[:, c % 2, :]
                    dve.wait_ge(s_tap, 2 * c + 1)
                    dve.scalar_tensor_tensor(yc, xnT[:, span(c, 1)], w_dw[:, 1:2], yc, ALU.mult, ALU.add).then_inc(s_tap, 1)
                    dve.wait_ge(s_tap, 2 * c + 2)
                    dve.scalar_tensor_tensor(yc, xnT[:, span(c, 2)], w_dw[:, 2:3], yc, ALU.mult, ALU.add).then_inc(s_y, 1)
                elif m == 1:
                    dve.wait_ge(s_g, number[("Y", c)] + 1)
                    out(("Y", c), dve.tensor_tensor(x1T[:, span(c, 1)], bank(("Y", c))[:], xnT[:, span(c, 2)], ALU.add))
                    if c == 0:
                        wait_out(dve, ("Y", c))
                        dve.tensor_copy(x1T[:, 0:1], x1T[:, 1:2]).then_inc(s_shift, 1)
                elif m in (2, 4):
                    j = (m - 2) // 2
                    k = "QK"[j]
                    if c > 0:
                        dve.wait_ge(s_phi, 2 * (c - 1) + j + 1)
                    for t, kk, tab in ((qk, k, cos), (qk2, k + "S", sin)):
                        dve.wait_ge(s_g, number[(kk, c)] + 1)
                        out((kk, c), dve.tensor_tensor(t[:, j, :], bank((kk, c))[:], tab[:, span(c)], ALU.mult))
                elif m in (5, 7):
                    j = (m - 5) // 2
                    dve.wait_ge(s_exp, 2 * c + j + 1)
                    if c >= 2:
                        dve.wait_ge(s_z, SC * (c - 1))
                    dve.scalar_tensor_tensor(phi[:, c % 2, j, :], qk[:, j, :], 0.0, neg[:, j, :], ALU.max,
                                             ALU.add).then_inc(s_phi, 1)

            def finish(c, m):
                if m == 3:
                    dve.wait_ge(s_zu, SC * (c + 1))
                    if c > 0:
                        dve.wait_ge(s_attn, c)
                        dve.wait_ge(s_g, number[("O", c - 1)] + 1)
                    step(dve.tensor_scalar(den[:], DEN[c % 2][:], EPS_DEN, None, ALU.add))
                elif m == 4:
                    step(dve.reciprocal(den[:], den[:]))
                elif m == 5:
                    dve.tensor_tensor(attn[:], N[c % 2][:], den[:], ALU.mult).then_inc(s_attn, 1)
                elif m == 7:
                    dve.wait_ge(s_g, number[("O", c)] + 1)
                    wait_out(dve, ("G", c))
                    out(("O", c), dve.tensor_tensor(x2T[:, span(c)], bank(("O", c))[:], gate[:, c % 2, :], ALU.mult))
                    wait_out(dve, ("O", c))
                    dve.tensor_tensor(x2T[:, span(c)], x2T[:, span(c)], x1T[:, span(c, 1)], ALU.add).then_inc(s_x2, 1)

            dve.wait_ge(s_x, 16 * NC)
            layernorm(dve, step, s_ln, s_sqrt, x_tok, stats, mv, vare, std, rstd, newt)
            for i in range(NT):
                dve.tensor_scalar(xn_tok[:, i, :], x_tok[:, i, :], mv[:, i, 0:1], rstd[:, i:i + 1], ALU.subtract,
                                  ALU.mult).then_inc(s_xn, 1)
            dve.memset(last[:], 0.0).then_inc(s_last, 1)
            dve.wait_ge(s_w, WLOAD)
            dve.wait_ge(s_pad, 1)
            for m in range(SC):
                projections(0, m)

            def product(c, m):
                g = MD * c + m
                dve.wait_ge(s_vr, g + 1)
                if g >= 2:
                    dve.wait_ge(s_cum, SC * ((g - 2) // MD) + (g - 2) % MD + 1)
                dve.tensor_tensor(kv[:, g % 2, :], V[g % 2][:], phi[:, c % 2, 1, :], ALU.mult).then_inc(s_kv, 1)

            for c in range(NC):
                if c == 0:
                    dve.wait_ge(s_phi, 2)
                    product(0, 0)
                for m in range(SC):
                    g = SC * c + m
                    if m + 1 < MD:
                        product(c, m + 1)
                    elif m == MD and c + 1 < NC:
                        dve.wait_ge(s_phi, 2 * c + 4)
                        product(c + 1, 0)
                    if m < MD:
                        dve.wait_ge(s_kv, MD * c + m + 1)
                        src = kv[:, (MD * c + m) % 2, :]
                    else:
                        src = phi[:, c % 2, 1, :]
                    if g >= 3:
                        dve.wait_ge(s_z, g - 2)
                        dve.wait_ge(s_last, g - 1)
                    dve.wait_ge(s_last, max(1, g - SC + 2))
                    dve.tensor_tensor_scan(cum[:, g % 3, :], ones[:], src, last[:, m:m + 1], ALU.mult,
                                           ALU.add).then_inc(s_cum, 1)
                    if c > 0:
                        finish(c - 1, m)
                    if c + 1 < NC:
                        projections(c + 1, m)
            for m in range(SC):
                finish(NC - 1, m)


def experts0(nc, dram, keep, t0):
    x_tok, W1, W2, be1, be2 = (t0[n] for n in ("x_tok", "W1", "W2", "be1", "be2"))
    ident = keep["ident"]
    xn_tok, xnT, x2T, s_tok = t0["xn_tok"], t0["xnT"], t0["x2T"], t0["s_tok"]
    slot, y_tok, xe = t0["slot"], t0["y_tok"], t0["xe"]
    with ExitStack() as ctx:
        def sb(name, shape, dt=F32):
            return ctx.enter_context(nc.sbuf_tensor(name, shape, dt))

        def sem(name):
            return ctx.enter_context(nc.semaphore(name))

        stats, mv = sb("stats0b", [P, NT, 6]), sb("mv0b", [P, NT, 2])
        vare, std, rstd, newt = (sb(n + "0b", [P, NT]) for n in ("vare", "std", "rstd", "newt"))
        lng, lnb, w_mg, w1, b1, w2, b2, wg, rank_order, below = (
            t0[n] for n in ("ln_g", "ln_b", "w_mg", "w1", "b1", "w2", "b2", "wg", "rank_order", "below"))
        h_tok, hT = x2T[:].rearrange("p (n d) -> p n d", d=D), keep["xT"]
        hid = sb("hid0", [P, 2, HB, CW])
        rdiff, rexp = sb("rdiff", [P, NT, RE]), sb("rexp", [P, NT, RE])
        cand, onehot = sb("cand", [P, NT, RE]), sb("onehot", [P, NT, RE])
        rmax, rsum, val, r1, r2, cmax, rank, over, slotf = (
            sb(n, [P, NT]) for n in ("rmax", "rsum0", "val", "r1", "r2", "cmax", "rank", "over", "slotf"))
        vparts_b, vparts = sb("vparts_b", [P, 2, NT], BF16), sb("vparts", [P, 3, NT])
        OH3, MV3 = sb("OH3", [P, NT, 3, RE]), sb("MV3", [P, NT, 3, RE])
        ohT, mvT = sb("ohT", [P, T], BF16), sb("mvT", [P, T], BF16)
        counts = sb("counts", [P, NT, NC + 2])
        seen, same = sb("seen", [P, 2, CW], BF16), sb("same", [P, 2, P], BF16)
        gdiff, gexp, gw = sb("gdiff", [P, NT, ME]), sb("gexp", [P, NT, ME]), sb("gw", [P, NT, ME])
        gmax, gsum = sb("gmax", [P, NT]), sb("gsum", [P, NT])
        xeT, yeT = sb("xeT", [P, SLOT_ROWS]), sb("yeT", [P, SLOT_ROWS])
        gwT = yeT[0:ME, 0:T]
        ye = xe
        hE = x2T[:, 0:3 * RH2 * CAP].rearrange("p (k b s) -> p k b s", k=3, b=RH2)
        g = xnT[:, 0:T].rearrange("p (n d) -> p n d", d=D)
        zero = sb("zero0", [P, P])
        G = [ctx.enter_context(nc.psum_tensor(f"EG{i}", [P, CW], F32)) for i in range(2)]
        H = [ctx.enter_context(nc.psum_tensor(f"EH{i}", [P, CW], F32)) for i in range(2)]
        E = [ctx.enter_context(nc.psum_tensor(f"EE{i}", [P, CW], F32)) for i in range(2)]
        R = [ctx.enter_context(nc.psum_tensor(f"ER{i}", [P, CW], F32)) for i in range(2)]

        s_v = sem("dve_step0b")
        s_ln, s_sqrt, s_hn = sem("ln_var0b"), sem("ln_sqrt0b"), sem("h_tiles")
        s_g, s_gf = sem("general_sums0b"), [sem(f"general_outb{i}") for i in range(2)]
        s_x2, s_hT = sem("x2_tokens"), sem("hT_chunks")
        s_rd, s_re = sem("route_diff"), sem("route_exp")
        s_oh, s_ohT = sem("onehots"), sem("onehots_turned")
        s_gd, s_ge, s_gw = sem("gate_diff"), sem("gate_exp"), sem("gate_weights")
        s_gwT, s_b2 = sem("gate_turned"), sem("bias_added")
        s_h, s_hid, s_e, s_acc = sem("hidden_sums"), sem("hidden"), sem("expert_sums"), sem("expert_added")
        s_r, s_rc = sem("route_rows"), sem("route_counted")
        s_slot, s_zero, s_fill = sem("slots"), sem("zero_set"), sem("slots_filled")
        s_sc, s_xe, s_y = sem("tokens_sent"), sem("tokens_back"), sem("y_filled")
        s_t, s_xT, s_rh, s_rhid = sem("xe_turned"), sem("xeT_out"), sem("routed_sums"), sem("routed_hidden")
        s_ry, s_yT, s_ye, s_st = sem("y_sums"), sem("yT_out"), sem("ye_out"), sem("ye_stored")
        s_ga, s_sg, s_m, s_end = sem("gathered"), sem("gates0b"), sem("s_times_g"), sem("x1_done")
        s_blank = sem("rows_blank")
        wq, wk, wv, wo, wpos, bpos, bq, ones = (keep[n] for n in ("wq", "wk", "wv", "wo", "wpos", "bpos", "bq", "ones"))
        s_sq, s_nsum, s_nrt = sem("squares1"), sem("norm_sums1"), sem("norm_roots1")
        s_rn, s_ncol, s_turn_w = sem("norm_recips1"), sem("norm_cols1"), sem("wqT_loaded1")
        s_wp, s_wpc = sem("wpos_sums1"), sem("wpos_copied1")
        KV = HEADS * HS
        free = xn_tok[:].rearrange("p n d -> p (n d)")
        sq, norm = free[:, 0:KV], free[:, KV:2 * KV]
        free = W1[:].rearrange("p e h -> p (e h)")
        wqT, pblk = (free[:, k * KV:(k + 1) * KV].rearrange("p (j r) -> p j r", r=P) for k in (0, 1))
        ncol = rsum
        XC = XT_ // TPC

        order = ([("RL", 0)] + [("X", c) for c in range(NC)] + [("OT", c) for c in range(NC)] + [("MT", c) for c in range(NC)]
                 + [("HT", c) for c in range(NC)] + [("GL", 0)] + [("GT", c) for c in range(NC)]
                 + [("B2", c) for c in range(NC)])
        number = {k: n for n, k in enumerate(order)}

        def bank(k):
            return G[number[k] % 2]

        def span(c, off=0):
            return slice(off + c * CW, off + (c + 1) * CW)

        def tiles(c):
            return slice(TPC * c, TPC * (c + 1))

        def t4(ap):
            return ap.rearrange("p (n d) -> p n d", n=TPC)

        UNITS = [(i, cc) for i in range(NT) for cc in range(NC)]
        GROUPS = [(c, e) for c in range(NC) for e in range(ME)]
        PER_HB = 2
        ROUTED_AT = 10
        block = ctx.enter_context(nc.Block())

        @block.sync
        def _(sp):
            sp.wait_ge(s_zero, 1)
            sp.dma_start(dram["xe_rows"].rearrange("(n p) d -> p n d", p=P),
                         zero[:].unsqueeze(1).to_broadcast([P, XT_, P])).then_inc(s_fill, 16)
            sp.wait_ge(s_sc, 16 * NT)
            sp.dma_start(xe[:], dram["xe_rows"].rearrange("(n p) d -> p n d", p=P)).then_inc(s_xe, 16)
            sp.wait_ge(s_rh, RE)
            for dst, src in ((wqT, "wqT"), (pblk, "pblk")):
                sp.dma_start(dst, dram[src]).then_inc(s_turn_w, 16)
            rows = dram["ye_rows"].rearrange("(n p) d -> p n d", p=P)
            for c in range(XC):
                a = slice(TPC * c, TPC * (c + 1))
                sp.wait_ge(s_ye, c + 1)
                sp.dma_start(rows[:, a, :], ye[:, a, :]).then_inc(s_st, 16)
            sp.wait_ge(s_st, 16 * XC)

        @block.gpsimd
        def _(pool):
            pool.memset(zero[:], 0.0).then_inc(s_zero, 1)
            pool.memset(ohT[:], 0.0)
            pool.memset(mvT[:], 0.0).then_inc(s_blank, 1)
            pool.tensor_copy(y_tok[:], xn_tok[:]).then_inc(s_y, 1)
            pool.wait_ge(s_fill, 16)
            pool.wait_ge(s_slot, 1)
            for i in range(NT):
                pool.indirect_dma_start(dram["xe_rows"], bass.IndirectOffsetOnAxis(slot[:, i:i + 1], 0), xn_tok[:, i, :], None,
                                        bounds_check=SLOT_ROWS - 1, oob_is_err=False).then_inc(s_sc, 16)
            pool.wait_ge(s_st, 16 * XC)
            pool.wait_ge(s_y, 1)
            for i in range(NT):
                pool.indirect_dma_start(y_tok[:, i, :], None, dram["ye_rows"], bass.IndirectOffsetOnAxis(slot[:, i:i + 1], 0),
                                        bounds_check=SLOT_ROWS - 1, oob_is_err=False).then_inc(s_ga, 16)

        @block.tensor
        def _(pe):
            def begin(k):
                n = number[k]
                if n >= 2:
                    pe.wait_ge(s_gf[n % 2], n // 2)

            def turn(k, src, rows=P, waits=None):
                begin(k)
                for i in range(TPC):
                    t = TPC * k[1] + i
                    if waits is not None:
                        pe.wait_ge(waits, t + 1)
                    ins = pe.transpose(bank(k)[0:rows, i * P:(i + 1) * P], src(t), ident[:])
                ins.then_inc(s_g, 1)

            for i in range(NT):
                ins = pe.matmul(bank(("RL", 0))[:, i * RE:(i + 1) * RE], xnT[:, 2 + i * P:2 + (i + 1) * P], wg[:],
                                start=True, stop=True)
            ins.then_inc(s_g, 1)
            for c in range(NC):
                turn(("X", c), lambda t: x2T[:, t * P:(t + 1) * P])
            pe.wait_ge(s_oh, 1)
            for c in range(NC):
                turn(("OT", c), lambda t: OH3[:, t, :, :].rearrange("p a b -> p (a b)"), 3 * RE)
            for c in range(NC):
                turn(("MT", c), lambda t: MV3[:, t, :, :].rearrange("p a b -> p (a b)"), 3 * RE)
            for c in range(NC):
                turn(("HT", c), lambda t: h_tok[:, t, :], P, s_hn)
            pe.wait_ge(s_hT, NC)
            begin(("GL", 0))
            for i in range(NT):
                ins = pe.matmul(bank(("GL", 0))[:, i * ME:(i + 1) * ME], hT[:, i * P:(i + 1) * P], w_mg[:],
                                start=True, stop=True)
            ins.then_inc(s_g, 1)

            def bias_part():
                pe.wait_ge(s_gw, 1)
                for c in range(NC):
                    turn(("GT", c), lambda t: gw[:, t, :], ME)
                for c in range(NC):
                    pe.wait_ge(s_gwT, c + 1)
                    begin(("B2", c))
                    for i in range(TPC):
                        t = TPC * c + i
                        ins = pe.matmul(bank(("B2", c))[:, i * P:(i + 1) * P], gwT[:, t * P:(t + 1) * P], b2[:],
                                        start=True, stop=True)
                    ins.then_inc(s_g, 1)

            unit = [0]

            def route_rows():
                for _ in range(PER_HB):
                    u = unit[0]
                    if u >= len(UNITS):
                        return
                    i, cc = UNITS[u]
                    if u == 0:
                        pe.wait_ge(s_ohT, 2 * NC)
                    if u >= 2:
                        pe.wait_ge(s_rc, u - 1)
                    pe.matmul(R[u % 2][:], ohT[:, i * P:(i + 1) * P], mvT[:, span(cc)], start=True, stop=True).then_inc(s_r, 1)
                    unit[0] += 1

            def first(n):
                c, e = GROUPS[n]
                for hb in range(HB):
                    k = n * HB + hb
                    if k >= 2:
                        pe.wait_ge(s_hid, k - 1)
                    pe.matmul(H[k % 2][:], w1[:, e * HB + hb, :], hT[:, span(c)], start=True, stop=True).then_inc(s_h, 1)
                    route_rows()

            def second(n):
                c, e = GROUPS[n]
                pe.wait_ge(s_hid, (n + 1) * HB)
                if n >= 2:
                    pe.wait_ge(s_acc, n - 1)
                for i in range(TPC):
                    for hb in range(HB):
                        ins = pe.matmul(E[n % 2][:, i * P:(i + 1) * P], hid[:, n % 2, hb, i * P:(i + 1) * P],
                                        w2[:, e * HB + hb, :], start=hb == 0, stop=hb == HB - 1)
                ins.then_inc(s_e, 1)

            def routed():
                pe.wait_ge(s_xe, 16)
                for c in range(XC):
                    if c < 2:
                        pe.wait_ge(s_gf[(len(order) + c) % 2], (len(order) + c) // 2)
                    else:
                        pe.wait_ge(s_xT, c - 1)
                    for i in range(TPC):
                        ins = pe.transpose(G[(len(order) + c) % 2][:, i * P:(i + 1) * P], xe[:, TPC * c + i, :], ident[:])
                    ins.then_inc(s_t, 1)

                def up(e):
                    pe.wait_ge(s_xT, -(-(e + 1) * CAP // CW))
                    pe.wait_ge(s_rc, len(UNITS)) if e == 0 else None
                    if e >= 2:
                        pe.wait_ge(s_rhid, 2 * (e - 1))
                    for b in range(RH2):
                        ins = pe.matmul(R[e % 2][:, b * CAP:(b + 1) * CAP], W1[:, e, b * P:(b + 1) * P],
                                        xeT[:, e * CAP:(e + 1) * CAP], start=True, stop=True)
                    ins.then_inc(s_rh, 1)

                def down(e):
                    pe.wait_ge(s_rhid, 2 * e + 2)
                    if e == 0:
                        pe.wait_ge(s_xT, XC)
                    if e >= 2:
                        pe.wait_ge(s_yT, e - 1)
                    for b in range(RH2):
                        ins = pe.matmul(G[e % 2][:, 0:CAP], W2[:, e, b, :], hE[:, e % 3, b, :], start=b == 0,
                                        stop=b == RH2 - 1)
                    ins.then_inc(s_ry, 1)

                for e in range(RE + 1):
                    if e < RE:
                        up(e)
                    if e >= 1:
                        down(e - 1)
                for c in range(XC):
                    pe.wait_ge(s_yT, -(-(c + 1) * CW // CAP))
                    if c >= 2:
                        pe.wait_ge(s_ye, c - 1)
                    for i in range(TPC):
                        t = TPC * c + i
                        ins = pe.transpose(R[c % 2][:, i * P:(i + 1) * P], yeT[:, t * P:(t + 1) * P], ident[:])
                    ins.then_inc(s_t, 1)

            def weights1(n):
                if n == ROUTED_AT + 1:
                    pe.wait_ge(s_sq, 1)
                    pe.wait_ge(s_ye, XC)
                    for k in range(2):
                        pe.matmul(R[k][:], ones[:], sq[:, k * CW:(k + 1) * CW], start=True, stop=True).then_inc(s_nsum, 1)
                elif n == ROUTED_AT + 2:
                    pe.wait_ge(s_turn_w, 32)
                    for k in range(2):
                        for i in range(TPC):
                            j = TPC * k + i
                            ins = pe.matmul(G[k][:, i * P:(i + 1) * P], wqT[:, j, :], pblk[:, j, :], start=True, stop=True)
                        ins.then_inc(s_wp, 1)
                elif n == ROUTED_AT + 3:
                    pe.wait_ge(s_wpc, 2)
                    for j in range(PAIRS):
                        ins = pe.matmul(G[0][:, j:j + 1], pblk[:, j, :], bq[:, j:j + 1], start=True, stop=True)
                    ins.then_inc(s_wp, 1)
                elif n == ROUTED_AT + 4:
                    pe.wait_ge(s_rn, 1)
                    for j in range(PAIRS):
                        ins = pe.matmul(G[1][:, j:j + 1], norm[0:1, j * P:(j + 1) * P], ones[0:1, 0:1], start=True, stop=True)
                    ins.then_inc(s_ncol, 1)

            first(0)
            bias_part()
            for n in range(len(GROUPS)):
                if n + 1 < len(GROUPS):
                    first(n + 1)
                if n == ROUTED_AT:
                    routed()
                weights1(n)
                second(n)

        @block.scalar
        def _(act):
            def out(k, dst, src, sem_done, n_done, func=ACT.Copy, **kw):
                act.wait_ge(s_g, number[k] + 1)
                act.activation(dst, src, func, **kw).then_inc(sem_done, 1)
                act.wait_ge(sem_done, n_done)
                act.sem_inc(s_gf[number[k] % 2], 1)

            for c in range(NC):
                out(("X", c), s_tok[:, tiles(c), :], t4(bank(("X", c))[:]), s_x2, c + 1)
            act.wait_ge(s_rd, 1)
            act.activation(rexp[:], rdiff[:], ACT.Exp).then_inc(s_re, 1)
            act.wait_ge(s_blank, 1)
            for c in range(NC):
                out(("OT", c), ohT[0:3 * RE, span(c)], bank(("OT", c))[0:3 * RE, :], s_ohT, c + 1)
            for c in range(NC):
                out(("MT", c), mvT[0:3 * RE, span(c)], bank(("MT", c))[0:3 * RE, :], s_ohT, NC + c + 1)
            act.wait_ge(s_ln, 1)
            act.activation(std[:], vare[:], ACT.Sqrt).then_inc(s_sqrt, 1)
            for c in range(NC):
                out(("HT", c), hT[:, span(c)], bank(("HT", c))[:], s_hT, c + 1, ACT.Identity, bias=lnb[:, 0:1],
                    scale=lng[:, 0:1])

            def hidden(n):
                c, e = GROUPS[n]
                for hb in range(HB):
                    k = n * HB + hb
                    act.wait_ge(s_h, k + 1)
                    if n >= 2:
                        act.wait_ge(s_e, n - 1)
                    act.activation(hid[:, n % 2, hb, :], H[k % 2][:], ACT.Silu,
                                   bias=b1[:, e * HB + hb:e * HB + hb + 1]).then_inc(s_hid, 1)

            act.wait_ge(s_gd, 1)
            act.activation(gexp[:], gdiff[:], ACT.Exp).then_inc(s_ge, 1)
            hidden(0)
            for c in range(NC):
                out(("GT", c), gwT[:, span(c)], bank(("GT", c))[0:ME, :], s_gwT, c + 1)
            def routed():
                for c in range(XC):
                    act.wait_ge(s_t, c + 1)
                    act.activation(xeT[:, c * CW:(c + 1) * CW], G[(len(order) + c) % 2][:], ACT.Copy).then_inc(s_xT, 1)
                for e in range(RE):
                    act.wait_ge(s_rh, e + 1)
                    if e >= 3:
                        act.wait_ge(s_ry, e - 2)
                    for b in range(RH2):
                        act.activation(hE[:, e % 3, b, :], R[e % 2][:, b * CAP:(b + 1) * CAP], ACT.Gelu_apprx_tanh,
                                       bias=be1[:, e, b:b + 1]).then_inc(s_rhid, 1)

            for n in range(len(GROUPS)):
                if n + 1 < len(GROUPS):
                    hidden(n + 1)
                if n == ROUTED_AT:
                    routed()
                elif n == ROUTED_AT + 1:
                    for k in range(2):
                        act.wait_ge(s_nsum, k + 1)
                        act.activation(norm[:, k * CW:(k + 1) * CW], R[k][:], ACT.Sqrt).then_inc(s_nrt, 1)
                elif n == ROUTED_AT + 2:
                    for k in range(2):
                        act.wait_ge(s_wp, k + 1)
                        act.activation(wpos[:, k * CW:(k + 1) * CW], G[k][:], ACT.Copy, scale=C_QKV).then_inc(s_wpc, 1)
                elif n == ROUTED_AT + 3:
                    act.wait_ge(s_wp, 3)
                    act.activation(bpos[:], G[0][:, 0:PAIRS], ACT.Copy).then_inc(s_wpc, 1)
            act.wait_ge(s_ga, 16 * NT)
            for c in range(NC):
                act.activation(g[:, tiles(c), :], y_tok[:, tiles(c), :], ACT.Silu).then_inc(s_sg, 1)

        @block.vector
        def _(dve):
            steps = [0]

            def step(ins):
                steps[0] += 1
                ins.then_inc(s_v, 1)
                dve.wait_ge(s_v, steps[0])

            def bc(t, n):
                return t[:].unsqueeze(2).to_broadcast([P, NT, n])

            dve.memset(counts[:], 0.0)
            L = bank(("RL", 0))[:, 0:NT * RE].rearrange("p (n e) -> p n e", n=NT)
            dve.wait_ge(s_g, 1)
            step(dve.tensor_reduce(rmax[:], L, AX_X, ALU.max))
            dve.tensor_tensor(rdiff[:], L, bc(rmax, RE), ALU.subtract).then_inc(s_rd, 1)
            step(dve.tensor_tensor(cand[:], L, bc(rmax, RE), ALU.is_ge))
            dve.sem_inc(s_gf[0], 1)
            step(dve.tensor_tensor(cand[:], cand[:], rank_order[:].unsqueeze(1).to_broadcast([P, NT, RE]), ALU.mult))
            step(dve.tensor_reduce(cmax[:], cand[:], AX_X, ALU.max))
            step(dve.tensor_tensor(onehot[:], cand[:], bc(cmax, RE), ALU.is_equal))
            dve.wait_ge(s_re, 1)
            step(dve.tensor_reduce(rsum[:], rexp[:], AX_X, ALU.add))
            step(dve.reciprocal(val[:], rsum[:]))
            step(dve.tensor_copy(vparts_b[:, 0, :], val[:]))
            step(dve.tensor_tensor(r1[:], val[:], vparts_b[:, 0, :], ALU.subtract))
            step(dve.tensor_copy(vparts_b[:, 1, :], r1[:]))
            dve.tensor_tensor(vparts[:, 2, :], r1[:], vparts_b[:, 1, :], ALU.subtract)
            step(dve.tensor_copy(vparts[:, 0:2, :], vparts_b[:]))
            for k in range(3):
                dve.tensor_copy(OH3[:, :, k, :], onehot[:])
                ins = dve.tensor_tensor(MV3[:, :, k, :], onehot[:], vparts[:, k, :].unsqueeze(2).to_broadcast([P, NT, RE]),
                                        ALU.mult)
            ins.then_inc(s_oh, 1)
            dve.wait_ge(s_x2, NC)
            layernorm(dve, step, s_ln, s_sqrt, s_tok, stats, mv, vare, std, rstd, newt)
            for i in range(NT):
                dve.tensor_scalar(h_tok[:, i, :], s_tok[:, i, :], mv[:, i, 0:1], rstd[:, i:i + 1], ALU.subtract,
                                  ALU.mult).then_inc(s_hn, 1)
            k = ("GL", 0)
            L2 = bank(k)[:, 0:NT * ME].rearrange("p (n e) -> p n e", n=NT)
            dve.wait_ge(s_g, number[k] + 1)
            step(dve.tensor_reduce(gmax[:], L2, AX_X, ALU.max))
            dve.tensor_tensor(gdiff[:], L2, bc(gmax, ME), ALU.subtract).then_inc(s_gd, 1)
            dve.wait_ge(s_gd, 1)
            dve.sem_inc(s_gf[number[k] % 2], 1)
            dve.wait_ge(s_ge, 1)
            step(dve.tensor_reduce(gsum[:], gexp[:], AX_X, ALU.add))
            step(dve.reciprocal(gsum[:], gsum[:]))
            dve.tensor_tensor(gw[:], gexp[:], bc(gsum, ME), ALU.mult).then_inc(s_gw, 1)

            unit = [0]

            def count_rows():
                u = unit[0]
                if u >= len(UNITS):
                    return
                i, cc = UNITS[u]
                r = R[u % 2]
                v = val[:, i:i + 1]
                dve.wait_ge(s_r, u + 1)
                own = i // TPC
                if u >= 2:
                    dve.wait_ge(s_rc, u - 1)
                k = u % 2
                if cc != own:
                    ins = dve.tensor_scalar(seen[:, k, :], r[:], v, None, ALU.is_ge if cc < own else ALU.is_gt, ALU.add,
                                            counts[:, i, cc:cc + 1])
                else:
                    q = (i % TPC) * P
                    if q:
                        dve.tensor_scalar(seen[:, k, 0:q], r[:, 0:q], v, None, ALU.is_ge, ALU.add, counts[:, i, cc:cc + 1])
                    dve.tensor_scalar(seen[:, k, q:], r[:, q:], v, None, ALU.is_gt, ALU.add, counts[:, i, NC:NC + 1])
                    ins = dve.scalar_tensor_tensor(same[:, k, :], r[:, q:q + P], v, below[:], ALU.is_equal, ALU.mult,
                                                   counts[:, i, NC + 1:NC + 2])
                ins.then_inc(s_rc, 1)
                unit[0] += 1
                if unit[0] == len(UNITS):
                    slots()

            def slots():
                dve.wait_ge(s_rc, len(UNITS))
                step(dve.tensor_reduce(rank[:], counts[:], AX_X, ALU.add))
                step(dve.tensor_scalar(over[:], rank[:], float(CAP) - 0.5, float(2 * SLOT_ROWS), ALU.is_ge, ALU.mult))
                step(dve.tensor_scalar(slotf[:], cmax[:], -float(CAP), float(CAP * RE), ALU.mult, ALU.add))
                step(dve.tensor_tensor(slotf[:], slotf[:], rank[:], ALU.add))
                step(dve.tensor_tensor(slotf[:], slotf[:], over[:], ALU.add))
                dve.tensor_copy(slot[:], slotf[:]).then_inc(s_slot, 1)

            def route_counts(k):
                for _ in range(k):
                    count_rows()

            def add(n):
                c, e = GROUPS[n]
                dve.wait_ge(s_e, n + 1)
                dve.wait_ge(s_b2, c + 1)
                if e > 0:
                    dve.wait_ge(s_acc, n)
                for i in range(TPC):
                    t = TPC * c + i
                    ins = dve.scalar_tensor_tensor(s_tok[:, t, :], E[n % 2][:, i * P:(i + 1) * P], gw[:, t, e:e + 1],
                                                   s_tok[:, t, :], ALU.mult, ALU.add)
                ins.then_inc(s_acc, 1)

            route_counts(PER_HB * HB)
            for c in range(NC):
                k = ("B2", c)
                dve.wait_ge(s_g, number[k] + 1)
                dve.tensor_tensor(s_tok[:, tiles(c), :], t4(bank(k)[:]), s_tok[:, tiles(c), :], ALU.add).then_inc(s_b2, 1)
                dve.wait_ge(s_b2, c + 1)
                dve.sem_inc(s_gf[number[k] % 2], 1)
            def routed():
                for e in range(RE):
                    dve.wait_ge(s_ry, e + 1)
                    dve.tensor_scalar(yeT[:, e * CAP:(e + 1) * CAP], G[e % 2][:, 0:CAP], be2[:, e:e + 1], None,
                                      ALU.add).then_inc(s_yT, 1)
                for c in range(XC):
                    dve.wait_ge(s_t, XC + c + 1)
                    dve.tensor_copy(ye[:, tiles(c), :], t4(R[c % 2][:])).then_inc(s_ye, 1)

            for n in range(len(GROUPS)):
                if n + 1 < len(GROUPS):
                    route_counts(PER_HB * HB)
                if n == ROUTED_AT:
                    routed()
                    dve.wait_ge(s_sc, 16 * NT)
                    dve.wait_ge(s_y, 1)
                    dve.tensor_tensor(sq, wv[:], wv[:], ALU.mult).then_inc(s_sq, 1)
                elif n == ROUTED_AT + 1:
                    dve.tensor_scalar(wq[:], wq[:], C_QKV, None, ALU.mult)
                    dve.tensor_scalar(wk[:], wk[:], C_QKV * HS ** -0.5, None, ALU.mult)
                elif n == ROUTED_AT + 2:
                    dve.wait_ge(s_nrt, 2)
                    step(dve.tensor_scalar(norm, norm, 1e-18, None, ALU.max))
                    step(dve.reciprocal(norm, norm))
                    dve.tensor_tensor(wv[:], wv[:], norm, ALU.mult).then_inc(s_rn, 1)
                add(n)
            for c in range(NC):
                dve.wait_ge(s_acc, ME * (c + 1))
                dve.wait_ge(s_sg, c + 1)
                dve.tensor_tensor(g[:, tiles(c), :], s_tok[:, tiles(c), :], g[:, tiles(c), :], ALU.mult).then_inc(s_m, 1)
                dve.wait_ge(s_m, c + 1)
                dve.tensor_tensor(x_tok[:, tiles(c), :], x_tok[:, tiles(c), :], g[:, tiles(c), :], ALU.add).then_inc(s_end, 1)
            dve.memset(wo[:, 0, :], 0.0)
            dve.wait_ge(s_ncol, 1)
            step(dve.reciprocal(ncol[:, 0:PAIRS], G[1][:, 0:PAIRS]))
            for j in range(PAIRS):
                ins = dve.tensor_scalar(wo[:, j + 1, :], wo[:, j + 1, :], ncol[:, j:j + 1], C_OUT * C_QKV, ALU.mult,
                                        ALU.mult)
            step(ins)


def before_attention1(nc, dram, keep):
    with ExitStack() as ctx:
        t0 = {}
        for name, shape, dt in (
                ("x_tok", [P, NT, D], F32), ("xn_tok", [P, NT, D], F32), ("s_tok", [P, NT, D], F32),
                ("x2T", [P, T], F32), ("xnT", [P, T + 2], F32), ("slot", [P, NT], I32),
                ("wg", [P, RE], F32), ("rank_order", [P, RE], F32), ("below", [P, P], F32),
                ("ln_g", [P, 1], F32), ("ln_b", [P, 1], F32), ("w_mg", [P, ME], F32),
                ("w1", [P, ME * HB, P], F32), ("b1", [P, ME * HB], F32),
                ("w2", [P, ME * HB, D], F32), ("b2", [ME, D], F32),
                ("W1", [P, RE, RH2 * P], F32), ("be1", [P, RE, RH2], F32),
                ("W2", [P, RE, RH2, D], F32), ("be2", [P, RE], F32)):
            t0[name] = ctx.enter_context(nc.sbuf_tensor(name, shape, dt))
        mixer0(nc, dram, keep, t0)
        with ExitStack() as inner:
            for name, shape in (("y_tok", [P, NT, D]), ("xe", [P, XT_, D])):
                t0[name] = inner.enter_context(nc.sbuf_tensor(name, shape, F32))
            experts0(nc, dram, keep, t0)
        setup1(nc, dram, keep, t0["x_tok"])


def setup1(nc, dram, keep, x1_tok):
    ident, xT = keep["ident"], keep["xT"]
    with ExitStack() as ctx:
        def sb(name, shape, dt=F32):
            return ctx.enter_context(nc.sbuf_tensor(name, shape, dt))

        def sem(name):
            return ctx.enter_context(nc.semaphore(name))

        stats = sb("stats1", [P, NT, 6])
        mv = sb("mv1", [P, NT, 2])
        vare = sb("vare1", [P, NT])
        std = sb("std1", [P, NT])
        rstd = sb("rstd1", [P, NT])
        newt = sb("newt1", [P, NT])
        xn = sb("xn1", [P, NT, D])
        diff = sb("diff1", [P, T])
        xr = sb("xr1", [P, T])
        xk = sb("xk1", [P, T])
        krelu = sb("krelu1", [P, T])
        kact = sb("kact1", [P, T])
        rsig = sb("rsig1", [P, NT, D])
        gate = sb("gate1", [P, NT, D])
        ffw = sb("ffw1", [P, 3, D])
        mu = sb("mu1", [P, 2])
        B = [ctx.enter_context(nc.psum_tensor(f"SB{i}", [P, CW], F32)) for i in range(8)]

        s_w = sem("w1_loaded")
        s_v = sem("dve_step1")
        s_ln = sem("ln_var1")
        s_sqrt = sem("ln_sqrt1")
        s_xn = sem("xn_tiles1")
        s_turn = sem("xn_turned1")
        s_xT = sem("xT_chunks1")
        s_mix = sem("mixed1")
        s_k = sem("k_sums1")
        s_relu = sem("k_relu1")
        s_kact = sem("k_act1")
        s_r = sem("r_sums1")
        s_sig = sem("r_sigmoid1")
        s_kv = sem("kv_sums1")
        s_rkv = sem("rkv1")
        s_gate = sem("gate_done1")
        s_st = sem("stored1")
        NLOAD = 16 * 3
        block = ctx.enter_context(nc.Block())

        @block.sync
        def _(sp):
            sp.dma_start(dram["x1_kept"], x1_tok[:].rearrange("p n d -> p (n d)")).then_inc(s_st, 16)
            for dst, src in ((mu[:], dram["mu"]), (ffw[:], dram["ffw"]), (keep["angle"][:], dram["angle"])):
                sp.dma_start(dst, src).then_inc(s_w, 16)
            sp.wait_ge(s_gate, NC)
            sp.dma_start(dram["gate_kept"], gate[:].rearrange("p n d -> p (n d)")).then_inc(s_st, 16)
            sp.wait_ge(s_st, 32)

        def square(dve, c):
            dve.wait_ge(s_relu, c + 1)
            dve.scalar_tensor_tensor(kact[:, c * CW:(c + 1) * CW], B[2 + c % 2][:], 0.0,
                                     krelu[:, c * CW:(c + 1) * CW], ALU.max, ALU.mult).then_inc(s_kact, 1)

        @block.vector
        def _(dve):
            steps = [0]

            def step(ins):
                steps[0] += 1
                ins.then_inc(s_v, 1)
                dve.wait_ge(s_v, steps[0])

            dve.memset(xT[:, 0:1], 0.0)
            for i in range(NT):
                ins = dve.bn_stats(stats[:, i, :], x1_tok[:, i, :])
            step(ins)
            for i in range(NT):
                ins = dve.bn_aggr(mv[:, i, :], stats[:, i, :])
            step(ins)
            dve.tensor_scalar(vare[:], mv[:, :, 1], EPS, None, ALU.add).then_inc(s_ln, 1)
            dve.wait_ge(s_sqrt, 1)
            step(dve.reciprocal(rstd[:], std[:]))
            step(dve.tensor_tensor(newt[:], rstd[:], rstd[:], ALU.mult))
            step(dve.tensor_tensor(newt[:], newt[:], vare[:], ALU.mult))
            step(dve.tensor_scalar(newt[:], newt[:], -0.5, 1.5, ALU.mult, ALU.add))
            step(dve.tensor_tensor(rstd[:], rstd[:], newt[:], ALU.mult))
            for i in range(NT):
                dve.tensor_scalar(xn[:, i, :], x1_tok[:, i, :], mv[:, i, 0:1], rstd[:, i:i + 1], ALU.subtract,
                                  ALU.mult).then_inc(s_xn, 1)
            dve.wait_ge(s_w, NLOAD)
            for c in range(NC):
                a, b = c * CW, (c + 1) * CW
                dve.wait_ge(s_xT, c + 1)
                step(dve.tensor_tensor(diff[:, a:b], xT[:, a + 1:b + 1], xT[:, a:b], ALU.subtract))
                dve.scalar_tensor_tensor(xk[:, a:b], diff[:, a:b], mu[:, 1:2], xT[:, a:b], ALU.mult,
                                         ALU.add).then_inc(s_mix, 1)
                dve.scalar_tensor_tensor(xr[:, a:b], diff[:, a:b], mu[:, 0:1], xT[:, a:b], ALU.mult,
                                         ALU.add).then_inc(s_mix, 1)
                if c > 0:
                    square(dve, c - 1)
            square(dve, NC - 1)
            for c in range(NC):
                dve.wait_ge(s_sig, c + 1)
                dve.wait_ge(s_kv, c + 1)
                dve.tensor_tensor(gate[:, TPC * c:TPC * (c + 1), :], B[6 + c % 2][:].rearrange("p (n d) -> p n d", d=D),
                                  rsig[:, TPC * c:TPC * (c + 1), :], ALU.mult).then_inc(s_rkv, 1)

        @block.scalar
        def _(act):
            act.wait_ge(s_ln, 1)
            act.activation(std[:], vare[:], ACT.Sqrt).then_inc(s_sqrt, 1)
            for c in range(NC):
                act.wait_ge(s_turn, c + 1)
                act.activation(xT[:, 1 + c * CW:1 + (c + 1) * CW], B[c % 2][:], ACT.Copy).then_inc(s_xT, 1)
            for c in range(NC):
                act.wait_ge(s_k, c + 1)
                act.activation(krelu[:, c * CW:(c + 1) * CW], B[2 + c % 2][:], ACT.Relu).then_inc(s_relu, 1)
                act.wait_ge(s_r, c + 1)
                act.activation(rsig[:, TPC * c:TPC * (c + 1), :], B[4 + c % 2][:].rearrange("p (n d) -> p n d", d=D),
                               ACT.Sigmoid).then_inc(s_sig, 1)
            for c in range(NC):
                act.wait_ge(s_rkv, c + 1)
                g = gate[:, TPC * c:TPC * (c + 1), :]
                act.activation(g, g, ACT.Silu).then_inc(s_gate, 1)

        @block.tensor
        def _(pe):
            for c in range(NC):
                if c >= 2:
                    pe.wait_ge(s_xT, c - 1)
                for i in range(TPC):
                    pe.wait_ge(s_xn, TPC * c + i + 1)
                    ins = pe.transpose(B[c % 2][:, i * P:(i + 1) * P], xn[:, TPC * c + i, :], ident[:])
                ins.then_inc(s_turn, 1)
            for c in range(NC):
                pe.wait_ge(s_mix, 2 * c + 2)
                if c >= 2:
                    pe.wait_ge(s_kact, c - 1)
                pe.matmul(B[2 + c % 2][:], ffw[:, 1, :], xk[:, c * CW:(c + 1) * CW], start=True, stop=True).then_inc(s_k, 1)
                if c >= 2:
                    pe.wait_ge(s_sig, c - 1)
                for i in range(TPC):
                    t = c * CW + i * P
                    ins = pe.matmul(B[4 + c % 2][:, i * P:(i + 1) * P], xr[:, t:t + P], ffw[:, 0, :], start=True, stop=True)
                ins.then_inc(s_r, 1)
            pe.wait_ge(s_kact, NC)
            for c in range(NC):
                if c >= 2:
                    pe.wait_ge(s_rkv, c - 1)
                for i in range(TPC):
                    t = c * CW + i * P
                    ins = pe.matmul(B[6 + c % 2][:, i * P:(i + 1) * P], kact[:, t:t + P], ffw[:, 2, :], start=True, stop=True)
                ins.then_inc(s_kv, 1)


def attention1(nc, dram, keep, out_dram):
    ident, identh, ones, xT, fold, angle = (keep[n] for n in ("ident", "identh", "ones", "xT", "fold", "angle"))
    mask_rows, mask_cols = keep["mask_rows"], keep["mask_cols"]
    wq, wk, wv, wo, wpos, bpos, bq = (keep[n] for n in ("wq", "wk", "wv", "wo", "wpos", "bpos", "bq"))
    RH = HS + FREQS
    KR = RH + 1
    QHI, QLO, KHI, KLO = range(4)
    with ExitStack() as ctx:
        def sb(name, shape, dt=F32):
            return ctx.enter_context(nc.sbuf_tensor(name, shape, dt))

        def sem(name):
            return ctx.enter_context(nc.semaphore(name))

        rows = [sb(f"rows{h}", [P, 4, T], F32R) for h in (0, 1)]
        heads = [[rows[h][:, k, :] for k in (QHI, QLO, KHI, KLO)] for h in (0, 1)]
        vh = [sb(f"V{h}", [P, NT, VW], F16) for h in (0, 1)]
        stage_rows = sb("stage_rows", [P, 4, T], F32R)
        stage = [stage_rows[:, k, :] for k in (QHI, QLO, KHI, KLO)]
        stage_pos = sb("stage_pos", [P, T], F32R)
        stage_v = sb("stage_v", [P, NT, 2, VW], F16)
        pair_wq = sb("pair_wq", [P, P])
        pair_wk = sb("pair_wk", [P, P])
        pair_wpos = sb("pair_wpos", [P, P])
        pair_b = sb("pair_b", [P, 2])
        turned = sb("turned", [P, CW])
        acc = sb("acc", [P, NT, D])
        negm = sb("negm", [P, 2, NT])
        part = sb("part", [P, 2, TPC])
        mrow = sb("mrow", [TPC, NC, P], F32R)
        prob = sb("prob", [P, PB, CW])
        plow = sb("plow", [P, PB, CW], F16)
        osb = sb("osb", [P, 2, TPC, VW])
        rsum = sb("rsum", [P, 2, TPC])
        oadd = sb("oadd", [P, TPC, HS])
        otok = sb("otok", [P, NT, P])
        oT = sb("oT", [P, CW])

        S = [ctx.enter_context(nc.psum_tensor(f"S{i}", [P, CW], F32)) for i in range(2)]
        A = [ctx.enter_context(nc.psum_tensor(f"A{i}", [P, CW], F32)) for i in range(2)]
        O = ctx.enter_context(nc.psum_tensor("O", [P, 2, CW], F32))
        M = [ctx.enter_context(nc.psum_tensor(f"M{i}", [P, CW], F32)) for i in range(2)]

        s_const = sem("const_loaded")
        s_init = sem("buffers_set")
        s_item = sem("item_sums")
        s_free = [sem(f"item_out{i}") for i in range(2)]
        s_high = sem("item_high")
        s_st = sem("scores")
        s_exp = sem("exps")
        s_low = sem("lows")
        s_low_pool = sem("lows_pool")
        s_pv = sem("values_added")
        s_a = sem("row_scores")
        s_max = sem("row_maxima")
        s_neg = sem("joined_maxima")
        s_pair = sem("pair_weights")
        s_oev = sem("outputs_copied")
        s_rec = sem("sums_inverted")
        s_oad = sem("outputs_joined")
        s_otok = sem("outputs_scaled")
        s_mrow = [sem(f"max_moved{c}") for c in range(NC)]
        s_move = [sem(f"rows_moved{c}") for c in range(NC)]
        s_mv = [sem(f"values_moved{h}") for h in (0, 1)]
        s_back = sem("reloaded")
        s_fin = sem("finished")
        s_out = sem("stored")
        MOVES = 3 * 16

        bank = Bank()
        pro_items = [(kind, 0, c, bank.take()) for c in range(NC) for kind in ("q", "k", "pos", "v", "possum")]
        pro_max = [("maxima", 0, c, bank.take()) for c in range(NC - 1)]
        base_n, base_bank = bank.n, list(bank.of_bank)
        plan = {}
        for last in (False, True):
            items, k = plan_items(last), 0
            plan[last] = {}
            for n in range(SLOTS):
                plan[last][n] = []
                for (kind, rel, c) in items[n]:
                    plan[last][n].append((kind, rel, c, (base_n + k, (k + base_n) % 2, base_bank[(k + base_n) % 2] + k // 2)))
                    k += 1
            if not last:
                PER = k
                assert PER % 2 == 0
            else:
                TAIL = k
        bank.n, bank.of_bank = 0, [0, 0]
        for _ in range(base_n + 7 * PER + TAIL):
            bank.take()
        fin_items = [("turn", 0, 3, bank.take()), ("project", 0, 3, bank.take())]

        PRO_A = NB - LEAD
        PER_A = len(A_SLOTS)
        HIGHS = 4 * NC

        def count(tok, p):
            n, b, before = tok
            return n + 1 + PER * p, b, before + (PER // 2) * p

        def split(engine, m, p, done):
            c, j = B_TILES[m % NB]
            w = CW - max(0, j - TPC * c) * P
            full = prob[:, m % PB, 0:w]
            engine.wait_ge(s_exp, SLOTS * p + m + 1)
            engine.tensor_tensor(plow[:, m % PB, 0:w], full, full.bitcast(BF16).rearrange("p (q e) -> p q e", e=2)[:, :, 1],
                                 ALU.subtract).then_inc(done, 1)

        def column(t, p):
            return t[:, p:p + 1] if isinstance(p, int) else t[:, bass.ds(p, 1)]

        block = ctx.enter_context(nc.Block())

        @block.sync
        def _(sp):
            sp.dma_start(acc[HS:RH, :, :].rearrange("p n d -> p (n d)"), dram["ktab"]).then_inc(s_const, 16)

            def move_chunk(h, c):
                a, b = c * CW, (c + 1) * CW
                sp.dma_start(raw(rows[h][0:HS, :, a:b]), raw(stage_rows[HS * h:HS * (h + 1), :, a:b])).then_inc(s_move[c], 16)
                for k in (QHI, QLO):
                    r = k * 2 * FREQS + FREQS * h
                    sp.dma_start(raw(heads[h][k][HS:RH, a:b]), raw(stage_pos[r:r + FREQS, a:b])).then_inc(s_move[c], 16)

            def move_values(h):
                sp.dma_start(vh[h][:], stage_v[:, :, h, :]).then_inc(s_mv[h], 16)

            def move_head(h):
                for c in range(NC):
                    move_chunk(h, c)
                move_values(h)

            def move_max(h, c, tok, p):
                _, b, before = count(tok, p)
                sp.wait_ge(s_free[b], before + 1)
                sp.dma_start(raw(heads[h][QHI][RH:KR, c * CW:(c + 1) * CW]), raw(mrow[:, c, :])).then_inc(s_mrow[c], 16)

            def staged(last_tok, before_tok, p):
                for tok in (last_tok, before_tok):
                    _, b, before = count(tok, p)
                    sp.wait_ge(s_free[b], before + 1)

            sp.wait_ge(s_init, 1)
            for c in range(NC):
                last = [x[3] for x in pro_items if x[2] == c][-2:]
                staged(last[1], last[0], 0)
                for h in (0, 1):
                    move_chunk(h, c)
            for h in (0, 1):
                move_values(h)
            sp.wait_ge(s_init, 6)
            sp.dma_start(acc[:], dram["out_bias"]).then_inc(s_const, 16)
            for (_, _, c, tok) in pro_max:
                move_max(0, c, tok, 0)

            def pair(p, last):
                items = plan[last]
                preps = [x[3] for n in range(SLOTS) for x in items[n] if x[0] in ("q", "k", "pos", "v", "possum")]
                for n in range(SLOTS):
                    for (kind, rel, c, tok) in items[n]:
                        if kind == "maxima":
                            move_max(rel % 2, c, tok, p)
                    if n == NB - 1 and not last:
                        staged(preps[-1], preps[-2], p)
                        sp.wait_ge(s_st, SLOTS * p + NB)
                        sp.wait_ge(s_pv, SLOTS * p + NB)
                        move_head(0)
                if not last:
                    sp.wait_ge(s_st, SLOTS * (p + 1))
                    sp.wait_ge(s_pv, SLOTS * (p + 1))
                    move_head(1)

            with sp.Fori(0, PAIRS - 1) as p:
                pair(p, False)
            sp.dma_start(angle[:], dram["x1_kept"]).then_inc(s_back, 16)
            sp.dma_start(xT[:, 0:T], dram["gate_kept"]).then_inc(s_back, 16)
            pair(PAIRS - 1, True)
            for c in range(NC):
                sp.wait_ge(s_fin, 2 * c + 2)
                sp.dma_start(out_dram.rearrange("b (n p) d -> p (b n) d", p=P)[:, TPC * c:TPC * (c + 1), :],
                             acc[:, TPC * c:TPC * (c + 1), :]).then_inc(s_out, 16)
            sp.wait_ge(s_out, 16 * NC)

        @block.gpsimd
        def _(pool):
            def weights(p, p_next, first):
                if not first:
                    pool.wait_ge(s_item, base_n + PER * p)
                at = slice(p_next * P, (p_next + 1) * P) if isinstance(p_next, int) else bass.ds(p_next * P, P)
                pool.tensor_copy(pair_wq[:], wq[:, at])
                pool.tensor_copy(pair_wk[:], wk[:, at])
                pool.tensor_copy(pair_b[:, 0:1], column(bq, p_next))
                pool.tensor_copy(pair_b[:, 1:2], column(bpos, p_next))
                pool.tensor_copy(pair_wpos[:], wpos[:, at]).then_inc(s_pair, 1)

            def scale(k, h, c, g):
                pool.wait_ge(s_oev, g + 2)
                pool.wait_ge(s_otok, g + 1)
                at = (slice(None), slice(TPC * c, TPC * (c + 1)), slice(HS * h, HS * (h + 1)))
                pool.tensor_tensor(oadd[:], osb[:, k, :, 0:HS], osb[:, k, :, HS + 1:VW], ALU.add).then_inc(s_oad, 1)
                pool.wait_ge(s_oad, g + 1)
                pool.wait_ge(s_rec, g + 1)
                pool.tensor_tensor(otok[at], oadd[:], rsum[:, k, :].unsqueeze(2).to_broadcast([P, TPC, HS]),
                                   ALU.mult).then_inc(s_otok, 1)

            for h in (0, 1):
                ins = pool.memset(stage_v[:, :, h, HS:HS + 1], 1.0)
            ins.then_inc(s_init, 1)
            weights(0, 0, True)
            pool.wait_ge(s_pair, 1)
            pool.wait_ge(s_const, 16)
            table = acc[HS:RH, :, :].rearrange("p n d -> p (n d)")
            for h in (0, 1):
                pool.wait_ge(s_init, 1 + h)
                pool.tensor_copy(heads[h][KHI][HS:RH, :], table).then_inc(s_init, 1)
            for h in (0, 1):
                pool.wait_ge(s_init, 3 + h)
                pool.tensor_tensor(heads[h][KLO][HS:RH, :], table, heads[h][KHI][HS:RH, :], ALU.subtract).then_inc(s_init, 1)
            pool.wait_ge(s_init, 5)
            pool.memset(otok[:], 0.0).then_inc(s_init, 1)
            pool.wait_ge(s_init, 6)
            pool.sem_inc(s_otok, 1)

            def pair(p, last):
                if not last:
                    weights(p, p + 1, False)
                for n in range(SLOTS + DRAIN + 2):
                    if n < SLOTS and on_pool(n):
                        split(pool, n, p, s_low_pool)
                    m = n - DRAIN - 2
                    if m >= 0:
                        h, (c, j) = m // NB, B_TILES[m % NB]
                        if j == TPC * (c + 1) - 1:
                            if h == 0 and c == 0:
                                first_turn = plan[last][4][0][3]
                                pool.wait_ge(s_item, count(first_turn, p)[0])
                            scale(c % 2, h, c, 2 * NC * p + NC * h + c)

            with pool.Fori(0, PAIRS - 1) as p:
                pair(p, False)
            pair(PAIRS - 1, True)

        def pos_item(items, c):
            return next(x[3] for n in range(SLOTS) for x in items[n] if x[0] == "pos" and x[2] == c)

        def turn_item(items, rel, c):
            return next(x[3] for n in range(SLOTS) for x in items[n] if x[:3] == ("turn", rel, c))

        @block.tensor
        def _(pe):
            def item(kind, rel, c, tok, p, pos_tok=None, turn_tok=None):
                _, b, before = count(tok, max(p, 0) if isinstance(p, int) else p)
                if not isinstance(before, int) or before > 0:
                    pe.wait_ge(s_free[b], before)
                out = M[b]
                a0, a1 = c * CW, (c + 1) * CW
                if kind in ("q", "k", "pos"):
                    if kind == "q" and c == 0:
                        pe.wait_ge(s_pair, p + 2)
                    w = {"q": pair_wq, "k": pair_wk, "pos": pair_wpos}[kind]
                    ins = pe.matmul(out[:], w[:], xT[:, 1 + a0:1 + a1], start=True, stop=True)
                elif kind == "possum":
                    _, b2, before2 = count(pos_tok, max(p, 0) if isinstance(p, int) else p)
                    pe.wait_ge(s_free[b2], before2 + 1)
                    ins = pe.matmul(out[0:2 * FREQS, :], fold[:], turned[:], start=True, stop=True)
                elif kind == "v":
                    w = wv[:, (p + 1) * P:(p + 2) * P] if isinstance(p, int) else wv[:, bass.ds((p + 1) * P, P)]
                    for i in range(TPC):
                        ins = pe.matmul(out[:, i * P:(i + 1) * P], xT[:, 1 + a0 + i * P:1 + a0 + (i + 1) * P], w,
                                        start=True, stop=True)
                elif kind == "maxima":
                    head = 2 * p + rel
                    if c == 0:
                        pe.wait_ge(s_max, a_end(0) if ahead(p) else PRO_A + PER_A * p + {1: LEAD, 2: LEAD + NB}[rel] + a_end(0))
                    else:
                        pe.wait_ge(s_neg, (NT - TPC) * (0 if ahead(p) else head) + TPC * c)
                    ins = pe.transpose(out[0:TPC, 0:P], negm[:, rel % 2, TPC * c:TPC * (c + 1)], ident[:])
                elif kind == "turn":
                    pe.wait_ge(s_otok, 2 * NC * p + (NC + c + 2 if rel == 0 else 1))
                    for i in range(TPC):
                        ins = pe.transpose(out[:, i * P:(i + 1) * P], otok[:, TPC * c + i, :], ident[:])
                elif kind == "project":
                    _, b2, before2 = count(turn_tok, p)
                    pe.wait_ge(s_free[b2], before2 + 1)
                    w = wo[:, p + 1 + rel, :] if isinstance(p, int) else wo[:, bass.ds(p + (1 + rel), 1), :]
                    for i in range(TPC):
                        ins = pe.matmul(out[:, i * P:(i + 1) * P], oT[:, i * P:(i + 1) * P], w, start=True, stop=True)
                ins.then_inc(s_item, 1)

            def row_scores(h, a, g):
                i, cc = A_TILES[a]
                out = A[g % 2]
                diagonal = cc == i // TPC
                w = (i % TPC + 1) * P if diagonal else CW
                if diagonal:
                    pe.matmul(out[:, w - P:w], identh[:], mask_rows[:], start=True, stop=False, skip_group_check=True)
                w = max(w, FAST)
                pe.matmul(out[:, 0:w], heads[h][QHI][0:RH, i * P:(i + 1) * P], heads[h][KHI][0:RH, cc * CW:cc * CW + w],
                          start=not diagonal, stop=True, skip_group_check=True).then_inc(s_a, 1)

            def scores(h, c, j, n):
                r = max(0, j - TPC * c)
                w = max(CW - r * P, FAST)
                off = w - (CW - r * P)
                out = S[n % 2]
                qh, ql, kh, kl = heads[h]
                q0, q1, k0, k1 = (c + 1) * CW - w, (c + 1) * CW, j * P, (j + 1) * P
                diagonal = j >= TPC * c
                if diagonal:
                    pe.matmul(out[:, off:off + P], identh[:], mask_cols[:], start=True, stop=False, skip_group_check=True)
                pe.matmul(out[:, 0:w], kh[0:KR, k0:k1], qh[0:KR, q0:q1], start=not diagonal, stop=False,
                          skip_group_check=True)
                pe.matmul(out[:, 0:w], kl[0:RH, k0:k1], qh[0:RH, q0:q1], start=False, stop=False, skip_group_check=True)
                pe.matmul(out[:, 0:w], kh[0:RH, k0:k1], ql[0:RH, q0:q1], start=False, stop=True,
                          skip_group_check=True).then_inc(s_st, 1)

            def values(h, c, j, n):
                r = max(0, j - TPC * c)
                high = prob[:, n % PB, :].bitcast(BF16).rearrange("p (q e) -> p q e", e=2)
                for s in range(r, TPC):
                    cs = slice((s - r) * P, (s - r + 1) * P)
                    at = (s % 2) * VW
                    done = j == TPC * c + s
                    pe.matmul(O[:, s // 2, at:at + VW], high[:, cs, 1], vh[h][:, j, :], start=(j == 0 and s % 2 == 0),
                              stop=False, skip_group_check=True)
                    ins = pe.matmul(O[:, s // 2, at:at + HS + 1], plow[:, n % PB, cs], vh[h][:, j, 0:HS + 1], start=False,
                                    stop=done, skip_group_check=True)
                ins.then_inc(s_pv, 1)

            pe.wait_ge(s_init, 1)
            for (kind, rel, c, tok) in pro_items:
                item(kind, rel, c, tok, -1, pos_tok=next(x[3] for x in pro_items if x[0] == "pos" and x[2] == c))
            pe.wait_ge(s_init, 5)
            for a in range(PRO_A):
                i, cc = A_TILES[a]
                if i % TPC == 0 and cc == 0:
                    pe.wait_ge(s_move[i // TPC], 2 * MOVES)
                if a >= 2:
                    pe.wait_ge(s_max, a - 1)
                row_scores(0, a, a)
                for (kind, rel, c, tok) in pro_max:
                    if a == a_end(c) + 1:
                        item(kind, rel, c, tok, -1)

            def pair(p, last):
                items = plan[last]

                def score_tile(n):
                    h, (c, j) = n // NB, B_TILES[n % NB]
                    if n >= 2:
                        pe.wait_ge(s_exp, SLOTS * p + n - 1)
                    if j == 0:
                        pe.wait_ge(s_mrow[c], 16 * (2 * p + h + 1))
                    scores(h, c, j, n)

                def row_tile(n):
                    rel, a = A_SLOTS[n]
                    if not (last and rel == 2):
                        i, cc = A_TILES[a]
                        if i % TPC == 0 and cc == 0 and rel > 0:
                            pe.wait_ge(s_move[i // TPC], 2 * MOVES * (p + 1) + (MOVES if rel == 2 else 0))
                        pe.wait_ge(s_max, PRO_A + PER_A * p + n - 1)
                        row_scores(rel % 2, a, PRO_A + n)

                def value_tile(m):
                    h, (c, j) = m // NB, B_TILES[m % NB]
                    if j == 0:
                        pe.wait_ge(s_oev, 2 * NC * p + NC * h + c + 1)
                        if c == 0:
                            pe.wait_ge(s_mv[h], 16 * (p + 1))
                    pool = on_pool(m)
                    pe.wait_ge(s_low_pool if pool else s_low, split_before(SLOTS - 1, pool) * p + split_before(m, pool))
                    values(h, c, j, m)

                for n in range(0, SLOTS + DRAIN, 2):
                    two = (n, n + 1)
                    for k in two:
                        if k < SLOTS:
                            score_tile(k)
                    for k in two:
                        if k < SLOTS:
                            row_tile(k)
                            for (kind, rel, c, tok) in items[k]:
                                item(kind, rel, c, tok, p, pos_tok=pos_item(items, c) if kind == "possum" else None,
                                     turn_tok=turn_item(items, rel, c) if kind == "project" else None)
                    for k in two:
                        if 0 <= k - DRAIN < SLOTS:
                            value_tile(k - DRAIN)

            with pe.Fori(0, PAIRS - 1) as p:
                pair(p, False)
            pair(PAIRS - 1, True)
            for (kind, rel, c, tok) in fin_items:
                item(kind, rel, c, (tok[0] - PER * (PAIRS - 1), tok[1], tok[2] - PER // 2 * (PAIRS - 1)), PAIRS - 1,
                     turn_tok=(fin_items[0][3][0], fin_items[0][3][1], fin_items[0][3][2] - PER // 2 * (PAIRS - 1)))

        @block.scalar
        def _(act):
            def item(kind, rel, c, tok, p, highs):
                it = max(p, 0) if isinstance(p, int) else p
                done, b, _ = count(tok, it)
                a0, a1 = c * CW, (c + 1) * CW
                if kind in ("pos", "project"):
                    return
                act.wait_ge(s_item, done)
                if kind in ("q", "k"):
                    if not ahead(p) and kind == "q":
                        act.wait_ge(s_move[c], 2 * MOVES * (p + 1))
                    if kind == "q":
                        act.activation(stage[QHI][:, a0:a1], M[b][:], ACT.Identity, bias=pair_b[:, 0:1]).then_inc(s_high, 1)
                    else:
                        act.activation(stage[KHI][:, a0:a1], M[b][:], ACT.Copy).then_inc(s_high, 1)
                elif kind == "possum":
                    act.activation(stage_pos[0:2 * FREQS, a0:a1], M[b][0:2 * FREQS, :], ACT.Copy).then_inc(s_high, 1)
                elif kind == "v":
                    if not ahead(p) and c == 0:
                        for h in (0, 1):
                            act.wait_ge(s_mv[h], 16 * (p + 1))
                    act.activation(stage_v[:, TPC * c:TPC * (c + 1), :, 0:HS],
                                   M[b][:].rearrange("p (n h d) -> p n h d", n=TPC, h=2), ACT.Copy).then_inc(s_high, 1)
                elif kind == "maxima":
                    if rel > 0:
                        act.wait_ge(s_mrow[c], 16 * (2 * p + rel))
                    act.activation(mrow[:, c, :], M[b][0:TPC, 0:P], ACT.Copy).then_inc(s_free[b], 1)
                elif kind == "turn":
                    act.activation(oT[:], M[b][:], ACT.Copy).then_inc(s_free[b], 1)

            act.sem_inc(s_oev, 1)
            for (kind, rel, c, tok) in pro_items:
                item(kind, rel, c, tok, -1, 0)
            for (kind, rel, c, tok) in pro_max:
                item(kind, rel, c, tok, -1, 0)

            def pair(p, last):
                for n in range(SLOTS + DRAIN):
                    if n < SLOTS:
                        h, (c, j) = n // NB, B_TILES[n % NB]
                        w = CW - max(0, j - TPC * c) * P
                        act.wait_ge(s_st, SLOTS * p + n + 1)
                        if n >= PB:
                            act.wait_ge(s_pv, SLOTS * p + n - PB + 1)
                        off = max(0, FAST - w)
                        act.activation(prob[:, n % PB, 0:w], S[n % 2][:, off:off + w], ACT.Exp).then_inc(s_exp, 1)
                        for (kind, rel, c, tok) in plan[last][n]:
                            item(kind, rel, c, tok, p, 0)
                    if n >= DRAIN:
                        m = n - DRAIN
                        h, (c, j) = m // NB, B_TILES[m % NB]
                        if j == TPC * (c + 1) - 1:
                            g = NC * h + c
                            act.wait_ge(s_pv, SLOTS * p + m + 1)
                            if g > 0:
                                act.wait_ge(s_otok, 2 * NC * p + g)
                            act.activation(osb[:, c % 2, :, :].rearrange("p (a b) v -> p a (b v)", a=2),
                                           O[:, :, 0:2 * VW], ACT.Copy).then_inc(s_oev, 1)

            with act.Fori(0, PAIRS - 1) as p:
                pair(p, False)
            pair(PAIRS - 1, True)
            kind, rel, c, tok = fin_items[0]
            act.wait_ge(s_item, tok[0] + 1)
            act.activation(oT[:], M[tok[1]][:], ACT.Copy).then_inc(s_free[tok[1]], 1)

        @block.vector
        def _(dve):
            def item(kind, rel, c, tok, p, high):
                it = max(p, 0) if isinstance(p, int) else p
                done, b, _ = count(tok, it)
                a0, a1 = c * CW, (c + 1) * CW
                if kind in ("maxima", "turn"):
                    return
                dve.wait_ge(s_item, done)
                if kind == "pos":
                    ins = dve.scalar_tensor_tensor(turned[:], M[b][:], pair_b[:, 1:2], angle[:, a0:a1], ALU.add, ALU.mult)
                elif kind == "project":
                    s = acc[:, TPC * c:TPC * (c + 1), :]
                    ins = dve.tensor_tensor(s, M[b][:].rearrange("p (n d) -> p n d", d=D), s, ALU.add)
                else:
                    dve.wait_ge(s_high, HIGHS * (p + 1) + high + 1)
                    if kind == "q":
                        ins = dve.scalar_tensor_tensor(stage[QLO][:, a0:a1], M[b][:], pair_b[:, 0:1], stage[QHI][:, a0:a1],
                                                       ALU.add, ALU.subtract)
                    elif kind == "k":
                        ins = dve.tensor_tensor(stage[KLO][:, a0:a1], M[b][:], stage[KHI][:, a0:a1], ALU.subtract)
                    elif kind == "possum":
                        ins = dve.tensor_tensor(stage_pos[2 * FREQS:4 * FREQS, a0:a1], M[b][0:2 * FREQS, :],
                                                stage_pos[0:2 * FREQS, a0:a1], ALU.subtract)
                    elif kind == "v":
                        t = slice(TPC * c, TPC * (c + 1))
                        ins = dve.tensor_tensor(stage_v[:, t, :, HS + 1:VW], M[b][:].rearrange("p (n h d) -> p n h d", n=TPC, h=2),
                                                stage_v[:, t, :, 0:HS], ALU.subtract)
                ins.then_inc(s_free[b], 1)

            def row_max(h, a, g, p, head):
                i, cc = A_TILES[a]
                w = (i % TPC + 1) * P if cc == i // TPC else CW
                dve.wait_ge(s_a, g + 1 + PER_A * p)
                joins = (NT - TPC) * head + i - TPC
                if cc == 0 and i >= TPC and not (isinstance(joins, int) and joins < 2):
                    dve.wait_ge(s_neg, joins - 1)
                out = negm[:, h, i:i + 1] if i < TPC else part[:, i % 2, cc:cc + 1]
                dve.tensor_reduce(out, A[g % 2][:, 0:w], AX_X, ALU.max, negate=i < TPC).then_inc(s_max, 1)
                if cc == i // TPC and i >= TPC:
                    dve.wait_ge(s_max, g + 1 + PER_A * p)
                    dve.tensor_reduce(negm[:, h, i:i + 1], part[:, i % 2, 0:cc + 1], AX_X, ALU.max, negate=True).then_inc(s_neg, 1)

            high = 0
            for (kind, rel, c, tok) in pro_items:
                item(kind, rel, c, tok, -1, high)
                if kind == "v" and c < 2:
                    dve.memset(heads[c][KHI][RH:KR, :].bitcast(F32), 1.0)
                high += kind != "pos"
            for a in range(PRO_A):
                row_max(0, a, a, 0, 0)
            dve.wait_ge(s_const, 32)

            def pair(p, last):
                high = 0
                for n in range(SLOTS + DRAIN + 1):
                    if 1 <= n <= SLOTS and not on_pool(n - 1):
                        split(dve, n - 1, p, s_low)
                    if n < SLOTS:
                        rel, a = A_SLOTS[n]
                        if not (last and rel == 2):
                            row_max(rel % 2, a, PRO_A + n, p, 2 * p + rel)
                        for (kind, rel, c, tok) in plan[last][n]:
                            item(kind, rel, c, tok, p, high)
                            high += kind in ("q", "k", "possum", "v")
                    if n >= DRAIN + 1:
                        m = n - DRAIN - 1
                        h, (c, j) = m // NB, B_TILES[m % NB]
                        if j == TPC * (c + 1) - 1:
                            dve.wait_ge(s_oev, 2 * NC * p + NC * h + c + 2)
                            dve.reciprocal(rsum[:, c % 2, :], osb[:, c % 2, :, HS]).then_inc(s_rec, 1)

            with dve.Fori(0, PAIRS - 1) as p:
                pair(p, False)
            pair(PAIRS - 1, True)
            dve.wait_ge(s_back, 32)
            for c in range(NC):
                s = acc[:, TPC * c:TPC * (c + 1), :].rearrange("p n d -> p (n d)")
                if c == NC - 1:
                    tok = fin_items[1][3]
                    dve.wait_ge(s_item, tok[0] + 1)
                    dve.tensor_tensor(s, M[tok[1]][:], s, ALU.add).then_inc(s_free[tok[1]], 1)
                else:
                    tok = next(x[3] for n in range(SLOTS) for x in plan[True][n] if x[:3] == ("project", 0, c))
                    tok = (tok[0], tok[1], count(tok, PAIRS - 1)[2])
                dve.wait_ge(s_free[tok[1]], tok[2] + 1)
                dve.tensor_tensor(s, s, xT[:, c * CW:(c + 1) * CW], ALU.mult).then_inc(s_fin, 1)
                dve.wait_ge(s_fin, 2 * c + 1)
                dve.tensor_tensor(s, s, angle[:, c * CW:(c + 1) * CW], ALU.add).then_inc(s_fin, 1)


def load_constants(nc, dram, keep):
    with ExitStack() as ctx:
        s_tables = ctx.enter_context(nc.semaphore("tables_loaded"))
        s_ones = ctx.enter_context(nc.semaphore("ones_set"))
        block = ctx.enter_context(nc.Block())

        @block.sync
        def _(sp):
            names = ("ident", "identh", "mask_rows", "mask_cols", "fold")
            for n in names:
                sp.dma_start(keep[n][:], dram[n]).then_inc(s_tables, 16)
            sp.wait_ge(s_tables, 16 * len(names))
            sp.wait_ge(s_ones, 1)

        @block.vector
        def _(dve):
            dve.memset(keep["ones"][:], 1.0).then_inc(s_ones, 1)


KEEP_BOTH = [("ident", [P, P], F32), ("identh", [P, P], BF16), ("mask_rows", [P, P], BF16),
             ("mask_cols", [P, P], BF16), ("ones", [P, P], F32), ("fold", [P, 2 * FREQS], F32)]
KEEP_L1 = [("wq", [P, HEADS * HS], F32), ("wk", [P, HEADS * HS], F32), ("wv", [P, HEADS * HS], F32),
           ("wpos", [P, PAIRS * P], F32), ("bpos", [P, PAIRS], F32), ("bq", [P, PAIRS], F32),
           ("wo", [P, PAIRS + 1, D], F32), ("xT", [P, T + 1], F32), ("angle", [P, T], F32)]
SCRATCH = [("x1_kept", [P, T]), ("gate_kept", [P, T]), ("xe_rows", [SLOT_ROWS, D]), ("ye_rows", [SLOT_ROWS, D])]


def build(nc, dram, out):
    for name, shape in SCRATCH:
        dram[name] = nc.dram_tensor(name, shape, F32, kind="Internal").ap()
    with ExitStack() as ctx:
        keep = {}
        for name, shape, dt in KEEP_BOTH + KEEP_L1:
            keep[name] = ctx.enter_context(nc.sbuf_tensor("keep_" + name, shape, dt))
        load_constants(nc, dram, keep)
        before_attention1(nc, dram, keep)
        attention1(nc, dram, keep, out)


def tables():
    f = np.float32
    i = np.arange(P)
    out = {}
    inv = (f(1.0) / np.power(f(10000.0), np.arange(0, MD, 2, dtype=f) / f(MD))).astype(f)
    theta = (np.arange(T, dtype=f)[:, None] * inv[None]).astype(np.float64)
    r = i % MD
    out["cos0"] = np.cos(theta)[:, r // 2].T.astype(f)
    out["sin0"] = (np.sin(theta)[:, r // 2] * np.where(r % 2 == 0, -1, 1)[None]).T.astype(f)
    same = (i // MD)[:, None] == (i // MD)[None]
    out["sel0"] = np.stack([same & (r[None] == m) for m in range(MD)] + [same], 1).astype(f)
    out["rank_order"] = np.broadcast_to(RE - np.arange(RE, dtype=f), (P, RE))
    out["below"] = (i[None] < i[:, None]).astype(f)
    w = 1250.0 ** (-(np.arange(0, FREQS, 2)) / FREQS)
    angle = w[:, None] * np.arange(T)[None]
    s, c = np.sin(angle), np.cos(angle)
    out["angle"] = np.concatenate([s, s, s, s, c, -c, c, -c]).astype(f)
    out["ktab"] = (np.concatenate([c, s]) / FREQS).astype(f)
    fold = np.zeros((P, 2 * FREQS), f)
    fold[i, i % (2 * FREQS)] = 1
    out["fold"] = fold
    bf16 = mybir.dt.np(BF16)
    out["ident"] = np.eye(P, dtype=f)
    out["identh"] = np.eye(P).astype(bf16)
    out["mask_rows"] = np.where(i[None] > i[:, None], -1e30, 0).astype(bf16)
    out["mask_cols"] = np.where(i[None] < i[:, None], -1e30, 0).astype(bf16)
    return out


def layout(a):
    out = {}
    out["x"] = a["L0_attn_x"][0]
    out["w_dw"] = a["L0_attn_w_dw"]
    wq, wk, wv = (a["L0_attn_w_qkv"][D * k:D * (k + 1)] for k in range(3))
    swap = np.arange(D) ^ 1
    out["w_sq"] = np.stack([a["L0_attn_w_pw"].T, wq.T, wq.T[:, swap], wk.T, wk.T[:, swap], a["L0_attn_w_gate"].T,
                            a["L0_attn_w_o"].T], 1)
    values = wv.T.reshape(D, MH, MD).transpose(0, 2, 1)
    out["w_vrep"] = np.repeat(values[:, :, :, None], MD, 3).reshape(D, MD, P)
    for name, key in (("b_gate", "b_gate"), ("ln_g", "ln_g"), ("ln_b", "ln_b")):
        out[name] = a["L0_attn_" + key][:, None]
    out["w_mg"] = a["L0_attn_w_moe_gate"].T
    out["w1"] = a["L0_attn_w1"].transpose(2, 0, 1).reshape(D, ME * HB, P)
    out["b1"] = a["L0_attn_b1"].reshape(ME * HB, P).T
    out["w2"] = a["L0_attn_w2"].reshape(ME, D, HB, P).transpose(3, 0, 2, 1).reshape(P, ME * HB, D)
    out["b2"] = a["L0_attn_b2"]
    out["wg"] = a["L0_ffn_Wg"]
    out["W1"] = a["L0_ffn_W1"].transpose(1, 0, 2)
    out["be1"] = a["L0_ffn_b1"].reshape(RE, RH2, P).transpose(2, 0, 1)
    out["W2"] = a["L0_ffn_W2"].reshape(RE, RH2, P, D).transpose(2, 0, 1, 3)
    out["be2"] = a["L0_ffn_b2"].T
    qkv = a["L1_attn_qkv"]
    for k, name in enumerate(("wq", "wk", "wv")):
        out[name] = qkv[:, k].reshape(D, HEADS * HS)
    out["wqT"] = qkv[:, 0].reshape(D, PAIRS, P).transpose(2, 1, 0)
    pos = a["L1_attn_positional"]
    even, odd = pos[0::2], pos[1::2]
    straight, swapped = np.concatenate([even, odd], 0), np.concatenate([odd, even], 0)
    pblk = np.zeros((P, PAIRS, P), pos.dtype)
    for h in (0, 1):
        rows = slice(HS * h, HS * (h + 1))
        pblk[rows, :, FREQS * h:FREQS * (h + 1)] = straight[:, h::2].transpose(2, 1, 0)
        pblk[rows, :, FREQS * (2 + h):FREQS * (3 + h)] = swapped[:, h::2].transpose(2, 1, 0)
    out["pblk"] = pblk
    out["bq"] = a["L1_attn_q_bias"].reshape(PAIRS, P).T
    out["wo"] = a["L1_attn_out_kernel"].reshape(PAIRS, P, D).transpose(1, 0, 2)
    out["out_bias"] = np.broadcast_to(a["L1_attn_out_bias"], (P, NT, D))
    out["ffw"] = np.stack([a["L1_ffn_W_r"].T, a["L1_ffn_W_k"].T, a["L1_ffn_W_v"].T], 1)
    out["mu"] = np.stack([a["L1_ffn_mu_r"], a["L1_ffn_mu_k"]], 1)
    return out


def kernel(**inputs):
    import concourse.bacc as _bacc
    from concourse.bass_utils import run_bass_kernel_spmd as _run

    nc = _bacc.Bacc("TRN2", target_bir_lowering=False, num_devices=1)
    arrays, dram = {}, {}
    host = {**layout({k: np.asarray(v) for k, v in inputs.items()}), **tables()}
    for name, a in host.items():
        a = np.ascontiguousarray(a)
        arrays["in_" + name] = a
        dram[name] = nc.dram_tensor("in_" + name, a.shape, mybir.dt.from_np(a.dtype), kind="ExternalInput").ap()
    out = nc.dram_tensor("out_0", (1, T, D), F32, kind="ExternalOutput").ap()
    build(nc, dram, out)
    r = _run(nc, [arrays], core_ids=[0])
    return r.results[0]["out_0"]
```
